# Optimizing a Trainium2 kernel written in Bass

```python
import numpy as np
import jax
import jax.numpy as jnp

def _softmax(x, axis=-1):
    return jax.nn.softmax(x, axis=axis)

def _gelu(x):
    return jax.nn.gelu(x, approximate=True)

def _silu(x):
    return jax.nn.silu(x)

def _sigmoid(x):
    return jax.nn.sigmoid(x)

def _layernorm(x, axis=-1, eps=1e-05):
    m = jnp.mean(x, axis=axis, keepdims=True)
    v = jnp.var(x, axis=axis, keepdims=True)
    return (x - m) / jnp.sqrt(v + eps)

def _scatter_add(tgt, idx, src, axis=0):
    return tgt.at[idx].add(src)

def _segment_sum(src, seg, n):
    return jax.ops.segment_sum(src, seg, n)
kernel_name = 'mk_prb_d1_jaxref_r4_a6d52a'

def setup_inputs(seed: int=0):
    np.random.seed(seed)
    _w = jnp.asarray

    def _L0_attn_setup():
        import jax, jax.numpy as jnp
        import numpy as np
        H_HEADS = 8
        WIN = 64

        def _layernorm(x, gamma, beta, eps=1e-05):
            mu = jnp.mean(x, axis=-1, keepdims=True)
            var = jnp.var(x, axis=-1, keepdims=True)
            return (x - mu) * jax.lax.rsqrt(var + eps) * gamma + beta
        key = jax.random.key(seed)
        ks = jax.random.split(key, 8)
        B, S, D = (4, 1024, 256)
        F = 4 * D
        s = 0.02
        return {'x': jax.random.normal(ks[0], (B, S, D), dtype=jnp.float32), 'Wq': jax.random.normal(ks[1], (D, D), dtype=jnp.float32) * s, 'bq': jnp.zeros((D,), jnp.float32), 'Wk': jax.random.normal(ks[2], (D, D), dtype=jnp.float32) * s, 'bk': jnp.zeros((D,), jnp.float32), 'Wv': jax.random.normal(ks[3], (D, D), dtype=jnp.float32) * s, 'bv': jnp.zeros((D,), jnp.float32), 'Wo': jax.random.normal(ks[4], (D, D), dtype=jnp.float32) * s, 'bo': jnp.zeros((D,), jnp.float32), 'gamma': jnp.ones((D,), jnp.float32), 'beta': jnp.zeros((D,), jnp.float32), 'W1': jax.random.normal(ks[5], (D, F), dtype=jnp.float32) * s, 'b1': jnp.zeros((F,), jnp.float32), 'W2': jax.random.normal(ks[6], (F, D), dtype=jnp.float32) * s, 'b2': jnp.zeros((D,), jnp.float32)}
    _L0_attn_in = _L0_attn_setup()

    def _L0_ffn_setup():
        import jax, jax.numpy as jnp
        import numpy as np
        from jax import lax
        B, S, D = (4, 512, 256)
        E = 8
        K = 2
        F = 816
        NORM_TOPK = True
        key = jax.random.key(seed)
        ks = jax.random.split(key, 8)
        sd = 0.02
        return {'x': jax.random.normal(ks[0], (B, S, D), jnp.float32), 'gate_w': jax.random.normal(ks[1], (E, D), jnp.float32) * sd, 'gate_b': jnp.zeros((E,), jnp.float32), 'up_w': jax.random.normal(ks[2], (E, F, D), jnp.float32) * sd, 'up_b': jnp.zeros((E, F), jnp.float32), 'gp_w': jax.random.normal(ks[3], (E, F, D), jnp.float32) * sd, 'gp_b': jnp.zeros((E, F), jnp.float32), 'down_w': jax.random.normal(ks[4], (E, D, F), jnp.float32) * sd, 'down_b': jnp.zeros((E, D), jnp.float32)}
    _L0_ffn_in = _L0_ffn_setup()
    _d = {'L0_attn_x': _L0_attn_in['x'], 'L0_attn_Wq': _L0_attn_in['Wq'], 'L0_attn_bq': _L0_attn_in['bq'], 'L0_attn_Wk': _L0_attn_in['Wk'], 'L0_attn_bk': _L0_attn_in['bk'], 'L0_attn_Wv': _L0_attn_in['Wv'], 'L0_attn_bv': _L0_attn_in['bv'], 'L0_attn_Wo': _L0_attn_in['Wo'], 'L0_attn_bo': _L0_attn_in['bo'], 'L0_attn_gamma': _L0_attn_in['gamma'], 'L0_attn_beta': _L0_attn_in['beta'], 'L0_attn_W1': _L0_attn_in['W1'], 'L0_attn_b1': _L0_attn_in['b1'], 'L0_attn_W2': _L0_attn_in['W2'], 'L0_attn_b2': _L0_attn_in['b2'], 'L0_ffn_gate_w': _L0_ffn_in['gate_w'], 'L0_ffn_gate_b': _L0_ffn_in['gate_b'], 'L0_ffn_up_w': _L0_ffn_in['up_w'], 'L0_ffn_up_b': _L0_ffn_in['up_b'], 'L0_ffn_gp_w': _L0_ffn_in['gp_w'], 'L0_ffn_gp_b': _L0_ffn_in['gp_b'], 'L0_ffn_down_w': _L0_ffn_in['down_w'], 'L0_ffn_down_b': _L0_ffn_in['down_b']}
    _x0 = _d['L0_attn_x']
    _d['L0_attn_x'] = jax.random.normal(jax.random.fold_in(jax.random.key(seed), 1), (1, 4096, 256), dtype=_x0.dtype)
    del _x0
    return _d

def reference(L0_attn_x, L0_attn_Wq, L0_attn_bq, L0_attn_Wk, L0_attn_bk, L0_attn_Wv, L0_attn_bv, L0_attn_Wo, L0_attn_bo, L0_attn_gamma, L0_attn_beta, L0_attn_W1, L0_attn_b1, L0_attn_W2, L0_attn_b2, L0_ffn_gate_w, L0_ffn_gate_b, L0_ffn_up_w, L0_ffn_up_b, L0_ffn_gp_w, L0_ffn_gp_b, L0_ffn_down_w, L0_ffn_down_b):

    def _L0_attn_ref(x, Wq, bq, Wk, bk, Wv, bv, Wo, bo, gamma, beta, W1, b1, W2, b2):
        import jax, jax.numpy as jnp
        import numpy as np
        H_HEADS = 8
        WIN = 64

        def _layernorm(x, gamma, beta, eps=1e-05):
            mu = jnp.mean(x, axis=-1, keepdims=True)
            var = jnp.var(x, axis=-1, keepdims=True)
            return (x - mu) * jax.lax.rsqrt(var + eps) * gamma + beta
        B, S, D = x.shape
        w, H = (WIN, H_HEADS)
        dh = D // H
        pad = -S % w
        if pad:
            x = jnp.pad(x, ((0, 0), (0, pad), (0, 0)))
        mask = jnp.concatenate([jnp.ones((B, S), jnp.float32), jnp.zeros((B, pad), jnp.float32)], axis=1)
        Sp = S + pad
        nc = Sp // w

        def proj(W, b):
            return (x @ W + b).reshape(B, Sp, H, dh).transpose(0, 2, 1, 3).reshape(B, H, nc, w, dh)
        q = proj(Wq, bq)
        k = proj(Wk, bk)
        v = proj(Wv, bv)

        def ext3(t):
            tp = jnp.pad(t, ((0, 0), (0, 0), (1, 1), (0, 0), (0, 0)))
            return jnp.concatenate([tp[:, :, :-2], tp[:, :, 1:-1], tp[:, :, 2:]], axis=3)
        k3 = ext3(k)
        v3 = ext3(v)
        mc = mask.reshape(B, nc, w)
        mp = jnp.pad(mc, ((0, 0), (1, 1), (0, 0)))
        m3 = jnp.concatenate([mp[:, :-2], mp[:, 1:-1], mp[:, 2:]], axis=2)
        qi = jnp.arange(w)
        kj = jnp.arange(3 * w)
        band = jnp.abs(qi[:, None] - (kj[None, :] - w)) <= w
        allow = band[None, None, None, :, :] & (m3[:, None, :, None, :] > 0)
        scale = float(dh) ** (-0.5)
        scores = jnp.einsum('bhcqd,bhckd->bhcqk', q, k3) * scale
        scores = jnp.where(allow, scores, jnp.float32(-1e+30))
        p = jax.nn.softmax(scores, axis=-1)
        o = jnp.einsum('bhcqk,bhckd->bhcqd', p, v3)
        o = o.reshape(B, H, Sp, dh).transpose(0, 2, 1, 3).reshape(B, Sp, D)
        attn = o @ Wo + bo
        x = x + attn
        x = _layernorm(x, gamma, beta)
        h = jax.nn.gelu(x @ W1 + b1, approximate=False)
        x = x + (h @ W2 + b2)
        return x

    def _L0_ffn_ref(x, gate_w, gate_b, up_w, up_b, gp_w, gp_b, down_w, down_b):
        import jax, jax.numpy as jnp
        import numpy as np
        from jax import lax
        B, S, D = (4, 512, 256)
        E = 8
        K = 2
        F = 816
        NORM_TOPK = True
        bs, slen, dim = x.shape
        xf = x.reshape(-1, dim)
        N = xf.shape[0]
        scores = jax.nn.softmax(xf @ gate_w.T + gate_b, axis=-1)
        top_w, top_idx = lax.top_k(scores, K)
        if NORM_TOPK:
            top_w = top_w / (top_w.sum(-1, keepdims=True) + 1e-20)
        comb = jnp.zeros((N, E), xf.dtype).at[jnp.arange(N)[:, None], top_idx].add(top_w)

        def step(acc, p):
            uw, ub, gw, gb, dw, db, w = p
            h = jax.nn.silu((xf @ gw.T + gb) * (xf @ uw.T + ub))
            return (acc + w[:, None] * (h @ dw.T + db), None)
        y0 = jnp.zeros_like(xf)
        y, _ = lax.scan(step, y0, (up_w, up_b, gp_w, gp_b, down_w, down_b, comb.T))
        return y.reshape(bs, slen, dim)
    x = L0_attn_x
    xn = _layernorm(x, axis=-1)
    x = x + _L0_attn_ref(xn, L0_attn_Wq, L0_attn_bq, L0_attn_Wk, L0_attn_bk, L0_attn_Wv, L0_attn_bv, L0_attn_Wo, L0_attn_bo, L0_attn_gamma, L0_attn_beta, L0_attn_W1, L0_attn_b1, L0_attn_W2, L0_attn_b2) + _L0_ffn_ref(xn, L0_ffn_gate_w, L0_ffn_gate_b, L0_ffn_up_w, L0_ffn_up_b, L0_ffn_gp_w, L0_ffn_gp_b, L0_ffn_down_w, L0_ffn_down_b)
    return x

_drawn_inputs = setup_inputs


def setup_inputs(seed=0):
    import zlib

    import numpy as np

    out = dict(_drawn_inputs(seed))
    spreads = {'L0_attn_bq': (0.0, 0.8),
     'L0_attn_bk': (0.0, 2.0),
     'L0_attn_bv': (0.0, 0.49),
     'L0_attn_bo': (0.0, 0.8),
     'L0_attn_gamma': (1.0, 0.2),
     'L0_attn_beta': (0.0, 0.46),
     'L0_attn_b1': (0.0, 0.476),
     'L0_attn_b2': (0.0, 0.386),
     'L0_ffn_gate_b': (0.0, 0.376),
     'L0_ffn_up_b': (0.0, 0.8),
     'L0_ffn_gp_b': (0.0, 0.8),
     'L0_ffn_down_b': (0.0, 0.58)}
    factors = {'L0_attn_Wq': 8.0,
     'L0_attn_Wk': 8.0,
     'L0_attn_Wv': 8.0,
     'L0_attn_Wo': 3.352,
     'L0_ffn_up_w': 5.208,
     'L0_ffn_gp_w': 5.224,
     'L0_ffn_down_w': 4.951}
    for name, (base, spread) in spreads.items():
        noise = np.random.default_rng([zlib.crc32(name.encode()), seed]).standard_normal(out[name].shape)
        drawn = base * np.exp(spread * noise) if base else spread * noise
        out[name] = jnp.asarray(drawn.astype(out[name].dtype))
    for name, factor in factors.items():
        out[name] = (out[name] * factor).astype(out[name].dtype)
    return out
```

```python
import concourse.bass as bass
from concourse import mybir
from contextlib import ExitStack
import numpy as np

F32, F32R = mybir.dt.float32, mybir.dt.float32r
I32, U32, BF16 = mybir.dt.int32, mybir.dt.uint32, mybir.dt.bfloat16
ALU, ACT, AX = mybir.AluOpType, mybir.ActivationFunctionType, mybir.AxisListType
ds = bass.ds

P = 128
S, D, H, DH, WIN = 4096, 256, 8, 32, 64
KC = D // P
F1 = 4 * D
FC1 = F1 // P
E, F = 8, 816
NT = S // P
GT = 4
GN = GT * P
NG = S // GN
WT = GT + 1
WN = WT * P
PADROWS = S + 2 * WIN
BT = 2 * P
NB = (2 * S - E) // BT + E
SLOTS = NB * BT
REC = D + 2
FCH = 7
FR = F - (FCH - 1) * P
GRW = WIN + FR
GUC = 2 * KC * P
GUW = (FCH - 1) * GUC + KC * GRW
DWW = FCH * D
ROWS_AT = 4
DV = 4
GA = 3
BIW = 2 * FCH
EPS = 1e-5
SCALE = float(DH) ** -0.5
NEG = -1e30

C_ID, C_TRI, C_ONE, C_REV, C_TOK, C_BLK = 0, P, 2 * P, 3 * P, 3 * P + E, 3 * P + E + NT
C_EPS = C_BLK + NB
C_HOT = C_EPS + 1
C_W = C_HOT + 1
C_MID, C_LAST, C_FIRST = C_W, C_W + 2 * P, C_W + 4 * P
C_ALL = C_W + 6 * P


def constants():
    c = np.zeros((P, C_ALL), np.float32)
    q, k = np.arange(P)[:, None], np.arange(2 * P)[None, :]
    band = (k >= q) & (k <= q + 2 * WIN)
    c[:, C_ID:C_ID + P] = np.eye(P)
    c[:, C_MID:C_MID + 2 * P] = np.where(band, 0, NEG)
    c[:, C_LAST:C_LAST + 2 * P] = np.where(band & (k < P + WIN), 0, NEG)
    c[:, C_FIRST:C_FIRST + 2 * P] = np.where(band & (k >= WIN), 0, NEG)
    c[:, C_TRI:C_TRI + P] = np.arange(P)[:, None] < np.arange(P)[None, :]
    c[:, C_ONE:C_ONE + P] = 1
    c[:, C_REV:C_REV + E] = E - np.arange(E)
    c[:, C_TOK:C_TOK + NT] = np.arange(P)[:, None] + P * np.arange(NT)[None, :]
    c[:, C_BLK:C_BLK + NB] = BT * np.arange(NB)[None, :]
    c[:, C_EPS] = EPS
    c[FR, C_HOT] = 1
    return c


PROJ_X = ["XT0", "XT1", "XT2"]
PROJ = ["Q0", "Q1", "K0", "K1", "K2", "K3"] + [f"V{j}" for j in range(WT)]
TURN = (["O0", "O1", "OT0", "A0", "O2", "OT1", "A1", "O3", "OT2", "A2"] + PROJ_X + ["OT3", "A3"] + PROJ
        + ["X0", "X1"] + [f"F{c}" for c in range(FC1)] + ["Y0", "Y1"])
LEAD = PROJ_X + PROJ
LAST = [u for u in TURN if u not in LEAD]
HI = ("XT", "OT", "Q", "K", "X")
assert len(TURN) % 2 == 0 and len(LEAD) % 2 == 0
ROUTE_EXP, ROUTE_PICKS = 14, 15


def m_use(name, g, last=False):
    if g is None:
        n = LEAD.index(name)
        return n % 2, n // 2
    n = (LAST if last else TURN).index(name)
    return n % 2, g * (len(TURN) // 2) + (len(LEAD) + n) // 2


def hi_use(name, g, last=False):
    def before(uses):
        return sum(u.startswith(HI) for u in uses)
    if g is None:
        return before(LEAD[:LEAD.index(name)])
    uses = LAST if last else TURN
    return g * before(TURN) + before(LEAD) + before(uses[:uses.index(name)])


def program(nc, x, wq, wk, wv, wo, w1, w2, gate, rows, cols, gu_rec, dw_rec, bi_rec, const, out):
    xn_dram = nc.dram_tensor("xn_dram", (PADROWS, D), F32, kind="Internal").ap()
    xs_dram = nc.dram_tensor("xs_dram", (SLOTS, REC), F32, kind="Internal").ap()
    y_dram = nc.dram_tensor("y_dram", (2 * S, D), F32, kind="Internal").ap()

    with ExitStack() as ctx:
        def sems(names):
            return [ctx.enter_context(nc.semaphore(n)) for n in names.split()]

        def phase():
            stack = ExitStack()

            def tile(name, shape, dtype=F32):
                return stack.enter_context(nc.sbuf_tensor(name, [P, *shape] if isinstance(shape, list) else shape, dtype))
            return stack, tile

        bank = [ctx.enter_context(nc.psum_tensor(f"bank{i}", [P, 512], F32)) for i in range(8)]
        s_bank, t_bank, m_bank = bank[0:4], bank[4:6], bank[6:8]

        whole, tile = phase()
        ctx.enter_context(whole)
        cst = tile("cst", [C_W])
        ident, eps = cst[:, C_ID:C_ID + P], cst[:, C_EPS:C_EPS + 1]
        xn = tile("xn", [NT, D])
        blk_e = tile("blk_e", (1, 2 * NB), I32)

        dense, tile = phase()
        wq_s, wk_s, wv_s, wo_s = (tile(n, [2, KC, D], F32R) for n in ("wq_s", "wk_s", "wv_s", "wo_s"))
        w1_s = tile("w1_s", [2, KC, F1], F32R)
        w2_s = tile("w2_s", [2, FC1, D], F32R)
        masks = tile("masks", [3, 2 * P])
        mid, end, begin = (masks[:, n, :] for n in range(3))
        rowb = tile("rowb", [5, D])
        bv_b, bo_b, gam_b, bet_b, b2_b = (rowb[:, n, :] for n in range(5))
        gb_b = tile("gb_b", [E])
        col = tile("col", [4 + FC1])
        slot = tile("slot", [2, NT], U32)
        meta = tile("meta", [2, NT, 2])
        stage = tile("stage", [2, 2, REC])
        sidx = tile("sidx", [4], U32)
        zrec = tile("zrec", [REC])
        first, tile = phase()
        gate_s = tile("gate_s", [KC, E])
        wraw = tile("wraw", [2, KC * F1])
        xg = tile("xg", [2, GT, D])
        xt = tile("xt", [2, KC, GN])
        st6 = tile("st6", [2, GT, 6])
        mv = tile("mv", [2, GT, 2])
        sd = tile("sd", [2, GT])
        rstd = tile("rstd", [2, GT])
        rt = [tile(f"rt{n}", [NT, E]) for n in range(12)]
        r1 = [tile(f"r1_{n}", [NT]) for n in range(10)]
        r8 = [tile(f"r8_{n}", [E]) for n in range(6)]
        r8i = [tile(f"r8i_{n}", [E], I32) for n in range(2)]
        rb = tile("rb", [NB, E])
        rbs, new = tile("rbs", [NB]), tile("new", [NB])
        first.close()
        second, tile = phase()
        xwin = tile("xwin", [WT, D])
        xres = tile("xres", [GT, D])
        xw_h, xw_l = (tile(n, [KC, WN], F32R) for n in ("xw_h", "xw_l"))
        q_h, q_l = (tile(n, [KC, GN], F32R) for n in ("q_h", "q_l"))
        k_h, k_l = (tile(n, [KC, WN], F32R) for n in ("k_h", "k_l"))
        v = tile("v", [WT, D])
        mask0 = tile("mask0", [2 * P])
        pt = tile("pt", [2, 4, P])
        mx, nmx, sums = (tile(n, [2, H]) for n in ("mx", "nmx", "sums"))
        rsum = tile("rsum", [H])
        on = tile("on", [2, D])
        ot_h, ot_l = (tile(n, [KC, P], F32R) for n in ("ot_h", "ot_l"))
        t1 = tile("t1", [D])
        u1 = tile("u1", [GT, D])
        st2, mv2, sd2, rs2 = tile("st2", [GT, 6]), tile("mv2", [GT, 2]), tile("sd2", [GT]), tile("rs2", [GT])
        x2 = tile("x2", [GT, D])
        x2t_h, x2t_l = (tile(n, [KC, GN], F32R) for n in ("x2t_h", "x2t_l"))
        h1 = tile("h1", [2, GN])
        h_h = tile("h_h", [FC1, GN], F32R)
        shared, tile = phase()
        sm = tile("sm", [2, H, 2 * P])
        shared.close()
        shared, tile = phase()
        h_l = tile("h_l", [FC1, GN], F32R)
        shared.close()
        second.close()
        dense.close()
        third, tile = phase()
        raw_gu = tile("raw_gu", [2, GUW])
        raw_dw = tile("raw_dw", [2, DWW])
        bias = tile("bias", [2, BIW])
        gu_s = tile("gu_s", [2, 2, GUW], F32R)
        dw_s = tile("dw_s", [2, 2, DWW], F32R)
        ht = tile("ht", [2, 2, FCH, BT], F32R)
        xr = tile("xr", [2, 2, REC])
        xt_h, xt_l = (tile(n, [2, KC, BT], F32R) for n in ("xt_h", "xt_l"))
        gs, hf = (tile(n, [4, BT]) for n in ("gs", "hf"))
        ys = tile("ys", [2, 2, D])
        dest = tile("dest", [4], U32)
        wgt = tile("wgt", [2, 2])
        third.close()
        fourth, tile = phase()
        yg = tile("yg", [2, 2, GT, D])
        fourth.close()

        const_loaded, small_loaded, zrec_ready, xs_filled, pads_filled = sems("const_loaded small_loaded zrec_ready xs_filled pads_filled")
        wraw_loaded = sems("wraw_loaded_0 wraw_loaded_1")
        wraw_hi, wraw_split = sems("wraw_hi wraw_split")
        xg_loaded = sems("xg_loaded_0 xg_loaded_1")
        stats6, stats_ready, sd_ready, rstd_ready, xn_ready, xn_kept, xn_stored = sems("stats6 stats_ready sd_ready rstd_ready xn_ready xn_kept xn_stored")
        xt_full, xt_copied, gate_full = sems("xt_full xt_copied gate_full")
        route, route_exp, counts_full, slots_ready = sems("route route_exp counts_full slots_ready")
        staged, = sems("staged")
        scattered = sems("scattered_0 scattered_1")
        win_loaded, xres_loaded = sems("win_loaded xres_loaded")
        m_full, m_free = sems("m_full_0 m_full_1"), sems("m_free_0 m_free_1")
        m_hi, = sems("m_hi")
        s_full, s_free = sems("s_full_0 s_full_1 s_full_2 s_full_3"), sems("s_free_0 s_free_1 s_free_2 s_free_3")
        t_full, t_free = sems("t_full_0 t_full_1"), sems("t_free_0 t_free_1")
        neg_max, probs_ready, rsum_ready, mask_set = sems("neg_max probs_ready rsum_ready mask_set")
        res_ready, pre_ready, ln6, ln_stats, ln_sd, ln_rstd, scaled, x2_ready, x2_half, x2_summed = sems(
            "res_ready pre_ready ln6 ln_stats ln_sd ln_rstd scaled x2_ready x2_half x2_summed")
        gelu_hi, gelu_split = sems("gelu_hi gelu_split")
        gu_loaded, dw_loaded, bi_loaded, xr_loaded = (sems(f"{n}_0 {n}_1") for n in ("gu_loaded", "dw_loaded", "bi_loaded", "xr_loaded"))
        gu_hi, gu_hi_act, gu_split, dw_hi, dw_split, dw_split_pool = sems("gu_hi gu_hi_act gu_split dw_hi dw_split dw_split_pool")
        ct_full, ct_hi, ct_split = sems("ct_full ct_hi ct_split")
        gu_full, gs_ready, z_ready, hf_ready, hhi_ready, h_split, pad_low, pad_high = sems("gu_full gs_ready z_ready hf_ready hhi_ready h_split pad_low pad_high")
        y_full, y_ready, y_kept = sems("y_full y_ready y_kept")
        y_sent = sems("y_sent_0 y_sent_1")
        yg_loaded = sems("yg_loaded_0 yg_loaded_1")
        sum_1, sum_2, out_stored = sems("sum_1 sum_2 out_stored")

        x_g = x.rearrange("(g t p) d -> g p t d", t=GT, p=P)
        out_g = out.rearrange("(g t p) d -> g p t d", t=GT, p=P)

        DENSE = [(wq, wq_s, KC, D), (wk, wk_s, KC, D), (wv, wv_s, KC, D), (wo, wo_s, KC, D), (w1, w1_s, KC, F1), (w2, w2_s, FC1, D)]

        passed = dict(zip((mybir.EngineType.SP, mybir.EngineType.Pool, mybir.EngineType.DVE), sems("passed_sp passed_pool passed_dve")))

        def one(ap):
            return ap.rearrange("p o d -> p (o d)")

        def spread(ap, shape):
            return ap.rearrange("p (n o) -> p n o", o=1).to_broadcast(shape)

        def across(ap, shape):
            return ap.rearrange("p (o n) -> p o n", o=1).to_broadcast(shape)

        def wait_dense_done(eng):
            b, n = m_use("Y1", NG - 1, True)
            eng.wait_ge(m_free[b], n + 1)
            for k in range(2):
                eng.wait_ge(scattered[k], 16 * NT)

        def ring(c):
            return c % 3 if c < FCH - 1 else 3

        def before(b, c):
            n = FCH * b + (c - 2 if 3 <= c < FCH - 1 else c - 3 if c < 3 else 0)
            return None if isinstance(b, int) and n <= 0 else n

        def settle(eng):
            eng.sem_inc(passed[eng.engine])

        def through(b, p, n):
            return (b - p) * (n // 2) + n

        def blocks_of(eng, body):
            body(0, 0)
            body(1, 1)
            with eng.Fori(0, (NB - 3) // 2) as i:
                body(i * 2 + 2, 0)
                body(i * 2 + 3, 1)
            body(NB - 1, (NB - 1) % 2)

        def gu_cols(c):
            return slice(c * GUC, (c + 1) * GUC if c < FCH - 1 else GUW)

        block = ctx.enter_context(nc.Block())

        @block.sync
        def _(sp):
            sp.dma_start(xg[:, 0], x_g[0]).then_inc(xg_loaded[0], 16)
            sp.dma_start(cst[:, :], const[:, 0:C_W]).then_inc(const_loaded, 16)
            sp.dma_start(xg[:, 1], x_g[1]).then_inc(xg_loaded[1], 16)
            sp.dma_start(gate_s[:, :, :], gate).then_inc(small_loaded, 16)
            sp.dma_start(gb_b[:, :], rows[5:6, 0:E].to_broadcast([P, E])).then_inc(small_loaded, 16)
            sp.dma_start(col[:, :], cols).then_inc(small_loaded, 16)
            sp.dma_start(masks[:, :, :].rearrange("p n c -> p (n c)"), const[:, C_W:C_ALL]).then_inc(small_loaded, 16)
            for n in range(5):
                sp.dma_start(rowb[:, n, :], rows[n:n + 1, :].to_broadcast([P, D])).then_inc(small_loaded, 16)

            def store_xn(g, par):
                sp.wait_ge(xn_ready, g * GT + GT)
                settle(sp)
                sp.dma_start(xn_dram[ds(g * GN + WIN, GN), :].rearrange("(t p) d -> p t d", p=P), xg[:, par]).then_inc(xn_stored, 16)
            with sp.Fori(0, NG // 2 - 1) as i:
                for par in range(2):
                    g = i * 2 + par
                    store_xn(g, par)
                    sp.wait_ge(xn_stored, g * 16 + 16)
                    settle(sp)
                    sp.wait_ge(xn_kept, g + 1)
                    settle(sp)
                    sp.wait_ge(xt_full, g + 1)
                    settle(sp)
                    sp.dma_start(xg[:, par], x_g[ds(g + 2, 1)].rearrange("o p t d -> p (o t) d")).then_inc(xg_loaded[par], 16)
            for g in (NG - 2, NG - 1):
                store_xn(g, g % 2)
            sp.wait_ge(zrec_ready, 2)
            sp.dma_start(xn_dram[0:WIN, :], zrec[0:WIN, 0:D]).then_inc(pads_filled, 16)
            sp.dma_start(xn_dram[WIN + S:PADROWS, :], zrec[0:WIN, 0:D]).then_inc(pads_filled, 16)
            sp.dma_start(xs_dram.rearrange("(n p) c -> p n c", p=P), across(zrec[:, :], [P, SLOTS // P, REC])).then_inc(xs_filled, 16)

            sp.wait_ge(pads_filled, 32)
            sp.wait_ge(xn_stored, 16 * NG)
            sp.wait_ge(slots_ready, 1)
            sp.wait_ge(wraw_split, len(DENSE))

            def load_group(g):
                sp.dma_start(xwin[:, :, :], xn_dram[ds(g * GN, WN), :].rearrange("(t p) d -> p t d", p=P)).then_inc(win_loaded, 16)

            def load_residual(g):
                sp.dma_start(xres[:, :, :], x_g[ds(g, 1)].rearrange("o p t d -> p (o t) d")).then_inc(xres_loaded, 16)
            load_group(0)
            load_residual(0)
            b, n = m_use("XT2", None)
            sp.wait_ge(m_full[b], n + 1)
            settle(sp)
            load_group(1)
            with sp.Fori(0, NG - 2) as g:
                b, n = m_use("XT2", g)
                sp.wait_ge(m_full[b], n + 1)
                settle(sp)
                load_group(g + 2)
                b, n = m_use("Y1", g)
                sp.wait_ge(m_free[b], n + 1)
                settle(sp)
                load_residual(g + 1)
            b, n = m_use("Y1", NG - 2)
            sp.wait_ge(m_free[b], n + 1)
            settle(sp)
            load_residual(NG - 1)

            wait_dense_done(sp)
            sp.wait_ge(xs_filled, 16)

            def load_record(dst, records, b, loaded):
                e = sp.value_load(blk_e[0:1, ds(b, 1)], min_val=0, max_val=E - 1)
                new = sp.value_load(blk_e[0:1, ds(b + NB, 1)], min_val=0, max_val=1)
                sp.dma_start(dst, records[ds(e, 1)].rearrange("o p w -> p (o w)"), cond=new).then_inc(loaded, 16)

            def load_gu(b, p, wait=True):
                if wait:
                    sp.wait_ge(gu_split, (b - 1) * FCH)
                settle(sp)
                load_record(raw_gu[:, p], gu_rec, b, gu_loaded[p])

            def load_rows_of(b, p, wait=True):
                if wait:
                    sp.wait_ge(ct_full, b - 1)
                    settle(sp)
                    sp.wait_ge(y_kept, (b - 1) * 2)
                    settle(sp)
                sp.dma_start(xr[:, p], xs_dram[ds(b * BT, BT), :].rearrange("(t p) c -> p t c", p=P)).then_inc(xr_loaded[p], 16)

            def load_dw(b, p, wait=True):
                if wait:
                    sp.wait_ge(dw_split, (b - 1) * DV)
                    settle(sp)
                    sp.wait_ge(dw_split_pool, (b - 1) * (FCH - DV))
                settle(sp)
                load_record(raw_dw[:, p], dw_rec, b, dw_loaded[p])

            def load_bias(b, p, wait=True):
                if wait:
                    sp.wait_ge(z_ready, (b - 1) * FCH)
                settle(sp)
                load_record(bias[:, p], bi_rec, b, bi_loaded[p])
            load_gu(0, 0, False)
            load_rows_of(0, 0, False)
            load_bias(0, 0, False)
            load_gu(1, 1, False)
            load_rows_of(1, 1, False)
            load_bias(1, 1, False)
            load_dw(0, 0, False)
            load_gu(2, 0)
            load_dw(1, 1, False)
            load_rows_of(2, 0)
            load_bias(2, 0)
            with sp.Fori(0, (NB - 3) // 2) as i:
                for b, p in ((i * 2 + 3, 1), (i * 2 + 4, 0)):
                    load_gu(b, p)
                    load_dw(b - 1, 1 - p)
                    load_rows_of(b, p)
                    load_bias(b, p)
            load_dw(NB - 1, (NB - 1) % 2)

            sp.wait_ge(y_sent[0], 32 * ((NB + 1) // 2))
            sp.wait_ge(y_sent[1], 32 * (NB // 2))

            def load_rows(g, p):
                for k in range(2):
                    sp.dma_start(yg[:, p, k], y_dram[ds(g * GN + k * S, GN), :].rearrange("(t p) d -> p t d", p=P)).then_inc(yg_loaded[p], 16)

            def store_out(g):
                sp.wait_ge(sum_2, g + 1)
                settle(sp)
                sp.dma_start(out_g[ds(g, 1)].rearrange("o p t d -> p (o t) d"), xn[:, ds(g * GT, GT), :]).then_inc(out_stored, 16)
            load_rows(0, 0)
            load_rows(1, 1)
            with sp.Fori(0, NG // 2 - 1) as i:
                for p in range(2):
                    store_out(i * 2 + p)
                    load_rows(i * 2 + (p + 2), p)
            store_out(NG - 2)
            store_out(NG - 1)
            sp.wait_ge(out_stored, 16 * NG)

        @block.gpsimd
        def _(pool):
            def load_dense(n):
                src, _, chunks, width = DENSE[n]
                if n >= 2:
                    pool.wait_ge(wraw_split, n - 1)
                pool.dma_start(wraw[:, n % 2, 0:chunks * width].rearrange("p (c n) -> p c n", c=chunks),
                               src.rearrange("(c p) n -> p c n", p=P)).then_inc(wraw_loaded[n % 2], 16)
            load_dense(0)
            nc.gpsimd.memset(zrec[:, :], 0.0).then_inc(zrec_ready, 1)
            pool.wait_ge(zrec_ready, 1)
            nc.gpsimd.iota(zrec[:, D:D + 1].bitcast(I32), [[0, 1]], base=2 * S, channel_multiplier=1).then_inc(zrec_ready, 1)
            for n, (_, dst, chunks, width) in enumerate(DENSE):
                if n + 1 < len(DENSE):
                    load_dense(n + 1)
                pool.wait_ge(wraw_loaded[n % 2], 16 * (n // 2 + 1))
                w = wraw[:, n % 2, 0:chunks * width]
                hi, lo = (dst[:, part].rearrange("p c n -> p (c n)") for part in range(2))
                nc.gpsimd.tensor_copy(hi, w).then_inc(wraw_hi, 1)
                pool.wait_ge(wraw_hi, n + 1)
                nc.gpsimd.tensor_tensor(lo, w, hi.bitcast(F32), ALU.subtract).then_inc(wraw_split, 1)

            def scatter(g):
                for j in range(GT):
                    par, t = j % 2, g * GT + j
                    for k in range(2):
                        index = sidx[:, 2 * par + k:2 * par + k + 1]
                        nc.gpsimd.tensor_copy(stage[:, par, k, 0:D], one(xn[:, ds(t, 1), :])).then_inc(staged, 1)
                        nc.gpsimd.tensor_copy(stage[:, par, k, D:REC], one(meta[:, k, ds(t, 1), :])).then_inc(staged, 1)
                        nc.gpsimd.tensor_copy(index, slot[:, k, ds(t, 1)]).then_inc(staged, 1)
                        pool.wait_ge(staged, t * 6 + (3 * k + 3))
                        settle(pool)
                        nc.gpsimd.indirect_dma_start(xs_dram, bass.IndirectOffsetOnAxis(index, 0), stage[:, par, k, :], None).then_inc(scattered[k], 16)
                    if par:
                        for k in range(2):
                            pool.wait_ge(scattered[k], t * 16 + 16)
                        settle(pool)

            def residual(g):
                pool.wait_ge(xres_loaded, g * 16 + 16)
                for j in range(GT):
                    pool.wait_ge(x2_ready, g * GT + (j + 1))
                    nc.gpsimd.tensor_tensor(xres[:, j, :], xres[:, j, :], x2[:, j, :], ALU.add).then_inc(x2_half, 1)
                    pool.wait_ge(x2_half, g * GT + (j + 1))
                    nc.gpsimd.tensor_tensor(xres[:, j, :], xres[:, j, :], b2_b, ALU.add).then_inc(x2_summed, 1)
            pool.wait_ge(small_loaded, 16 * 9)
            pool.wait_ge(xs_filled, 16)
            pool.wait_ge(slots_ready, 1)
            pool.wait_ge(xn_kept, NG)
            with pool.Fori(0, NG) as g:
                scatter(g)
                residual(g)

            wait_dense_done(pool)
            for p in range(2):
                nc.gpsimd.memset(ht[:, p, 1, FCH - 1, :].bitcast(F32), 0.0).then_inc(pad_low, 1)
            pool.wait_ge(pad_low, 2)

            def keep_meta(b, p):
                pool.wait_ge(xr_loaded[p], through(b, p, 16))
                if not isinstance(b, int) or b >= 2:
                    pool.wait_ge(y_sent[p], (b - p) * 16)
                    pool.wait_ge(y_ready, b - 1)
                settle(pool)
                nc.gpsimd.tensor_copy(dest[:, 2 * p:2 * p + 2], xr[:, p, :, D].bitcast(U32)).then_inc(y_kept, 1)
                nc.gpsimd.tensor_copy(wgt[:, p, :], xr[:, p, :, D + 1]).then_inc(y_kept, 1)

            def dw_low(b, p, c):
                cs = slice(c * D, (c + 1) * D)
                if c == DV:
                    pool.wait_ge(dw_hi, b * 2 + 2)
                nc.gpsimd.tensor_tensor(dw_s[:, p, 1, cs], raw_dw[:, p, cs], dw_s[:, p, 0, cs].bitcast(F32), ALU.subtract).then_inc(dw_split_pool, 1)

            def h_low(b, p, c):
                m = P if c < FCH - 1 else FR
                pool.wait_ge(hhi_ready, b * FCH + (c + 1))
                nc.gpsimd.tensor_tensor(ht[0:m, p, 1, c, :], hf[0:m, ring(c), :], ht[0:m, p, 0, c, :].bitcast(F32), ALU.subtract).then_inc(h_split, 1)

            def send(b, p):
                pool.wait_ge(y_ready, b + 1)
                settle(pool)
                for t in range(2):
                    index = dest[:, 2 * p + t:2 * p + t + 1]
                    nc.gpsimd.indirect_dma_start(y_dram, bass.IndirectOffsetOnAxis(index, 0), ys[:, p, t, :], None,
                                                 bounds_check=2 * S - 1, oob_is_err=False).then_inc(y_sent[p], 16)

            def body(b, p):
                for c in range(FCH):
                    h_low(b, p, c)
                    if c == 2:
                        keep_meta(b, p)
                for c in range(DV, FCH):
                    dw_low(b, p, c)
                if not isinstance(b, int) or b >= 1:
                    send(b - 1, 1 - p)
            blocks_of(pool, body)
            send(NB - 1, (NB - 1) % 2)

        @block.scalar
        def _(act):
            def sqrt_group(g, par):
                act.wait_ge(stats_ready, g * GT + GT)
                nc.scalar.activation(sd[:, par], mv[:, par, :, 1], ACT.Sqrt, bias=eps).then_inc(sd_ready, 1)

            def copy_group(g, par, pair):
                act.wait_ge(xn_ready, g * GT + GT)
                nc.scalar.activation(xn[:, ds(g * GT, GT), :], xg[:, par], ACT.Copy).then_inc(xn_kept, 1)
                act.wait_ge(xt_full, g + 1)
                act.wait_ge(gate_full, pair * 2 + 2)
                for k in range(KC):
                    nc.scalar.activation(xt[:, par, k, :], bank[2 * par + k][:, :], ACT.Copy).then_inc(xt_copied, 1)
            act.sem_inc(xt_copied, 4)
            act.wait_ge(const_loaded, 16)
            with act.Fori(0, NG // 2) as i:
                for par in range(2):
                    sqrt_group(i * 2 + par, par)
                    copy_group(i * 2 + par, par, i)
            act.wait_ge(route, ROUTE_EXP)
            nc.scalar.activation(rt[8][:, :, :], rt[7][:, :, :], ACT.Exp).then_inc(route_exp, 1)
            nc.scalar.activation(r1[6][:, :], r1[5][:, :], ACT.Exp).then_inc(route_exp, 1)

            def full(name, g, last=False):
                b, n = m_use(name, g, last)
                act.wait_ge(m_full[b], n + 1)
                return m_bank[b]

            def window_hi(g):
                for n in range(3):
                    w = BT if n < 2 else P
                    bk = full(f"XT{n}", g)
                    nc.scalar.activation(xw_h[:, :, n * BT:n * BT + w], bk[:, :].rearrange("p (k c) -> p k c", k=KC)[:, :, 0:w], ACT.Copy).then_inc(m_hi, 1)

            def q_hi(g):
                for c in range(KC):
                    bk = full(f"Q{c}", g)
                    nc.scalar.activation(q_h[:, c, :], bk[:, :], ACT.Identity, bias=col[:, c:c + 1]).then_inc(m_hi, 1)

            def k_hi(g):
                for n in range(4):
                    c, half = n // 2, n % 2
                    bk = full(f"K{n}", g)
                    nc.scalar.activation(k_h[:, c, half * WN // 2:(half + 1) * WN // 2], bk[:, 0:WN // 2], ACT.Identity, bias=col[:, 2 + c:3 + c]).then_inc(m_hi, 1)

            def probs(g, j):
                act.wait_ge(neg_max, g * GT + (j + 1))
                for r in range(4):
                    for c in range(KC):
                        h = r + 4 * c
                        nc.scalar.activation(sm[:, j % 2, h, :], sm[:, j % 2, h, :], ACT.Exp, bias=nmx[:, j % 2, h:h + 1], scale=SCALE,
                                             accum_out=sums[:, j % 2, h:h + 1]).then_inc(probs_ready, 1)

            def pt_copy(g, j):
                for u in (1, 3):
                    act.wait_ge(t_full[1], (g * GT + j) * 2 + (u // 2 + 1))
                    nc.scalar.activation(pt[:, 1].rearrange("p a n -> p (a n)"), t_bank[1][:, :], ACT.Copy).then_inc(t_free[1], 1)

            def ot_hi(g, j, last):
                bk = full(f"OT{j}", g, last)
                nc.scalar.activation(ot_h[:, :, :].rearrange("p k n -> p (k n)"), bk[:, 0:D], ACT.Copy).then_inc(m_hi, 1)

            def x2_hi(g, last):
                for n in range(2):
                    bk = full(f"X{n}", g, last)
                    nc.scalar.activation(x2t_h[:, :, n * BT:(n + 1) * BT], bk[:, :].rearrange("p (k c) -> p k c", k=KC), ACT.Copy).then_inc(m_hi, 1)

            def gelu(g, last):
                for c in range(FC1):
                    bk = full(f"F{c}", g, last)
                    b, n = m_use(f"F{c}", g, last)
                    if c >= 2:
                        act.wait_ge(gelu_split, g * FC1 + (c - 1))
                    nc.scalar.activation(h1[:, c % 2, :], bk[:, :], ACT.Gelu, bias=col[:, 4 + c:5 + c]).then_inc(m_free[b], 1)
                    act.wait_ge(m_free[b], n + 1)
                    nc.scalar.activation(h_h[:, c, :], h1[:, c % 2, :], ACT.Copy).then_inc(gelu_hi, 1)

            act.sem_inc(t_free[1], 1)
            act.wait_ge(small_loaded, 16 * 9)
            window_hi(None)
            q_hi(None)
            k_hi(None)

            def turn(g, last):
                probs(g, 0)
                probs(g, 1)
                pt_copy(g, 0)
                probs(g, 2)
                pt_copy(g, 1)
                ot_hi(g, 0, last)
                probs(g, 3)
                pt_copy(g, 2)
                ot_hi(g, 1, last)
                pt_copy(g, 3)
                ot_hi(g, 2, last)
                if not last:
                    window_hi(g)
                ot_hi(g, 3, last)
                if not last:
                    q_hi(g)
                act.wait_ge(ln_stats, g * GT + GT)
                nc.scalar.activation(sd2[:, :], mv2[:, :, 1], ACT.Sqrt, bias=eps).then_inc(ln_sd, 1)
                if not last:
                    k_hi(g)
                x2_hi(g, last)
                gelu(g, last)
            with act.Fori(0, NG - 1) as g:
                turn(g, False)
            turn(NG - 1, True)

            wait_dense_done(act)

            def rows_hi(b, p):
                act.wait_ge(ct_full, b + 1)
                nc.scalar.activation(xt_h[:, p], bank[4][:, :].rearrange("p (k c) -> p k c", k=KC), ACT.Copy).then_inc(ct_hi, 1)

            def gate_bias(b, p, c):
                act.wait_ge(gu_full, b * FCH + (c + 1))
                if c < FCH - 1:
                    nc.scalar.activation(gs[:, ring(c), :], bank[ring(c)][:, 0:BT], ACT.Identity, bias=bias[:, p, c:c + 1]).then_inc(gs_ready, 1)
                else:
                    nc.scalar.activation(gs[WIN:WIN + FR, 3, :], bank[3][0:FR, 0:BT], ACT.Identity, bias=bias[0:FR, p, c:c + 1]).then_inc(gs_ready, 1)

            def silu(b, p, c):
                m = P if c < FCH - 1 else FR
                act.wait_ge(z_ready, b * FCH + (c + 1))
                nc.scalar.activation(hf[0:m, ring(c), :], hf[0:m, ring(c), :], ACT.Silu).then_inc(hf_ready, 1)
                if c == 0 and (not isinstance(b, int) or b >= 2):
                    act.wait_ge(y_full, b - 1)
                act.wait_ge(hf_ready, b * FCH + (c + 1))
                nc.scalar.activation(ht[0:m, p, 0, c, :], hf[0:m, ring(c), :], ACT.Copy).then_inc(hhi_ready, 1)

            def gu_high(b, p, c):
                if c == FCH - GA:
                    act.wait_ge(gu_loaded[p], through(b, p, 16))
                    if not isinstance(b, int) or b >= 2:
                        act.wait_ge(gu_full, (b - 1) * FCH)
                nc.scalar.activation(gu_s[:, p, 0, gu_cols(c)], raw_gu[:, p, gu_cols(c)], ACT.Copy).then_inc(gu_hi_act, 1)

            def dw_high(b, p):
                act.wait_ge(dw_loaded[p], through(b, p, 16))
                if not isinstance(b, int) or b >= 2:
                    act.wait_ge(y_full, b - 1)
                for cs in (slice(0, DV * D), slice(DV * D, DWW)):
                    nc.scalar.activation(dw_s[:, p, 0, cs], raw_dw[:, p, cs], ACT.Copy).then_inc(dw_hi, 1)

            def body(b, p):
                act.wait_ge(bi_loaded[p], through(b, p, 16))
                more = not isinstance(b, int) or b < NB - 1
                for c in range(FCH + 1):
                    if c < FCH:
                        gate_bias(b, p, c)
                    if c >= 1:
                        silu(b, p, c - 1)
                    if c == ROWS_AT and more:
                        rows_hi(b + 1, 1 - p)
                if more:
                    for c in range(FCH - GA, FCH):
                        gu_high(b + 1, 1 - p, c)
                dw_high(b, p)
            act.wait_ge(pad_high, 2)
            for c in range(FCH - GA, FCH):
                gu_high(0, 0, c)
            rows_hi(0, 0)
            blocks_of(act, body)

        @block.vector
        def _(dve):
            dve.wait_ge(const_loaded, 16)
            with dve.Fori(0, NG // 2) as i:
                for par in range(2):
                    g = i * 2 + par
                    dve.wait_ge(xg_loaded[par], i * 16 + 16)
                    for t in range(GT):
                        nc.vector.bn_stats(st6[:, par, t, :], xg[:, par, t, :]).then_inc(stats6, 1)
                    dve.wait_ge(stats6, g * GT + GT)
                    settle(dve)
                    for t in range(GT):
                        nc.vector.bn_aggr(mv[:, par, t, :], st6[:, par, t, :]).then_inc(stats_ready, 1)
                    dve.wait_ge(sd_ready, g + 1)
                    nc.vector.reciprocal(rstd[:, par], sd[:, par]).then_inc(rstd_ready, 1)
                    dve.wait_ge(rstd_ready, g + 1)
                    for t in range(GT):
                        nc.vector.tensor_scalar(xg[:, par, t, :], xg[:, par, t, :], mv[:, par, t, 0:1], rstd[:, par, t:t + 1],
                                                ALU.subtract, ALU.mult).then_inc(xn_ready, 1)

            steps = [0]

            def link(ins):
                steps[0] += 1
                ins.then_inc(route, 1)
                dve.wait_ge(route, steps[0])
            big, tok = [P, NT, E], [P, NT]
            rev = across(cst[:, C_REV:C_REV + E], big)
            logits, one1, one2 = rt[0], rt[2], rt[6]
            dve.wait_ge(gate_full, NG + 2)
            dve.wait_ge(small_loaded, 16 * 9)
            link(nc.vector.tensor_tensor(logits[:, :, :], bank[4][:, 0:NT * E].rearrange("p (t e) -> p t e", e=E), across(gb_b[:, :], big), ALU.add))

            def pick(values, top, sel, scratch, index):
                link(nc.vector.tensor_reduce(top[:, :], values[:, :, :], AX.X, ALU.max))
                link(nc.vector.tensor_tensor(scratch[:, :, :], values[:, :, :], spread(top[:, :], big), ALU.is_equal))
                link(nc.vector.tensor_tensor(scratch[:, :, :], scratch[:, :, :], rev, ALU.mult))
                link(nc.vector.tensor_reduce(index[:, :], scratch[:, :, :], AX.X, ALU.max))
                link(nc.vector.tensor_tensor(sel[:, :, :], spread(index[:, :], big), rev, ALU.is_equal))
            pick(logits, r1[0], one1, rt[1], r1[1])
            link(nc.vector.scalar_tensor_tensor(rt[3][:, :, :], one1[:, :, :], -3e38, logits[:, :, :], ALU.mult, ALU.add))
            pick(rt[3], r1[2], one2, rt[4], r1[3])
            link(nc.vector.tensor_tensor(rt[7][:, :, :], logits[:, :, :], spread(r1[0][:, :], big), ALU.subtract))
            link(nc.vector.tensor_tensor(r1[5][:, :], r1[2][:, :], r1[0][:, :], ALU.subtract))
            assert steps[0] == ROUTE_EXP
            link(nc.vector.tensor_tensor(rt[9][:, :, :], one1[:, :, :], one2[:, :, :], ALU.add))
            assert steps[0] == ROUTE_PICKS
            dve.wait_ge(route_exp, 2)
            link(nc.vector.tensor_reduce(r1[4][:, :], rt[8][:, :, :], AX.X, ALU.add))
            link(nc.vector.scalar_tensor_tensor(r1[7][:, :], r1[4][:, :], 1e-20, r1[6][:, :], ALU.mult, ALU.add))
            link(nc.vector.tensor_scalar(r1[8][:, :], r1[7][:, :], 1.0, None, ALU.add))
            link(nc.vector.reciprocal(r1[9][:, :], r1[8][:, :]))
            link(nc.vector.tensor_copy(meta[:, 0, :, 1], r1[9][:, :]))
            link(nc.vector.tensor_tensor(meta[:, 1, :, 1], r1[9][:, :], r1[6][:, :], ALU.mult))
            for k in range(2):
                link(nc.vector.tensor_scalar(meta[:, k, :, 0].bitcast(I32), cst[:, C_TOK:C_TOK + NT], float(k * S), None, ALU.add))
            dve.wait_ge(counts_full, 1)
            link(nc.vector.tensor_copy(rt[5][:, :, :], bank[5][:, NT * E:2 * NT * E].rearrange("p (t e) -> p t e", e=E)))
            src, other = rt[5], [rt[10], rt[11]]
            for n in range(5):
                dst, s = other[n % 2], 1 << n
                link(nc.vector.tensor_tensor(dst[:, s:NT, :], src[:, s:NT, :], src[:, 0:NT - s, :], ALU.add))
                link(nc.vector.tensor_copy(dst[:, 0:s, :], src[:, 0:s, :]))
                src = dst
            incl = src
            link(nc.vector.tensor_tensor(rt[1][:, :, :], incl[:, :, :], rt[5][:, :, :], ALU.subtract))
            link(nc.vector.tensor_tensor(rt[3][:, :, :], bank[5][:, 0:NT * E].rearrange("p (t e) -> p t e", e=E), rt[1][:, :, :], ALU.add))
            link(nc.vector.tensor_scalar(r8i[0][:, :], incl[:, NT - 1, :], float(BT - 1), None, ALU.add))
            link(nc.vector.tensor_scalar(r8i[1][:, :], r8i[0][:, :], BT.bit_length() - 1, None, ALU.logical_shift_right))
            link(nc.vector.tensor_scalar(r8[0][:, :], r8i[1][:, :], float(BT), None, ALU.mult))
            src8 = r8[0]
            for n in range(3):
                dst, s = r8[1 + n], 1 << n
                link(nc.vector.tensor_tensor(dst[:, s:E], src8[:, s:E], src8[:, 0:E - s], ALU.add))
                link(nc.vector.tensor_copy(dst[:, 0:s], src8[:, 0:s]))
                src8 = dst
            link(nc.vector.tensor_tensor(r8[4][:, :], src8[:, :], r8[0][:, :], ALU.subtract))
            link(nc.vector.tensor_tensor(rt[4][:, :, :], rt[3][:, :, :], across(r8[4][:, :], big), ALU.add))
            for k, sel in enumerate((one1, one2)):
                link(nc.vector.tensor_tensor(rt[1][:, :, :], rt[4][:, :, :], sel[:, :, :], ALU.mult))
                link(nc.vector.tensor_reduce(r1[k][:, :], rt[1][:, :, :], AX.X, ALU.add))
                link(nc.vector.tensor_copy(slot[:, k, :], r1[k][:, :]))
            wide = [P, NB, E]
            link(nc.vector.tensor_tensor(rb[:, :, :], spread(cst[:, C_BLK:C_BLK + NB], wide), across(src8[:, :], wide), ALU.is_ge))
            link(nc.vector.tensor_reduce(rbs[:, :], rb[:, :, :], AX.X, ALU.add))
            link(nc.vector.tensor_scalar(rbs[0:1, :], rbs[0:1, :], float(E - 1), None, ALU.min))
            link(nc.vector.tensor_copy(new[0:1, :], cst[0:1, C_ONE:C_ONE + NB]))
            link(nc.vector.tensor_tensor(new[0:1, 2:NB], rbs[0:1, 2:NB], rbs[0:1, 0:NB - 2], ALU.not_equal))
            link(nc.vector.tensor_copy(blk_e[0:1, NB:2 * NB], new[0:1, :]))
            nc.vector.tensor_copy(blk_e[0:1, 0:NB], rbs[0:1, :]).then_inc(slots_ready, 1)

            def full(name, g, last=False):
                b, n = m_use(name, g, last)
                dve.wait_ge(m_full[b], n + 1)
                if name.startswith(HI):
                    dve.wait_ge(m_hi, hi_use(name, g, last) + 1)
                return m_bank[b], m_free[b]

            def window_lo(g):
                for n in range(3):
                    w = BT if n < 2 else P
                    bk, free = full(f"XT{n}", g)
                    cs = slice(n * BT, n * BT + w)
                    nc.vector.tensor_tensor(xw_l[:, :, cs], bk[:, :].rearrange("p (k c) -> p k c", k=KC)[:, :, 0:w], xw_h[:, :, cs].bitcast(F32), ALU.subtract).then_inc(free, 1)

            def q_lo(g):
                for c in range(KC):
                    bk, free = full(f"Q{c}", g)
                    nc.vector.scalar_tensor_tensor(q_l[:, c, :], bk[:, :], col[:, c:c + 1], q_h[:, c, :].bitcast(F32), ALU.add, ALU.subtract).then_inc(free, 1)

            def k_lo(g):
                for n in range(4):
                    c, half = n // 2, n % 2
                    bk, free = full(f"K{n}", g)
                    cs = slice(half * WN // 2, (half + 1) * WN // 2)
                    nc.vector.scalar_tensor_tensor(k_l[:, c, cs], bk[:, 0:WN // 2], col[:, 2 + c:3 + c], k_h[:, c, cs].bitcast(F32), ALU.add, ALU.subtract).then_inc(free, 1)

            def v_copy(g):
                for j in range(WT):
                    bk, free = full(f"V{j}", g)
                    nc.vector.tensor_tensor(v[:, j, :], bk[:, 0:D], bv_b, ALU.add).then_inc(free, 1)

            def maxima(g, j, mask):
                for r in range(4):
                    dve.wait_ge(s_full[r], g * GT + (j + 1))
                    settle(dve)
                    for c in range(KC):
                        h = r + 4 * c
                        nc.vector.tensor_tensor_reduce(out=sm[:, j % 2, h, :], in0=s_bank[r][:, c * 2 * P:(c + 1) * 2 * P], in1=mask, scale=1.0,
                                                             scalar=-3e38, op0=ALU.add, op1=ALU.max, accum_out=mx[:, j % 2, h:h + 1]).then_inc(s_free[r], 1)
                for r in range(4):
                    dve.wait_ge(s_free[r], (g * GT + (j + 1)) * KC + KC)
                nc.vector.tensor_scalar(nmx[:, j % 2, :], mx[:, j % 2, :], -SCALE, None, ALU.mult).then_inc(neg_max, 1)

            def pt_copy(g, j):
                for u in (0, 2):
                    dve.wait_ge(t_full[0], (g * GT + j) * 2 + (u // 2 + 1))
                    nc.vector.tensor_copy(pt[:, 0].rearrange("p a n -> p (a n)"), t_bank[0][:, :]).then_inc(t_free[0], 1)

            def normalise(g, j, last):
                dve.wait_ge(probs_ready, (g * GT + (j + 1)) * H)
                nc.vector.reciprocal(rsum[:, :], sums[:, j % 2, :]).then_inc(rsum_ready, 1)
                bk, free = full(f"O{j}", g, last)
                dve.wait_ge(rsum_ready, g * GT + (j + 1))
                nc.vector.tensor_tensor(on[:, j % 2, :].rearrange("p (h d) -> p h d", d=DH), bk[:, 0:D].rearrange("p (h d) -> p h d", d=DH),
                                        spread(rsum[:, :], [P, H, DH]), ALU.mult).then_inc(free, 1)

            def ot_lo(g, j, last):
                bk, free = full(f"OT{j}", g, last)
                nc.vector.tensor_tensor(ot_l[:, :, :].rearrange("p k n -> p (k n)"), bk[:, 0:D], ot_h[:, :, :].rearrange("p k n -> p (k n)").bitcast(F32), ALU.subtract).then_inc(free, 1)

            def add_attention(g, j, last):
                bk, free = full(f"A{j}", g, last)
                n = g * GT + (j + 1)
                b, k = m_use(f"A{j}", g, last)
                nc.vector.tensor_tensor(t1[:, :], bk[:, 0:D], one(xn[:, ds(g * GT + j, 1), :]), ALU.add).then_inc(free, 1)
                dve.wait_ge(free, k + 1)
                nc.vector.tensor_tensor(u1[:, j, :], t1[:, :], bo_b, ALU.add).then_inc(pre_ready, 1)
                dve.wait_ge(pre_ready, n)
                nc.vector.bn_stats(st2[:, j, :], u1[:, j, :]).then_inc(ln6, 1)
                dve.wait_ge(ln6, n)
                settle(dve)
                nc.vector.bn_aggr(mv2[:, j, :], st2[:, j, :]).then_inc(ln_stats, 1)

            def layernorm(g):
                dve.wait_ge(ln_stats, g * GT + GT)
                dve.wait_ge(ln_sd, g + 1)
                nc.vector.reciprocal(rs2[:, :], sd2[:, :]).then_inc(ln_rstd, 1)
                dve.wait_ge(ln_rstd, g + 1)
                for j in range(GT):
                    nc.vector.scalar_tensor_tensor(x2[:, j, :], u1[:, j, :], mv2[:, j, 0:1], gam_b, ALU.subtract, ALU.mult).then_inc(scaled, 1)
                for j in range(GT):
                    dve.wait_ge(scaled, g * GT + (j + 1))
                    nc.vector.scalar_tensor_tensor(x2[:, j, :], x2[:, j, :], rs2[:, j:j + 1], bet_b, ALU.mult, ALU.add).then_inc(x2_ready, 1)

            def x2_lo(g, last):
                for n in range(2):
                    bk, free = full(f"X{n}", g, last)
                    cs = slice(n * BT, (n + 1) * BT)
                    nc.vector.tensor_tensor(x2t_l[:, :, cs], bk[:, :].rearrange("p (k c) -> p k c", k=KC), x2t_h[:, :, cs].bitcast(F32), ALU.subtract).then_inc(free, 1)

            def gelu_lo(g):
                for c in range(FC1):
                    dve.wait_ge(gelu_hi, g * FC1 + (c + 1))
                    nc.vector.tensor_tensor(h_l[:, c, :], h1[:, c % 2, :], h_h[:, c, :].bitcast(F32), ALU.subtract).then_inc(gelu_split, 1)

            def dense_sum(g, last):
                for k in range(2):
                    dve.wait_ge(scattered[k], g * (16 * GT) + 16 * GT)
                for n in range(2):
                    dve.wait_ge(x2_summed, g * GT + (2 * n + 2))
                    bk, free = full(f"Y{n}", g, last)
                    nc.vector.tensor_tensor(xn[:, ds(g * GT + 2 * n, 2), :], bk[:, :].rearrange("p (t d) -> p t d", t=2), xres[:, 2 * n:2 * n + 2, :], ALU.add).then_inc(free, 1)

            for r in range(4):
                dve.sem_inc(s_free[r], KC)
            dve.sem_inc(t_free[0], 1)
            dve.wait_ge(xn_stored, 16 * NG)
            dve.wait_ge(wraw_split, len(DENSE))
            dve.wait_ge(slots_ready, 1)
            nc.vector.tensor_copy(mask0[:, :], begin).then_inc(mask_set, 1)
            window_lo(None)
            q_lo(None)
            k_lo(None)
            v_copy(None)

            def turn(g, last):
                dve.wait_ge(mask_set, g + 1)
                maxima(g, 0, mask0[:, :])
                maxima(g, 1, mid)
                pt_copy(g, 0)
                normalise(g, 0, last)
                maxima(g, 2, mid)
                if not last:
                    nc.vector.tensor_copy(mask0[:, :], mid).then_inc(mask_set, 1)
                pt_copy(g, 1)
                normalise(g, 1, last)
                ot_lo(g, 0, last)
                add_attention(g, 0, last)
                maxima(g, 3, end if last else mid)
                pt_copy(g, 2)
                normalise(g, 2, last)
                ot_lo(g, 1, last)
                add_attention(g, 1, last)
                pt_copy(g, 3)
                normalise(g, 3, last)
                ot_lo(g, 2, last)
                add_attention(g, 2, last)
                if not last:
                    window_lo(g)
                ot_lo(g, 3, last)
                add_attention(g, 3, last)
                if not last:
                    q_lo(g)
                layernorm(g)
                if not last:
                    k_lo(g)
                    v_copy(g)
                x2_lo(g, last)
                gelu_lo(g)
                dense_sum(g, last)
            with dve.Fori(0, NG - 1) as g:
                turn(g, False)
            turn(NG - 1, True)

            wait_dense_done(dve)
            for p in range(2):
                nc.vector.tensor_copy(ht[:, p, 0, FCH - 1, :], cst[:, C_HOT:C_HOT + 1].to_broadcast([P, BT])).then_inc(pad_high, 1)

            def gu_high(b, p, c):
                if c == 0:
                    dve.wait_ge(gu_loaded[p], through(b, p, 16))
                    if not isinstance(b, int) or b >= 2:
                        dve.wait_ge(gu_full, (b - 1) * FCH)
                nc.vector.tensor_copy(gu_s[:, p, 0, gu_cols(c)], raw_gu[:, p, gu_cols(c)]).then_inc(gu_hi, 1)

            def gu_low(b, p, c):
                if c < FCH - GA:
                    dve.wait_ge(gu_hi, b * (FCH - GA) + (c + 1))
                else:
                    dve.wait_ge(gu_hi_act, b * GA + (c + 1 - (FCH - GA)))
                nc.vector.tensor_tensor(gu_s[:, p, 1, gu_cols(c)], raw_gu[:, p, gu_cols(c)], gu_s[:, p, 0, gu_cols(c)].bitcast(F32), ALU.subtract).then_inc(gu_split, 1)

            def dw_low(b, p):
                dve.wait_ge(dw_hi, b * 2 + 1)
                cs = slice(0, DV * D)
                nc.vector.tensor_tensor(dw_s[:, p, 1, cs], raw_dw[:, p, cs], dw_s[:, p, 0, cs].bitcast(F32), ALU.subtract).then_inc(dw_split, DV)

            def up_times_gate(b, p, c):
                dve.wait_ge(gs_ready, b * FCH + (c + 1))
                n = before(b, c)
                if n is not None:
                    dve.wait_ge(h_split, n)
                if c < FCH - 1:
                    nc.vector.scalar_tensor_tensor(hf[:, ring(c), :], bank[ring(c)][:, BT:2 * BT], bias[:, p, FCH + c:FCH + c + 1], gs[:, ring(c), :],
                                                   ALU.add, ALU.mult).then_inc(z_ready, 1)
                else:
                    nc.vector.scalar_tensor_tensor(hf[0:FR, 3, :], bank[3][WIN:WIN + FR, 0:BT], bias[WIN:WIN + FR, p, FCH + c:FCH + c + 1], gs[WIN:WIN + FR, 3, :],
                                                   ALU.add, ALU.mult).then_inc(z_ready, 1)

            def rows_lo(b, p):
                dve.wait_ge(ct_hi, b + 1)
                nc.vector.tensor_tensor(xt_l[:, p], bank[4][:, :].rearrange("p (k c) -> p k c", k=KC), xt_h[:, p].bitcast(F32), ALU.subtract).then_inc(ct_split, 1)

            def weigh(b, p):
                dve.wait_ge(y_full, b + 1)
                dve.wait_ge(y_kept, b * 2 + 2)
                if not isinstance(b, int) or b >= 2:
                    dve.wait_ge(y_sent[p], (b - p) * 16)
                for t in range(2):
                    ins = nc.vector.tensor_scalar(ys[:, p, t, :], bank[5 + p][:, t * D:(t + 1) * D], wgt[:, p, t:t + 1], None, ALU.mult)
                ins.then_inc(y_ready, 1)

            def body(b, p):
                dve.wait_ge(bi_loaded[p], through(b, p, 16))
                more = not isinstance(b, int) or b < NB - 1
                for c in range(FCH):
                    if more and c < FCH - GA:
                        gu_high(b + 1, 1 - p, c)
                    up_times_gate(b, p, c)
                    if more and c < FCH - GA:
                        gu_low(b + 1, 1 - p, c)
                    if more and c == ROWS_AT:
                        rows_lo(b + 1, 1 - p)
                if more:
                    for c in range(FCH - GA, FCH):
                        gu_low(b + 1, 1 - p, c)
                dw_low(b, p)
                if not isinstance(b, int) or b >= 1:
                    weigh(b - 1, 1 - p)
            for c in range(FCH):
                if c < FCH - GA:
                    gu_high(0, 0, c)
                gu_low(0, 0, c)
            rows_lo(0, 0)
            blocks_of(dve, body)
            weigh(NB - 1, (NB - 1) % 2)

            def add_rows(g, p, n):
                dve.wait_ge(yg_loaded[p], n * 32 + 32)
                span = xn[:, ds(g * GT, GT), :]
                nc.vector.tensor_tensor(span, span, yg[:, p, 0], ALU.add).then_inc(sum_1, 1)
                dve.wait_ge(sum_1, g + 1)
                nc.vector.tensor_tensor(span, span, yg[:, p, 1], ALU.add).then_inc(sum_2, 1)
            with dve.Fori(0, NG // 2) as i:
                for p in range(2):
                    add_rows(i * 2 + p, p, i)

        @block.tensor
        def _(pe):
            def passes(dst, lhs, rhs, start, stop):
                nc.tensor.matmul(dst, lhs[0], rhs[0], start=start, stop=False)
                nc.tensor.matmul(dst, lhs[0], rhs[1], start=False, stop=False)
                return nc.tensor.matmul(dst, lhs[1], rhs[0], start=False, stop=stop)

            pe.sem_inc(gate_full, 2)
            pe.wait_ge(const_loaded, 16)
            pe.wait_ge(small_loaded, 16 * 9)
            with pe.Fori(0, NG // 2) as i:
                for par in range(2):
                    g = i * 2 + par
                    pe.wait_ge(xn_ready, g * GT + GT)
                    pe.wait_ge(xt_copied, i * 4 + 4)
                    for k in range(KC):
                        for t in range(GT):
                            ins = nc.tensor.transpose(bank[2 * par + k][:, t * P:(t + 1) * P], xg[:, par, t, k * P:(k + 1) * P], ident)
                    ins.then_inc(xt_full, 1)
                    pe.wait_ge(xt_copied, g * 2 + 6)
                    for t in range(GT):
                        for k in range(KC):
                            ins = nc.tensor.matmul(bank[4][:, ds(g * (GT * E) + t * E, E)], xt[:, par, k, t * P:(t + 1) * P], gate_s[:, k, :],
                                                   start=(k == 0), stop=(k == KC - 1))
                    ins.then_inc(gate_full, 1)
            pe.wait_ge(route, ROUTE_PICKS)
            picks = rt[9][:, :, :].rearrange("p t e -> p (t e)")
            nc.tensor.matmul(bank[5][:, 0:NT * E], cst[:, C_TRI:C_TRI + P], picks, start=True, stop=True)
            nc.tensor.matmul(bank[5][:, NT * E:2 * NT * E], cst[:, C_ONE:C_ONE + P], picks, start=True, stop=True).then_inc(counts_full, 1)

            def take(name, g, last=False, after=()):
                b, n = m_use(name, g, last)
                for other in after:
                    bo, no = m_use(other, g, last)
                    if bo != b:
                        pe.wait_ge(m_free[bo], no + 1)
                if not isinstance(n, int) or n > 0:
                    pe.wait_ge(m_free[b], n)
                return m_bank[b], m_full[b]

            def parts(w, k, cs):
                return [w[:, part, k, cs] for part in range(2)]

            def pair(h, l, *at):
                return [h[at], l[at]]

            def window(g, n_loaded):
                pe.wait_ge(win_loaded, n_loaded)
                for n in range(3):
                    bk, full = take(f"XT{n}", g)
                    for j in range(2 * n, min(2 * n + 2, WT)):
                        for k in range(KC):
                            ins = nc.tensor.transpose(bk[:, k * BT + (j % 2) * P:k * BT + (j % 2) * P + P], xwin[:, j, k * P:(k + 1) * P], ident)
                    ins.then_inc(full, 1)

            def project(g):
                every = slice(None)
                for c in range(KC):
                    bk, full = take(f"Q{c}", g, False, ("XT2",) if c == 0 else ("XT1",))
                    for k in range(KC):
                        ins = passes(bk[:, :], parts(wq_s, k, slice(c * P, (c + 1) * P)), pair(xw_h, xw_l, every, k, slice(WIN, WIN + GN)), k == 0, k == KC - 1)
                    ins.then_inc(full, 1)
                for n in range(4):
                    c, half = n // 2, n % 2
                    bk, full = take(f"K{n}", g)
                    for k in range(KC):
                        ins = passes(bk[:, 0:WN // 2], parts(wk_s, k, slice(c * P, (c + 1) * P)),
                                     pair(xw_h, xw_l, every, k, slice(half * WN // 2, (half + 1) * WN // 2)), k == 0, k == KC - 1)
                    ins.then_inc(full, 1)
                for j in range(WT):
                    bk, full = take(f"V{j}", g)
                    for k in range(KC):
                        ins = passes(bk[:, 0:D], pair(xw_h, xw_l, every, k, slice(j * P, (j + 1) * P)), parts(wv_s, k, every), k == 0, k == KC - 1)
                    ins.then_inc(full, 1)

            def scores(g, j):
                for r in range(4):
                    pe.wait_ge(s_free[r], (g * GT + j) * KC + KC)
                    rows = slice(r * DH, (r + 1) * DH)
                    for c in range(KC):
                        ins = passes(s_bank[r][:, c * 2 * P:(c + 1) * 2 * P], pair(q_h, q_l, rows, c, slice(j * P, (j + 1) * P)),
                                     pair(k_h, k_l, rows, c, slice(j * P, (j + 2) * P)), True, True)
                    ins.then_inc(s_full[r], 1)

            def attend(g, j, last):
                o, o_full = take(f"O{j}", g, last)

                def turn_probs(r):
                    pe.wait_ge(probs_ready, (g * GT + j) * H + (2 * r + 2))
                    pe.wait_ge(t_free[r % 2], (g * GT + j) * 2 + (r // 2 + 1))
                    for c in range(KC):
                        for kb in range(2):
                            ins = nc.tensor.transpose(t_bank[r % 2][:, (2 * c + kb) * P:(2 * c + kb + 1) * P], sm[:, j % 2, r + 4 * c, kb * P:(kb + 1) * P], ident)
                    ins.then_inc(t_full[r % 2], 1)

                def times_v(r):
                    pe.wait_ge(t_free[r % 2], (g * GT + j) * 2 + (r // 2 + 2))
                    for c in range(KC):
                        h = r + 4 * c
                        for kb in range(2):
                            ins = nc.tensor.matmul(o[:, h * DH:(h + 1) * DH], pt[:, r % 2, 2 * c + kb, :], v[:, j + kb, h * DH:(h + 1) * DH],
                                                   start=(kb == 0), stop=(kb == 1))
                    return ins
                turn_probs(0)
                turn_probs(1)
                times_v(0)
                turn_probs(2)
                times_v(1)
                turn_probs(3)
                times_v(2)
                times_v(3).then_inc(o_full, 1)

            def turn_o(g, j, last):
                bk, full = take(f"OT{j}", g, last, (f"O{j}",))
                for k in range(KC):
                    ins = nc.tensor.transpose(bk[:, k * P:(k + 1) * P], on[:, j % 2, k * P:(k + 1) * P], ident)
                ins.then_inc(full, 1)

            def out_project(g, j, last):
                bk, full = take(f"A{j}", g, last, (f"OT{j}",))
                every = slice(None)
                for k in range(KC):
                    ins = passes(bk[:, 0:D], pair(ot_h, ot_l, every, k, every), parts(wo_s, k, every), k == 0, k == KC - 1)
                ins.then_inc(full, 1)

            def turn_x2(g, last):
                for n in range(2):
                    bk, full = take(f"X{n}", g, last)
                    for j in range(2 * n, 2 * n + 2):
                        pe.wait_ge(x2_ready, g * GT + (j + 1))
                        for k in range(KC):
                            ins = nc.tensor.transpose(bk[:, k * BT + (j % 2) * P:k * BT + (j % 2) * P + P], x2[:, j, k * P:(k + 1) * P], ident)
                    ins.then_inc(full, 1)

            def feed_forward(g, last):
                every = slice(None)
                for c in range(FC1):
                    bk, full = take(f"F{c}", g, last, ("X0", "X1") if c == 0 else ())
                    for k in range(KC):
                        ins = passes(bk[:, :], parts(w1_s, k, slice(c * P, (c + 1) * P)), pair(x2t_h, x2t_l, every, k, every), k == 0, k == KC - 1)
                    ins.then_inc(full, 1)
                for n in range(2):
                    bk, full = take(f"Y{n}", g, last)
                    for j in range(2 * n, 2 * n + 2):
                        for c in range(FC1):
                            if n == 0 and j == 0:
                                pe.wait_ge(gelu_split, g * FC1 + (c + 1))
                            ins = passes(bk[:, (j % 2) * D:(j % 2 + 1) * D], pair(h_h, h_l, every, c, slice(j * P, (j + 1) * P)), parts(w2_s, c, every), c == 0, c == FC1 - 1)
                    ins.then_inc(full, 1)

            pe.wait_ge(slots_ready, 1)
            pe.wait_ge(wraw_split, len(DENSE))
            window(None, 16)
            project(None)
            for b in range(2):
                pe.wait_ge(m_free[b], len(LEAD) // 2)

            def turn(g, last):
                scores(g, 0)
                scores(g, 1)
                attend(g, 0, last)
                scores(g, 2)
                attend(g, 1, last)
                turn_o(g, 0, last)
                out_project(g, 0, last)
                scores(g, 3)
                attend(g, 2, last)
                turn_o(g, 1, last)
                out_project(g, 1, last)
                attend(g, 3, last)
                turn_o(g, 2, last)
                out_project(g, 2, last)
                if not last:
                    window(g, g * 16 + 32)
                turn_o(g, 3, last)
                out_project(g, 3, last)
                if not last:
                    project(g)
                turn_x2(g, last)
                feed_forward(g, last)
            with pe.Fori(0, NG - 1) as g:
                turn(g, False)
            turn(NG - 1, True)

            wait_dense_done(pe)

            def turn_rows(b, p):
                pe.wait_ge(xr_loaded[p], through(b, p, 16))
                pe.wait_ge(ct_split, b)
                for k in range(KC):
                    for t in range(2):
                        ins = nc.tensor.transpose(bank[4][:, k * BT + t * P:k * BT + (t + 1) * P], xr[:, p, t, k * P:(k + 1) * P], ident)
                ins.then_inc(ct_full, 1)

            def gate_up(b, p):
                pe.wait_ge(ct_split, b + 1)
                for c in range(FCH):
                    pe.wait_ge(gu_split, b * FCH + (c + 1))
                    n = before(b, c)
                    if n is not None:
                        pe.wait_ge(z_ready, n)
                    w = P if c < FCH - 1 else GRW
                    for part in range(2 if c < FCH - 1 else 1):
                        for k in range(KC):
                            o = c * GUC + (k * 2 * P + part * P if c < FCH - 1 else k * GRW)
                            ins = passes(bank[ring(c)][0:w, part * BT:(part + 1) * BT], [gu_s[:, p, i, o:o + w] for i in range(2)],
                                         [xt_h[:, p, k, :], xt_l[:, p, k, :]], k == 0, k == KC - 1)
                    ins.then_inc(gu_full, 1)
                    if c == ROWS_AT - 1 and (not isinstance(b, int) or b < NB - 1):
                        turn_rows(b + 1, 1 - p)

            def down(b, p):
                pe.wait_ge(dw_split, b * DV + DV)
                pe.wait_ge(dw_split_pool, b * (FCH - DV) + (FCH - DV))
                pe.wait_ge(h_split, b * FCH + FCH)
                if not isinstance(b, int) or b >= 2:
                    pe.wait_ge(y_ready, b - 1)
                for t in range(2):
                    for c in range(FCH):
                        ins = passes(bank[5 + p][:, t * D:(t + 1) * D], [ht[:, p, i, c, t * P:(t + 1) * P] for i in range(2)],
                                     [dw_s[:, p, i, c * D:(c + 1) * D] for i in range(2)], c == 0, c == FCH - 1)
                ins.then_inc(y_full, 1)

            def body(b, p):
                gate_up(b, p)
                if not isinstance(b, int) or b >= 1:
                    down(b - 1, 1 - p)
            turn_rows(0, 0)
            blocks_of(pe, body)
            down(NB - 1, (NB - 1) % 2)


def kernel(**inputs):
    import concourse.bacc as bacc
    from concourse.bass_utils import run_bass_kernel_spmd

    a = {n: np.ascontiguousarray(v) for n, v in inputs.items()}

    def attn(n):
        return a["L0_attn_" + n]
    rows = np.zeros((6, D), np.float32)
    for n, name in enumerate(("bv", "bo", "gamma", "beta", "b2")):
        rows[n] = attn(name)
    rows[5, 0:E] = a["L0_ffn_gate_b"]
    cols = np.concatenate([attn("bq").reshape(KC, P).T, attn("bk").reshape(KC, P).T, attn("b1").reshape(FC1, P).T], axis=1)
    gate = a["L0_ffn_gate_w"].T.reshape(KC, P, E).transpose(1, 0, 2)
    gate_t = a["L0_ffn_gp_w"].transpose(0, 2, 1).reshape(E, KC, P, F)
    up_t = a["L0_ffn_up_w"].transpose(0, 2, 1).reshape(E, KC, P, F)
    gu = np.zeros((E, P, GUW), np.float32)
    for c in range(FCH):
        for k in range(KC):
            if c < FCH - 1:
                o = c * GUC + k * 2 * P
                gu[:, :, o:o + P] = gate_t[:, k, :, c * P:(c + 1) * P]
                gu[:, :, o + P:o + 2 * P] = up_t[:, k, :, c * P:(c + 1) * P]
            else:
                o = c * GUC + k * GRW
                gu[:, :, o:o + FR] = gate_t[:, k, :, c * P:F]
                gu[:, :, o + WIN:o + WIN + FR] = up_t[:, k, :, c * P:F]
    down = np.zeros((E, FCH * P, D), np.float32)
    down[:, 0:F] = a["L0_ffn_down_w"].transpose(0, 2, 1)
    down[:, F] = a["L0_ffn_down_b"]
    down = down.reshape(E, FCH, P, D).transpose(0, 2, 1, 3).reshape(E, P, DWW)
    bi = np.zeros((E, P, BIW), np.float32)
    for n, (name, last) in enumerate((("gp_b", 0), ("up_b", WIN))):
        v = a["L0_ffn_" + name]
        bi[:, :, n * FCH:n * FCH + FCH - 1] = v[:, 0:(FCH - 1) * P].reshape(E, FCH - 1, P).transpose(0, 2, 1)
        bi[:, last:last + FR, n * FCH + FCH - 1] = v[:, (FCH - 1) * P:F]

    named = [("x", attn("x").reshape(S, D)), ("wq", attn("Wq")), ("wk", attn("Wk")), ("wv", attn("Wv")), ("wo", attn("Wo")), ("w1", attn("W1")), ("w2", attn("W2")),
             ("gate", gate), ("rows", rows), ("cols", cols), ("gu", gu), ("dw", down), ("bi", bi), ("const", constants())]
    nc = bacc.Bacc("TRN2", target_bir_lowering=False, num_devices=1)
    arrays, args = {}, []
    for name, v in named:
        v = np.ascontiguousarray(v)
        arrays[f"in_{name}_dram"] = v
        args.append(nc.dram_tensor(f"in_{name}_dram", v.shape, mybir.dt.from_np(v.dtype), kind="ExternalInput").ap())
    args.append(nc.dram_tensor("out_0_dram", (S, D), F32, kind="ExternalOutput").ap())
    program(nc, *args)
    r = run_bass_kernel_spmd(nc, [arrays], core_ids=[0])
    return r.results[0]["out_0_dram"].reshape(1, S, D)
```

```python
import concourse.bass as bass
from concourse import mybir
from collections import namedtuple
from contextlib import ExitStack
import numpy as np

F32, F32R = mybir.dt.float32, mybir.dt.float32r
I32, U32, BF16 = mybir.dt.int32, mybir.dt.uint32, mybir.dt.bfloat16
ALU, ACT, AX = mybir.AluOpType, mybir.ActivationFunctionType, mybir.AxisListType
ds = bass.ds

P = 128
S, D, H, DH, WIN = 4096, 256, 8, 32, 64
KC = D // P
F1 = 4 * D
FC1 = F1 // P
E, F = 8, 816
NT = S // P
GT = 4
GN = GT * P
NG = S // GN
WT = GT + 1
WN = WT * P
PADROWS = S + 2 * WIN
BT = 2 * P
NB = (2 * S - E) // BT + E
SLOTS = NB * BT
REC = D + 2
FCH = 7
FR = F - (FCH - 1) * P
GRW = WIN + FR
GUC = 2 * KC * P
GUW = (FCH - 1) * GUC + KC * GRW
DWW = FCH * D
ROWS_AT = 4
DV = 4
GA = 3
BIW = 2 * FCH
EPS = 1e-5
SCALE = float(DH) ** -0.5
NEG = -1e30

C_ID, C_TRI, C_ONE, C_REV, C_TOK, C_BLK = 0, P, 2 * P, 3 * P, 3 * P + E, 3 * P + E + NT
C_EPS = C_BLK + NB
C_HOT = C_EPS + 1
C_W = C_HOT + 1
C_MID, C_LAST, C_FIRST = C_W, C_W + 2 * P, C_W + 4 * P
C_ALL = C_W + 6 * P


def constants():
    c = np.zeros((P, C_ALL), np.float32)
    q, k = np.arange(P)[:, None], np.arange(2 * P)[None, :]
    band = (k >= q) & (k <= q + 2 * WIN)
    c[:, C_ID:C_ID + P] = np.eye(P)
    c[:, C_MID:C_MID + 2 * P] = np.where(band, 0, NEG)
    c[:, C_LAST:C_LAST + 2 * P] = np.where(band & (k < P + WIN), 0, NEG)
    c[:, C_FIRST:C_FIRST + 2 * P] = np.where(band & (k >= WIN), 0, NEG)
    c[:, C_TRI:C_TRI + P] = np.arange(P)[:, None] < np.arange(P)[None, :]
    c[:, C_ONE:C_ONE + P] = 1
    c[:, C_REV:C_REV + E] = E - np.arange(E)
    c[:, C_TOK:C_TOK + NT] = np.arange(P)[:, None] + P * np.arange(NT)[None, :]
    c[:, C_BLK:C_BLK + NB] = BT * np.arange(NB)[None, :]
    c[:, C_EPS] = EPS
    c[FR, C_HOT] = 1
    return c


V = [f"V{j}" for j in range(WT)]
LEAD = ["XT0", "XT1", "XT2", "Q0", "Q1", "K0", "K1", "K2", "K3"] + V
TURN = (["Y0", "XT0", "OT0", "A0", "Y1", "XT1", "OT1", "A1", "Y2", "XT2", "OT2", "Q0", "A2", "Q1", "K0", "K1", "K2", "Y3", "OT3", "K3", "A3"]
        + V + ["X0", "X1"] + [f"F{c}" for c in range(FC1)])
FIRST = [u for u in TURN if u[0] != "Y"]
LAST = [u for u in TURN if u not in LEAD]
TAIL = [f"Y{j}" for j in range(GT)]
SEGMENTS = dict(lead=LEAD, first=FIRST, mid=TURN, last=LAST, tail=TAIL)
HI = ("XT", "OT", "Q", "K", "X")
assert all(len(uses) % 2 == 0 for uses in SEGMENTS.values())

Turn = namedtuple("Turn", "seg g f")
LEADING, OPENING, CLOSING, TRAILING = Turn("lead", 0, 0), Turn("first", 0, 0), Turn("last", NG - 1, NG - 2), Turn("tail", NG, NG - 1)


def uses_before(turn, count):
    lead, opening, middle = count(LEAD), count(FIRST), count(TURN)
    if turn.seg == "lead":
        return 0
    if turn.seg == "first":
        return lead
    if turn.seg == "tail":
        return lead + opening + (NG - 2) * middle + count(LAST)
    return turn.f * middle + lead + opening


def m_use(name, turn):
    n = SEGMENTS[turn.seg].index(name)
    return n % 2, uses_before(turn, lambda uses: len(uses) // 2) + n // 2


def hi_use(name, turn):
    def rounded(uses):
        return sum(u.startswith(HI) for u in uses)
    uses = SEGMENTS[turn.seg]
    return uses_before(turn, rounded) + rounded(uses[:uses.index(name)])


SB = 3
PAIRS = 4


def s_use(turn, j, r):
    n = (j - 1) * PAIRS + r
    if turn.seg == "lead":
        return r % SB, r // SB
    b = n % SB
    return b, turn.g * len(range(b, GT * PAIRS, SB)) + len(range(b, PAIRS, SB)) + n // SB


ROUTE_EXP, ROUTE_PICKS = 14, 15


def program(nc, x, wq, wk, wv, wo, w1, w2, gate, rows, cols, gu_rec, dw_rec, bi_rec, const, out):
    xn_dram = nc.dram_tensor("xn_dram", (PADROWS, D), F32, kind="Internal").ap()
    xs_dram = nc.dram_tensor("xs_dram", (SLOTS, REC), F32, kind="Internal").ap()
    y_dram = nc.dram_tensor("y_dram", (2 * S, D), F32, kind="Internal").ap()

    with ExitStack() as ctx:
        def sems(names):
            return [ctx.enter_context(nc.semaphore(n)) for n in names.split()]

        def phase():
            stack = ExitStack()

            def tile(name, shape, dtype=F32):
                return stack.enter_context(nc.sbuf_tensor(name, [P, *shape] if isinstance(shape, list) else shape, dtype))
            return stack, tile

        bank = [ctx.enter_context(nc.psum_tensor(f"bank{i}", [P, 512], F32)) for i in range(8)]
        s_bank, o_bank, t_bank, m_bank = bank[0:SB], bank[SB], bank[4:6], bank[6:8]

        whole, tile = phase()
        ctx.enter_context(whole)
        cst = tile("cst", [C_W])
        ident, eps = cst[:, C_ID:C_ID + P], cst[:, C_EPS:C_EPS + 1]
        xn = tile("xn", [NT, D])
        blk_e = tile("blk_e", (1, 2 * NB), I32)

        dense, tile = phase()
        wq_s, wk_s, wv_s, wo_s = (tile(n, [2, KC, D], F32R) for n in ("wq_s", "wk_s", "wv_s", "wo_s"))
        w1_s = tile("w1_s", [2, KC, F1], F32R)
        w2_s = tile("w2_s", [2, FC1, D], F32R)
        masks = tile("masks", [3, 2 * P])
        mid, end, begin = (masks[:, n, :] for n in range(3))
        rowb = tile("rowb", [5, D])
        bv_b, bo_b, gam_b, bet_b, b2_b = (rowb[:, n, :] for n in range(5))
        gb_b = tile("gb_b", [E])
        col = tile("col", [4 + FC1])
        slot = tile("slot", [2, NT], U32)
        meta = tile("meta", [2, NT, 2])
        stage = tile("stage", [2, REC])
        sidx = tile("sidx", [2], U32)
        first, tile = phase()
        gate_s = tile("gate_s", [KC, E])
        zrec = tile("zrec", [REC])
        wraw = tile("wraw", [2, KC * F1])
        xg = tile("xg", [2, GT, D])
        xt = tile("xt", [2, KC, GN])
        st6 = tile("st6", [2, GT, 6])
        mv = tile("mv", [2, GT, 2])
        sd = tile("sd", [2, GT])
        rstd = tile("rstd", [2, GT])
        rt = [tile(f"rt{n}", [NT, E]) for n in range(12)]
        r1 = [tile(f"r1_{n}", [NT]) for n in range(10)]
        r8 = [tile(f"r8_{n}", [E]) for n in range(6)]
        r8i = [tile(f"r8i_{n}", [E], I32) for n in range(2)]
        rb = tile("rb", [NB, E])
        rbs, new = tile("rbs", [NB]), tile("new", [NB])
        first.close()
        second, tile = phase()
        xwin = tile("xwin", [WT, D])
        xres = tile("xres", [GT, D])
        xw_h, xw_l = (tile(n, [KC, WN], F32R) for n in ("xw_h", "xw_l"))
        q_h, q_l = (tile(n, [KC, GN], F32R) for n in ("q_h", "q_l"))
        k_h, k_l = (tile(n, [KC, WN], F32R) for n in ("k_h", "k_l"))
        v = tile("v", [WT, H, DH + 1])
        pt = tile("pt", [2, 4, P])
        mx, nmx = (tile(n, [2, H]) for n in ("mx", "nmx"))
        rsum = tile("rsum", [H])
        on = tile("on", [D])
        ot_h, ot_l = (tile(n, [KC, P], F32R) for n in ("ot_h", "ot_l"))
        x2 = tile("x2", [GT, D])
        st2, mv2, sd2, rs2 = tile("st2", [GT, 6]), tile("mv2", [GT, 2]), tile("sd2", [GT]), tile("rs2", [GT])
        x2t_h, x2t_l = (tile(n, [KC, GN], F32R) for n in ("x2t_h", "x2t_l"))
        h1 = tile("h1", [2, GN])
        h_h, h_l = (tile(n, [FC1, GN], F32R) for n in ("h_h", "h_l"))
        sm = tile("sm", [2, H, 2 * P])
        second.close()
        dense.close()
        third, tile = phase()
        raw_gu = tile("raw_gu", [2, GUW])
        raw_dw = tile("raw_dw", [2, DWW])
        bias = tile("bias", [2, BIW])
        gu_s = tile("gu_s", [2, 2, GUW], F32R)
        dw_s = tile("dw_s", [2, 2, DWW], F32R)
        ht = tile("ht", [2, 2, FCH, BT], F32R)
        xr = tile("xr", [2, 2, REC])
        xt_h, xt_l = (tile(n, [2, KC, BT], F32R) for n in ("xt_h", "xt_l"))
        gs, hf = (tile(n, [4, BT]) for n in ("gs", "hf"))
        ys = tile("ys", [2, 2, D])
        dest = tile("dest", [4], U32)
        wgt = tile("wgt", [2, 2])
        third.close()
        fourth, tile = phase()
        yg = tile("yg", [2, 2, GT, D])
        fourth.close()

        const_loaded, small_loaded, zrec_ready, xs_filled, pads_filled = sems("const_loaded small_loaded zrec_ready xs_filled pads_filled")
        wraw_loaded = sems("wraw_loaded_0 wraw_loaded_1")
        wraw_hi, wraw_split = sems("wraw_hi wraw_split")
        xg_loaded = sems("xg_loaded_0 xg_loaded_1")
        stats6, stats_ready, sd_ready, rstd_ready, xn_ready, xn_kept, xn_stored = sems("stats6 stats_ready sd_ready rstd_ready xn_ready xn_kept xn_stored")
        xt_full, xt_copied, gate_full = sems("xt_full xt_copied gate_full")
        route, route_exp, counts_full, slots_ready = sems("route route_exp counts_full slots_ready")
        staged, = sems("staged")
        scattered = sems("scattered_0 scattered_1")
        win_loaded, xres_loaded = sems("win_loaded xres_loaded")
        m_full, m_free = sems("m_full_0 m_full_1"), sems("m_free_0 m_free_1")
        m_hi, = sems("m_hi")
        s_full, s_free = sems("s_full_0 s_full_1 s_full_2"), sems("s_free_0 s_free_1 s_free_2")
        o_full, o_free = sems("o_full o_free")
        t_full, t_free = sems("t_full_0 t_full_1"), sems("t_free_0 t_free_1")
        neg_max, probs_ready, rsum_ready, ones_set = sems("neg_max probs_ready rsum_ready ones_set")
        res_ready, pre_ready, ln6, ln_stats, ln_sd, ln_rstd, scaled, x2_ready, x2_half, x2_summed = sems(
            "res_ready pre_ready ln6 ln_stats ln_sd ln_rstd scaled x2_ready x2_half x2_summed")
        gelu_hi, gelu_split = sems("gelu_hi gelu_split")
        gu_loaded, dw_loaded, bi_loaded, xr_loaded = (sems(f"{n}_0 {n}_1") for n in ("gu_loaded", "dw_loaded", "bi_loaded", "xr_loaded"))
        gu_hi, gu_hi_act, gu_split, dw_hi, dw_split, dw_split_pool = sems("gu_hi gu_hi_act gu_split dw_hi dw_split dw_split_pool")
        ct_full, ct_hi, ct_split = sems("ct_full ct_hi ct_split")
        gu_full, gs_ready, z_ready, hf_ready, hhi_ready, h_split, pad_low, pad_high = sems("gu_full gs_ready z_ready hf_ready hhi_ready h_split pad_low pad_high")
        y_full, y_ready, y_kept = sems("y_full y_ready y_kept")
        y_sent = sems("y_sent_0 y_sent_1")
        yg_loaded = sems("yg_loaded_0 yg_loaded_1")
        sum_1, sum_2, out_stored = sems("sum_1 sum_2 out_stored")

        x_g = x.rearrange("(g t p) d -> g p t d", t=GT, p=P)
        out_g = out.rearrange("(g t p) d -> g p t d", t=GT, p=P)

        DENSE = [(wq, wq_s, KC, D), (wk, wk_s, KC, D), (wv, wv_s, KC, D), (wo, wo_s, KC, D), (w1, w1_s, KC, F1), (w2, w2_s, FC1, D)]

        passed = dict(zip((mybir.EngineType.SP, mybir.EngineType.Pool, mybir.EngineType.DVE), sems("passed_sp passed_pool passed_dve")))

        def one(ap):
            return ap.rearrange("p o d -> p (o d)")

        def spread(ap, shape):
            return ap.rearrange("p (n o) -> p n o", o=1).to_broadcast(shape)

        def across(ap, shape):
            return ap.rearrange("p (o n) -> p o n", o=1).to_broadcast(shape)

        def wait_dense_done(eng):
            b, n = m_use("Y3", TRAILING)
            eng.wait_ge(m_free[b], n + 1)
            for k in range(2):
                eng.wait_ge(scattered[k], 16 * NT)

        def ring(c):
            return c % 3 if c < FCH - 1 else 3

        def before(b, c):
            n = FCH * b + (c - 2 if 3 <= c < FCH - 1 else c - 3 if c < 3 else 0)
            return None if isinstance(b, int) and n <= 0 else n

        def settle(eng):
            eng.sem_inc(passed[eng.engine])

        def through(b, p, n):
            return (b - p) * (n // 2) + n

        def blocks_of(eng, body):
            body(0, 0)
            body(1, 1)
            with eng.Fori(0, (NB - 3) // 2) as i:
                body(i * 2 + 2, 0)
                body(i * 2 + 3, 1)
            body(NB - 1, (NB - 1) % 2)

        def gu_cols(c):
            return slice(c * GUC, (c + 1) * GUC if c < FCH - 1 else GUW)

        def turns_of(eng, turn):
            turn(OPENING)
            with eng.Fori(0, NG - 2) as f:
                turn(Turn("mid", f + 1, f))
            turn(CLOSING)

        block = ctx.enter_context(nc.Block())

        @block.sync
        def _(sp):
            sp.dma_start(xg[:, 0], x_g[0]).then_inc(xg_loaded[0], 16)
            sp.dma_start(cst[:, :], const[:, 0:C_W]).then_inc(const_loaded, 16)
            sp.dma_start(xg[:, 1], x_g[1]).then_inc(xg_loaded[1], 16)
            sp.dma_start(gate_s[:, :, :], gate).then_inc(small_loaded, 16)
            sp.dma_start(gb_b[:, :], rows[5:6, 0:E].to_broadcast([P, E])).then_inc(small_loaded, 16)
            sp.dma_start(col[:, :], cols).then_inc(small_loaded, 16)
            sp.dma_start(masks[:, :, :].rearrange("p n c -> p (n c)"), const[:, C_W:C_ALL]).then_inc(small_loaded, 16)
            for n in range(5):
                sp.dma_start(rowb[:, n, :], rows[n:n + 1, :].to_broadcast([P, D])).then_inc(small_loaded, 16)

            def store_xn(g, par):
                sp.wait_ge(xn_ready, g * GT + GT)
                settle(sp)
                sp.dma_start(xn_dram[ds(g * GN + WIN, GN), :].rearrange("(t p) d -> p t d", p=P), xg[:, par]).then_inc(xn_stored, 16)
            with sp.Fori(0, NG // 2 - 1) as i:
                for par in range(2):
                    g = i * 2 + par
                    store_xn(g, par)
                    sp.wait_ge(xn_stored, g * 16 + 16)
                    settle(sp)
                    sp.wait_ge(xn_kept, g + 1)
                    settle(sp)
                    sp.wait_ge(xt_full, g + 1)
                    settle(sp)
                    sp.dma_start(xg[:, par], x_g[ds(g + 2, 1)].rearrange("o p t d -> p (o t) d")).then_inc(xg_loaded[par], 16)
            for g in (NG - 2, NG - 1):
                store_xn(g, g % 2)
            sp.wait_ge(zrec_ready, 2)
            sp.dma_start(xn_dram[0:WIN, :], zrec[0:WIN, 0:D]).then_inc(pads_filled, 16)
            sp.dma_start(xn_dram[WIN + S:PADROWS, :], zrec[0:WIN, 0:D]).then_inc(pads_filled, 16)
            sp.dma_start(xs_dram.rearrange("(n p) c -> p n c", p=P), across(zrec[:, :], [P, SLOTS // P, REC])).then_inc(xs_filled, 16)

            sp.wait_ge(pads_filled, 32)
            sp.wait_ge(xn_stored, 16 * NG)
            sp.wait_ge(slots_ready, 1)
            sp.wait_ge(wraw_split, len(DENSE))

            def load_group(g):
                sp.dma_start(xwin[:, :, :], xn_dram[ds(g * GN, WN), :].rearrange("(t p) d -> p t d", p=P)).then_inc(win_loaded, 16)

            def load_residual(g):
                sp.dma_start(xres[:, :, :], x_g[ds(g, 1)].rearrange("o p t d -> p (o t) d")).then_inc(xres_loaded, 16)
            load_group(0)
            load_residual(0)
            b, n = m_use("XT2", LEADING)
            sp.wait_ge(m_full[b], n + 1)
            settle(sp)
            load_group(1)

            def turn(at):
                if at.seg != "last":
                    b, n = m_use("XT2", at)
                    sp.wait_ge(m_full[b], n + 1)
                    settle(sp)
                if at.seg == "first":
                    load_group(2)
                    return
                b, n = m_use("Y3", at)
                sp.wait_ge(m_free[b], n + 1)
                settle(sp)
                load_residual(at.g)
            turn(OPENING)
            with sp.Fori(0, NG - 3) as f:
                turn(Turn("mid", f + 1, f))
                load_group(f + 3)
            turn(Turn("mid", NG - 2, NG - 3))
            turn(CLOSING)

            wait_dense_done(sp)
            sp.wait_ge(xs_filled, 16)

            def load_record(dst, records, b, loaded):
                e = sp.value_load(blk_e[0:1, ds(b, 1)], min_val=0, max_val=E - 1)
                new = sp.value_load(blk_e[0:1, ds(b + NB, 1)], min_val=0, max_val=1)
                sp.dma_start(dst, records[ds(e, 1)].rearrange("o p w -> p (o w)"), cond=new).then_inc(loaded, 16)

            def load_gu(b, p, wait=True):
                if wait:
                    sp.wait_ge(gu_split, (b - 1) * FCH)
                settle(sp)
                load_record(raw_gu[:, p], gu_rec, b, gu_loaded[p])

            def load_rows_of(b, p, wait=True):
                if wait:
                    sp.wait_ge(ct_full, b - 1)
                    settle(sp)
                    sp.wait_ge(y_kept, (b - 1) * 2)
                    settle(sp)
                sp.dma_start(xr[:, p], xs_dram[ds(b * BT, BT), :].rearrange("(t p) c -> p t c", p=P)).then_inc(xr_loaded[p], 16)

            def load_dw(b, p, wait=True):
                if wait:
                    sp.wait_ge(dw_split, (b - 1) * DV)
                    settle(sp)
                    sp.wait_ge(dw_split_pool, (b - 1) * (FCH - DV))
                settle(sp)
                load_record(raw_dw[:, p], dw_rec, b, dw_loaded[p])

            def load_bias(b, p, wait=True):
                if wait:
                    sp.wait_ge(z_ready, (b - 1) * FCH)
                settle(sp)
                load_record(bias[:, p], bi_rec, b, bi_loaded[p])
            load_gu(0, 0, False)
            load_rows_of(0, 0, False)
            load_bias(0, 0, False)
            load_gu(1, 1, False)
            load_rows_of(1, 1, False)
            load_bias(1, 1, False)
            load_dw(0, 0, False)
            load_gu(2, 0)
            load_dw(1, 1, False)
            load_rows_of(2, 0)
            load_bias(2, 0)
            with sp.Fori(0, (NB - 3) // 2) as i:
                for b, p in ((i * 2 + 3, 1), (i * 2 + 4, 0)):
                    load_gu(b, p)
                    load_dw(b - 1, 1 - p)
                    load_rows_of(b, p)
                    load_bias(b, p)
            load_dw(NB - 1, (NB - 1) % 2)

            sp.wait_ge(y_sent[0], 32 * ((NB + 1) // 2))
            sp.wait_ge(y_sent[1], 32 * (NB // 2))

            def load_rows(g, p):
                for k in range(2):
                    sp.dma_start(yg[:, p, k], y_dram[ds(g * GN + k * S, GN), :].rearrange("(t p) d -> p t d", p=P)).then_inc(yg_loaded[p], 16)

            def store_out(g):
                sp.wait_ge(sum_2, g + 1)
                settle(sp)
                sp.dma_start(out_g[ds(g, 1)].rearrange("o p t d -> p (o t) d"), xn[:, ds(g * GT, GT), :]).then_inc(out_stored, 16)
            load_rows(0, 0)
            load_rows(1, 1)
            with sp.Fori(0, NG // 2 - 1) as i:
                for p in range(2):
                    store_out(i * 2 + p)
                    load_rows(i * 2 + (p + 2), p)
            store_out(NG - 2)
            store_out(NG - 1)
            sp.wait_ge(out_stored, 16 * NG)

        @block.gpsimd
        def _(pool):
            def load_dense(n):
                src, _, chunks, width = DENSE[n]
                if n >= 2:
                    pool.wait_ge(wraw_split, n - 1)
                pool.dma_start(wraw[:, n % 2, 0:chunks * width].rearrange("p (c n) -> p c n", c=chunks),
                               src.rearrange("(c p) n -> p c n", p=P)).then_inc(wraw_loaded[n % 2], 16)
            load_dense(0)
            nc.gpsimd.memset(zrec[:, :], 0.0).then_inc(zrec_ready, 1)
            pool.wait_ge(zrec_ready, 1)
            nc.gpsimd.iota(zrec[:, D:D + 1].bitcast(I32), [[0, 1]], base=2 * S, channel_multiplier=1).then_inc(zrec_ready, 1)
            for n, (_, dst, chunks, width) in enumerate(DENSE):
                if n + 1 < len(DENSE):
                    load_dense(n + 1)
                pool.wait_ge(wraw_loaded[n % 2], 16 * (n // 2 + 1))
                w = wraw[:, n % 2, 0:chunks * width]
                hi, lo = (dst[:, part].rearrange("p c n -> p (c n)") for part in range(2))
                nc.gpsimd.tensor_copy(hi, w).then_inc(wraw_hi, 1)
                pool.wait_ge(wraw_hi, n + 1)
                nc.gpsimd.tensor_tensor(lo, w, hi.bitcast(F32), ALU.subtract).then_inc(wraw_split, 1)

            def scatter(g):
                for j in range(GT):
                    t = g * GT + j
                    for k in range(2):
                        nc.gpsimd.tensor_copy(stage[:, k, 0:D], one(xn[:, ds(t, 1), :])).then_inc(staged, 1)
                        nc.gpsimd.tensor_copy(stage[:, k, D:REC], one(meta[:, k, ds(t, 1), :])).then_inc(staged, 1)
                        nc.gpsimd.tensor_copy(sidx[:, k:k + 1], slot[:, k, ds(t, 1)]).then_inc(staged, 1)
                        pool.wait_ge(staged, t * 6 + (3 * k + 3))
                        settle(pool)
                        nc.gpsimd.indirect_dma_start(xs_dram, bass.IndirectOffsetOnAxis(sidx[:, k:k + 1], 0), stage[:, k, :], None).then_inc(scattered[k], 16)
                    for k in range(2):
                        pool.wait_ge(scattered[k], t * 16 + 16)
                    settle(pool)

            def residual(g):
                pool.wait_ge(xres_loaded, g * 16 + 16)
                for j in range(GT):
                    pool.wait_ge(x2_ready, g * GT + (j + 1))
                    nc.gpsimd.tensor_tensor(xres[:, j, :], xres[:, j, :], x2[:, j, :], ALU.add).then_inc(x2_half, 1)
                    pool.wait_ge(x2_half, g * GT + (j + 1))
                    nc.gpsimd.tensor_tensor(xres[:, j, :], xres[:, j, :], b2_b, ALU.add).then_inc(x2_summed, 1)
            pool.wait_ge(small_loaded, 16 * 9)
            pool.wait_ge(xs_filled, 16)
            pool.wait_ge(slots_ready, 1)
            pool.wait_ge(xn_kept, NG)
            with pool.Fori(0, NG) as g:
                scatter(g)
                residual(g)

            wait_dense_done(pool)
            for p in range(2):
                nc.gpsimd.memset(ht[:, p, 1, FCH - 1, :].bitcast(F32), 0.0).then_inc(pad_low, 1)
            pool.wait_ge(pad_low, 2)

            def keep_meta(b, p):
                pool.wait_ge(xr_loaded[p], through(b, p, 16))
                if not isinstance(b, int) or b >= 2:
                    pool.wait_ge(y_sent[p], (b - p) * 16)
                    pool.wait_ge(y_ready, b - 1)
                settle(pool)
                nc.gpsimd.tensor_copy(dest[:, 2 * p:2 * p + 2], xr[:, p, :, D].bitcast(U32)).then_inc(y_kept, 1)
                nc.gpsimd.tensor_copy(wgt[:, p, :], xr[:, p, :, D + 1]).then_inc(y_kept, 1)

            def dw_low(b, p, c):
                cs = slice(c * D, (c + 1) * D)
                if c == DV:
                    pool.wait_ge(dw_hi, b * 2 + 2)
                nc.gpsimd.tensor_tensor(dw_s[:, p, 1, cs], raw_dw[:, p, cs], dw_s[:, p, 0, cs].bitcast(F32), ALU.subtract).then_inc(dw_split_pool, 1)

            def h_low(b, p, c):
                m = P if c < FCH - 1 else FR
                pool.wait_ge(hhi_ready, b * FCH + (c + 1))
                nc.gpsimd.tensor_tensor(ht[0:m, p, 1, c, :], hf[0:m, ring(c), :], ht[0:m, p, 0, c, :].bitcast(F32), ALU.subtract).then_inc(h_split, 1)

            def send(b, p):
                pool.wait_ge(y_ready, b + 1)
                settle(pool)
                for t in range(2):
                    index = dest[:, 2 * p + t:2 * p + t + 1]
                    nc.gpsimd.indirect_dma_start(y_dram, bass.IndirectOffsetOnAxis(index, 0), ys[:, p, t, :], None,
                                                 bounds_check=2 * S - 1, oob_is_err=False).then_inc(y_sent[p], 16)

            def body(b, p):
                for c in range(FCH):
                    h_low(b, p, c)
                    if c == 2:
                        keep_meta(b, p)
                for c in range(DV, FCH):
                    dw_low(b, p, c)
                if not isinstance(b, int) or b >= 1:
                    send(b - 1, 1 - p)
            blocks_of(pool, body)
            send(NB - 1, (NB - 1) % 2)

        @block.scalar
        def _(act):
            def sqrt_group(g, par):
                act.wait_ge(stats_ready, g * GT + GT)
                nc.scalar.activation(sd[:, par], mv[:, par, :, 1], ACT.Sqrt, bias=eps).then_inc(sd_ready, 1)

            def copy_group(g, par, pair):
                act.wait_ge(xn_ready, g * GT + GT)
                nc.scalar.activation(xn[:, ds(g * GT, GT), :], xg[:, par], ACT.Copy).then_inc(xn_kept, 1)
                act.wait_ge(xt_full, g + 1)
                act.wait_ge(gate_full, pair * 2 + 2)
                for k in range(KC):
                    nc.scalar.activation(xt[:, par, k, :], bank[2 * par + k][:, :], ACT.Copy).then_inc(xt_copied, 1)
            act.sem_inc(xt_copied, 4)
            act.wait_ge(const_loaded, 16)
            with act.Fori(0, NG // 2) as i:
                for par in range(2):
                    sqrt_group(i * 2 + par, par)
                    copy_group(i * 2 + par, par, i)
            act.wait_ge(route, ROUTE_EXP)
            nc.scalar.activation(rt[8][:, :, :], rt[7][:, :, :], ACT.Exp).then_inc(route_exp, 1)
            nc.scalar.activation(r1[6][:, :], r1[5][:, :], ACT.Exp).then_inc(route_exp, 1)

            def full(name, at):
                b, n = m_use(name, at)
                act.wait_ge(m_full[b], n + 1)
                return m_bank[b]

            def window_hi(at, n):
                w = BT if n < 2 else P
                bk = full(f"XT{n}", at)
                nc.scalar.activation(xw_h[:, :, n * BT:n * BT + w], bk[:, :].rearrange("p (k c) -> p k c", k=KC)[:, :, 0:w], ACT.Copy).then_inc(m_hi, 1)

            def q_hi(at, c):
                bk = full(f"Q{c}", at)
                nc.scalar.activation(q_h[:, c, :], bk[:, :], ACT.Identity, bias=col[:, c:c + 1]).then_inc(m_hi, 1)

            def k_hi(at, n):
                c, half = n // 2, n % 2
                bk = full(f"K{n}", at)
                nc.scalar.activation(k_h[:, c, half * WN // 2:(half + 1) * WN // 2], bk[:, 0:WN // 2], ACT.Identity, bias=col[:, 2 + c:3 + c]).then_inc(m_hi, 1)

            def probs(g, j, pairs):
                if 0 in pairs:
                    act.wait_ge(neg_max, g * GT + (j + 1))
                for r in pairs:
                    for c in range(KC):
                        h = r + 4 * c
                        nc.scalar.activation(sm[:, j % 2, h, :], sm[:, j % 2, h, :], ACT.Exp, bias=nmx[:, j % 2, h:h + 1], scale=SCALE).then_inc(probs_ready, 1)

            def pt_copy(g, j, u):
                act.wait_ge(t_full[1], (g * GT + j) * 2 + (u // 2 + 1))
                nc.scalar.activation(pt[:, 1].rearrange("p a n -> p (a n)"), t_bank[1][:, :], ACT.Copy).then_inc(t_free[1], 1)

            def ot_hi(at, j):
                bk = full(f"OT{j}", at)
                nc.scalar.activation(ot_h[:, :, :].rearrange("p k n -> p (k n)"), bk[:, 0:D], ACT.Copy).then_inc(m_hi, 1)

            def x2_hi(at):
                for n in range(2):
                    bk = full(f"X{n}", at)
                    nc.scalar.activation(x2t_h[:, :, n * BT:(n + 1) * BT], bk[:, :].rearrange("p (k c) -> p k c", k=KC), ACT.Copy).then_inc(m_hi, 1)

            def gelu(at):
                for c in range(FC1):
                    bk = full(f"F{c}", at)
                    b, n = m_use(f"F{c}", at)
                    if c >= 2:
                        act.wait_ge(gelu_split, at.g * FC1 + (c - 1))
                    nc.scalar.activation(h1[:, c % 2, :], bk[:, :], ACT.Gelu, bias=col[:, 4 + c:5 + c]).then_inc(m_free[b], 1)
                    act.wait_ge(m_free[b], n + 1)
                    nc.scalar.activation(h_h[:, c, :], h1[:, c % 2, :], ACT.Copy).then_inc(gelu_hi, 1)

            act.sem_inc(t_free[1], 1)
            act.wait_ge(small_loaded, 16 * 9)
            for n in range(3):
                window_hi(LEADING, n)
            for c in range(KC):
                q_hi(LEADING, c)
            for n in range(4):
                k_hi(LEADING, n)

            def turn(at):
                g, more = at.g, at.seg != "last"
                probs(g, 0, range(PAIRS))
                for j in range(GT - 1):
                    if j:
                        ot_hi(at, j - 1)
                    pt_copy(g, j, 1)
                    probs(g, j + 1, range(2))
                    pt_copy(g, j, 3)
                    probs(g, j + 1, range(2, PAIRS))
                    if more:
                        window_hi(at, j)
                ot_hi(at, GT - 2)
                pt_copy(g, GT - 1, 1)
                if more:
                    q_hi(at, 0)
                    q_hi(at, 1)
                pt_copy(g, GT - 1, 3)
                if more:
                    k_hi(at, 0)
                    k_hi(at, 1)
                    k_hi(at, 2)
                ot_hi(at, GT - 1)
                if more:
                    k_hi(at, 3)
                act.wait_ge(ln_stats, g * GT + GT)
                nc.scalar.activation(sd2[:, :], mv2[:, :, 1], ACT.Sqrt, bias=eps).then_inc(ln_sd, 1)
                x2_hi(at)
                gelu(at)
            turns_of(act, turn)

            wait_dense_done(act)

            def rows_hi(b, p):
                act.wait_ge(ct_full, b + 1)
                nc.scalar.activation(xt_h[:, p], bank[4][:, :].rearrange("p (k c) -> p k c", k=KC), ACT.Copy).then_inc(ct_hi, 1)

            def gate_bias(b, p, c):
                act.wait_ge(gu_full, b * FCH + (c + 1))
                if c < FCH - 1:
                    nc.scalar.activation(gs[:, ring(c), :], bank[ring(c)][:, 0:BT], ACT.Identity, bias=bias[:, p, c:c + 1]).then_inc(gs_ready, 1)
                else:
                    nc.scalar.activation(gs[WIN:WIN + FR, 3, :], bank[3][0:FR, 0:BT], ACT.Identity, bias=bias[0:FR, p, c:c + 1]).then_inc(gs_ready, 1)

            def silu(b, p, c):
                m = P if c < FCH - 1 else FR
                act.wait_ge(z_ready, b * FCH + (c + 1))
                nc.scalar.activation(hf[0:m, ring(c), :], hf[0:m, ring(c), :], ACT.Silu).then_inc(hf_ready, 1)
                if c == 0 and (not isinstance(b, int) or b >= 2):
                    act.wait_ge(y_full, b - 1)
                act.wait_ge(hf_ready, b * FCH + (c + 1))
                nc.scalar.activation(ht[0:m, p, 0, c, :], hf[0:m, ring(c), :], ACT.Copy).then_inc(hhi_ready, 1)

            def gu_high(b, p, c):
                if c == FCH - GA:
                    act.wait_ge(gu_loaded[p], through(b, p, 16))
                    if not isinstance(b, int) or b >= 2:
                        act.wait_ge(gu_full, (b - 1) * FCH)
                nc.scalar.activation(gu_s[:, p, 0, gu_cols(c)], raw_gu[:, p, gu_cols(c)], ACT.Copy).then_inc(gu_hi_act, 1)

            def dw_high(b, p):
                act.wait_ge(dw_loaded[p], through(b, p, 16))
                if not isinstance(b, int) or b >= 2:
                    act.wait_ge(y_full, b - 1)
                for cs in (slice(0, DV * D), slice(DV * D, DWW)):
                    nc.scalar.activation(dw_s[:, p, 0, cs], raw_dw[:, p, cs], ACT.Copy).then_inc(dw_hi, 1)

            def body(b, p):
                act.wait_ge(bi_loaded[p], through(b, p, 16))
                more = not isinstance(b, int) or b < NB - 1
                for c in range(FCH + 1):
                    if c < FCH:
                        gate_bias(b, p, c)
                    if c >= 1:
                        silu(b, p, c - 1)
                    if c == ROWS_AT and more:
                        rows_hi(b + 1, 1 - p)
                if more:
                    for c in range(FCH - GA, FCH):
                        gu_high(b + 1, 1 - p, c)
                dw_high(b, p)
            act.wait_ge(pad_high, 2)
            for c in range(FCH - GA, FCH):
                gu_high(0, 0, c)
            rows_hi(0, 0)
            blocks_of(act, body)

        @block.vector
        def _(dve):
            dve.wait_ge(const_loaded, 16)
            with dve.Fori(0, NG // 2) as i:
                for par in range(2):
                    g = i * 2 + par
                    dve.wait_ge(xg_loaded[par], i * 16 + 16)
                    for t in range(GT):
                        nc.vector.bn_stats(st6[:, par, t, :], xg[:, par, t, :]).then_inc(stats6, 1)
                    dve.wait_ge(stats6, g * GT + GT)
                    settle(dve)
                    for t in range(GT):
                        nc.vector.bn_aggr(mv[:, par, t, :], st6[:, par, t, :]).then_inc(stats_ready, 1)
                    dve.wait_ge(sd_ready, g + 1)
                    nc.vector.reciprocal(rstd[:, par], sd[:, par]).then_inc(rstd_ready, 1)
                    dve.wait_ge(rstd_ready, g + 1)
                    for t in range(GT):
                        nc.vector.tensor_scalar(xg[:, par, t, :], xg[:, par, t, :], mv[:, par, t, 0:1], rstd[:, par, t:t + 1],
                                                ALU.subtract, ALU.mult).then_inc(xn_ready, 1)

            steps = [0]

            def link(ins):
                steps[0] += 1
                ins.then_inc(route, 1)
                dve.wait_ge(route, steps[0])
            big, tok = [P, NT, E], [P, NT]
            rev = across(cst[:, C_REV:C_REV + E], big)
            logits, one1, one2 = rt[0], rt[2], rt[6]
            dve.wait_ge(gate_full, NG + 2)
            dve.wait_ge(small_loaded, 16 * 9)
            link(nc.vector.tensor_tensor(logits[:, :, :], bank[4][:, 0:NT * E].rearrange("p (t e) -> p t e", e=E), across(gb_b[:, :], big), ALU.add))

            def pick(values, top, sel, scratch, index):
                link(nc.vector.tensor_reduce(top[:, :], values[:, :, :], AX.X, ALU.max))
                link(nc.vector.tensor_tensor(scratch[:, :, :], values[:, :, :], spread(top[:, :], big), ALU.is_equal))
                link(nc.vector.tensor_tensor(scratch[:, :, :], scratch[:, :, :], rev, ALU.mult))
                link(nc.vector.tensor_reduce(index[:, :], scratch[:, :, :], AX.X, ALU.max))
                link(nc.vector.tensor_tensor(sel[:, :, :], spread(index[:, :], big), rev, ALU.is_equal))
            pick(logits, r1[0], one1, rt[1], r1[1])
            link(nc.vector.scalar_tensor_tensor(rt[3][:, :, :], one1[:, :, :], -3e38, logits[:, :, :], ALU.mult, ALU.add))
            pick(rt[3], r1[2], one2, rt[4], r1[3])
            link(nc.vector.tensor_tensor(rt[7][:, :, :], logits[:, :, :], spread(r1[0][:, :], big), ALU.subtract))
            link(nc.vector.tensor_tensor(r1[5][:, :], r1[2][:, :], r1[0][:, :], ALU.subtract))
            assert steps[0] == ROUTE_EXP
            link(nc.vector.tensor_tensor(rt[9][:, :, :], one1[:, :, :], one2[:, :, :], ALU.add))
            assert steps[0] == ROUTE_PICKS
            dve.wait_ge(route_exp, 2)
            link(nc.vector.tensor_reduce(r1[4][:, :], rt[8][:, :, :], AX.X, ALU.add))
            link(nc.vector.scalar_tensor_tensor(r1[7][:, :], r1[4][:, :], 1e-20, r1[6][:, :], ALU.mult, ALU.add))
            link(nc.vector.tensor_scalar(r1[8][:, :], r1[7][:, :], 1.0, None, ALU.add))
            link(nc.vector.reciprocal(r1[9][:, :], r1[8][:, :]))
            link(nc.vector.tensor_copy(meta[:, 0, :, 1], r1[9][:, :]))
            link(nc.vector.tensor_tensor(meta[:, 1, :, 1], r1[9][:, :], r1[6][:, :], ALU.mult))
            for k in range(2):
                link(nc.vector.tensor_scalar(meta[:, k, :, 0].bitcast(I32), cst[:, C_TOK:C_TOK + NT], float(k * S), None, ALU.add))
            dve.wait_ge(counts_full, 1)
            link(nc.vector.tensor_copy(rt[5][:, :, :], bank[5][:, NT * E:2 * NT * E].rearrange("p (t e) -> p t e", e=E)))
            src, other = rt[5], [rt[10], rt[11]]
            for n in range(5):
                dst, s = other[n % 2], 1 << n
                link(nc.vector.tensor_tensor(dst[:, s:NT, :], src[:, s:NT, :], src[:, 0:NT - s, :], ALU.add))
                link(nc.vector.tensor_copy(dst[:, 0:s, :], src[:, 0:s, :]))
                src = dst
            incl = src
            link(nc.vector.tensor_tensor(rt[1][:, :, :], incl[:, :, :], rt[5][:, :, :], ALU.subtract))
            link(nc.vector.tensor_tensor(rt[3][:, :, :], bank[5][:, 0:NT * E].rearrange("p (t e) -> p t e", e=E), rt[1][:, :, :], ALU.add))
            link(nc.vector.tensor_scalar(r8i[0][:, :], incl[:, NT - 1, :], float(BT - 1), None, ALU.add))
            link(nc.vector.tensor_scalar(r8i[1][:, :], r8i[0][:, :], BT.bit_length() - 1, None, ALU.logical_shift_right))
            link(nc.vector.tensor_scalar(r8[0][:, :], r8i[1][:, :], float(BT), None, ALU.mult))
            src8 = r8[0]
            for n in range(3):
                dst, s = r8[1 + n], 1 << n
                link(nc.vector.tensor_tensor(dst[:, s:E], src8[:, s:E], src8[:, 0:E - s], ALU.add))
                link(nc.vector.tensor_copy(dst[:, 0:s], src8[:, 0:s]))
                src8 = dst
            link(nc.vector.tensor_tensor(r8[4][:, :], src8[:, :], r8[0][:, :], ALU.subtract))
            link(nc.vector.tensor_tensor(rt[4][:, :, :], rt[3][:, :, :], across(r8[4][:, :], big), ALU.add))
            for k, sel in enumerate((one1, one2)):
                link(nc.vector.tensor_tensor(rt[1][:, :, :], rt[4][:, :, :], sel[:, :, :], ALU.mult))
                link(nc.vector.tensor_reduce(r1[k][:, :], rt[1][:, :, :], AX.X, ALU.add))
                link(nc.vector.tensor_copy(slot[:, k, :], r1[k][:, :]))
            wide = [P, NB, E]
            link(nc.vector.tensor_tensor(rb[:, :, :], spread(cst[:, C_BLK:C_BLK + NB], wide), across(src8[:, :], wide), ALU.is_ge))
            link(nc.vector.tensor_reduce(rbs[:, :], rb[:, :, :], AX.X, ALU.add))
            link(nc.vector.tensor_scalar(rbs[0:1, :], rbs[0:1, :], float(E - 1), None, ALU.min))
            link(nc.vector.tensor_copy(new[0:1, :], cst[0:1, C_ONE:C_ONE + NB]))
            link(nc.vector.tensor_tensor(new[0:1, 2:NB], rbs[0:1, 2:NB], rbs[0:1, 0:NB - 2], ALU.not_equal))
            link(nc.vector.tensor_copy(blk_e[0:1, NB:2 * NB], new[0:1, :]))
            nc.vector.tensor_copy(blk_e[0:1, 0:NB], rbs[0:1, :]).then_inc(slots_ready, 1)

            def full(name, at):
                b, n = m_use(name, at)
                dve.wait_ge(m_full[b], n + 1)
                if name.startswith(HI):
                    dve.wait_ge(m_hi, hi_use(name, at) + 1)
                return m_bank[b], m_free[b]

            def window_lo(at, n):
                w = BT if n < 2 else P
                bk, free = full(f"XT{n}", at)
                cs = slice(n * BT, n * BT + w)
                nc.vector.tensor_tensor(xw_l[:, :, cs], bk[:, :].rearrange("p (k c) -> p k c", k=KC)[:, :, 0:w], xw_h[:, :, cs].bitcast(F32), ALU.subtract).then_inc(free, 1)

            def q_lo(at, c):
                bk, free = full(f"Q{c}", at)
                nc.vector.scalar_tensor_tensor(q_l[:, c, :], bk[:, :], col[:, c:c + 1], q_h[:, c, :].bitcast(F32), ALU.add, ALU.subtract).then_inc(free, 1)

            def k_lo(at, n):
                c, half = n // 2, n % 2
                bk, free = full(f"K{n}", at)
                cs = slice(half * WN // 2, (half + 1) * WN // 2)
                nc.vector.scalar_tensor_tensor(k_l[:, c, cs], bk[:, 0:WN // 2], col[:, 2 + c:3 + c], k_h[:, c, cs].bitcast(F32), ALU.add, ALU.subtract).then_inc(free, 1)

            def v_copy(at, j):
                bk, free = full(f"V{j}", at)
                nc.vector.tensor_tensor(v[:, j, :, 0:DH], bk[:, 0:D].rearrange("p (h d) -> p h d", d=DH), bv_b.rearrange("p (h d) -> p h d", d=DH), ALU.add).then_inc(free, 1)

            def masked_max(at, j, r, mask):
                b, n = s_use(at, j, r)
                dve.wait_ge(s_full[b], n + 1)
                settle(dve)
                for c in range(KC):
                    h = r + 4 * c
                    nc.vector.tensor_tensor_reduce(out=sm[:, j % 2, h, :], in0=s_bank[b][:, c * 2 * P:(c + 1) * 2 * P], in1=mask, scale=1.0,
                                                   scalar=-3e38, op0=ALU.add, op1=ALU.max, accum_out=mx[:, j % 2, h:h + 1]).then_inc(s_free[b], 1)

            def negate_max(at, j):
                for r in range(1, PAIRS):
                    b, n = s_use(at, j, r)
                    dve.wait_ge(s_free[b], (n + 1) * KC + KC)
                nc.vector.tensor_scalar(nmx[:, j % 2, :], mx[:, j % 2, :], -SCALE, None, ALU.mult).then_inc(neg_max, 1)

            def pt_copy(g, j, u):
                dve.wait_ge(t_full[0], (g * GT + j) * 2 + (u // 2 + 1))
                nc.vector.tensor_copy(pt[:, 0].rearrange("p a n -> p (a n)"), t_bank[0][:, :]).then_inc(t_free[0], 1)

            def normalise(at, j):
                n = at.g * GT + j
                o = o_bank[:, 0:H * (DH + 1)].rearrange("p (h d) -> p h d", d=DH + 1)
                dve.wait_ge(o_full, n + 1)
                nc.vector.reciprocal(rsum[:, :], o[:, :, DH]).then_inc(rsum_ready, 1)
                dve.wait_ge(rsum_ready, n + 1)
                nc.vector.tensor_tensor(on[:, :].rearrange("p (h d) -> p h d", d=DH), o[:, :, 0:DH],
                                        spread(rsum[:, :], [P, H, DH]), ALU.mult).then_inc(o_free, 1)

            def ot_lo(at, j):
                bk, free = full(f"OT{j}", at)
                nc.vector.tensor_tensor(ot_l[:, :, :].rearrange("p k n -> p (k n)"), bk[:, 0:D], ot_h[:, :, :].rearrange("p k n -> p (k n)").bitcast(F32), ALU.subtract).then_inc(free, 1)

            def add_attention(at, j):
                bk, free = full(f"A{j}", at)
                n = at.g * GT + (j + 1)
                _, k = m_use(f"A{j}", at)
                nc.vector.tensor_tensor(x2[:, j, :], bk[:, 0:D], one(xn[:, ds(at.g * GT + j, 1), :]), ALU.add).then_inc(free, 1)
                dve.wait_ge(free, k + 1)
                nc.vector.tensor_tensor(x2[:, j, :], x2[:, j, :], bo_b, ALU.add).then_inc(pre_ready, 1)
                dve.wait_ge(pre_ready, n)
                nc.vector.bn_stats(st2[:, j, :], x2[:, j, :]).then_inc(ln6, 1)
                dve.wait_ge(ln6, n)
                settle(dve)
                nc.vector.bn_aggr(mv2[:, j, :], st2[:, j, :]).then_inc(ln_stats, 1)
                dve.wait_ge(ln_stats, n)
                nc.vector.scalar_tensor_tensor(x2[:, j, :], x2[:, j, :], mv2[:, j, 0:1], gam_b, ALU.subtract, ALU.mult).then_inc(scaled, 1)

            def layernorm_scale(g):
                dve.wait_ge(ln_sd, g + 1)
                nc.vector.reciprocal(rs2[:, :], sd2[:, :]).then_inc(ln_rstd, 1)
                dve.wait_ge(ln_rstd, g + 1)
                dve.wait_ge(scaled, g * GT + GT)

            def layernorm(g, j):
                nc.vector.scalar_tensor_tensor(x2[:, j, :], x2[:, j, :], rs2[:, j:j + 1], bet_b, ALU.mult, ALU.add).then_inc(x2_ready, 1)

            def x2_lo(at, n):
                bk, free = full(f"X{n}", at)
                cs = slice(n * BT, (n + 1) * BT)
                nc.vector.tensor_tensor(x2t_l[:, :, cs], bk[:, :].rearrange("p (k c) -> p k c", k=KC), x2t_h[:, :, cs].bitcast(F32), ALU.subtract).then_inc(free, 1)

            def gelu_lo(g):
                for c in range(FC1):
                    dve.wait_ge(gelu_hi, g * FC1 + (c + 1))
                    nc.vector.tensor_tensor(h_l[:, c, :], h1[:, c % 2, :], h_h[:, c, :].bitcast(F32), ALU.subtract).then_inc(gelu_split, 1)

            def dense_sum(at, j):
                if j == 0:
                    for k in range(2):
                        dve.wait_ge(scattered[k], at.f * (16 * GT) + 16 * GT)
                dve.wait_ge(x2_summed, at.f * GT + (j + 1))
                bk, free = full(f"Y{j}", at)
                nc.vector.tensor_tensor(one(xn[:, ds(at.f * GT + j, 1), :]), bk[:, 0:D], xres[:, j, :], ALU.add).then_inc(free, 1)

            for b in range(SB):
                dve.sem_inc(s_free[b], KC)
            dve.sem_inc(t_free[0], 1)
            dve.sem_inc(o_free, 1)
            dve.wait_ge(xn_stored, 16 * NG)
            dve.wait_ge(wraw_split, len(DENSE))
            dve.wait_ge(slots_ready, 1)
            dve.wait_ge(xs_filled, 16)
            nc.vector.tensor_copy(v[:, :, :, DH], cst[:, C_ONE:C_ONE + WT * H].rearrange("p (j h) -> p j h", h=H)).then_inc(ones_set, 1)
            for n in range(3):
                window_lo(LEADING, n)
            for c in range(KC):
                q_lo(LEADING, c)
            for n in range(4):
                k_lo(LEADING, n)

            def next_scores(at, mask, between):
                v_copy(at, 0)
                v_copy(at, 1)
                for r in range(PAIRS):
                    between(r)
                    masked_max(at, GT, r, mask)
                    if r + 2 < WT - 1:
                        v_copy(at, r + 2)
                negate_max(at, GT)
            next_scores(LEADING, begin, lambda r: None)
            v_copy(LEADING, WT - 1)

            def turn(at):
                g, more = at.g, at.seg != "last"
                for j in range(GT - 1):
                    mask = end if at.seg == "last" and j == GT - 2 else mid
                    masked_max(at, j + 1, 0, mask)
                    if j:
                        ot_lo(at, j - 1)
                    masked_max(at, j + 1, 1, mask)
                    masked_max(at, j + 1, 2, mask)
                    pt_copy(g, j, 0)
                    if j:
                        add_attention(at, j - 1)
                    masked_max(at, j + 1, 3, mask)
                    negate_max(at, j + 1)
                    pt_copy(g, j, 2)
                    if at.seg != "first":
                        dense_sum(at, j)
                    normalise(at, j)
                    if more:
                        window_lo(at, j)
                pt_copy(g, GT - 1, 0)
                ot_lo(at, GT - 2)
                if more:
                    q_lo(at, 0)
                add_attention(at, GT - 2)
                pt_copy(g, GT - 1, 2)
                if more:
                    q_lo(at, 1)
                    k_lo(at, 0)
                    k_lo(at, 1)
                normalise(at, GT - 1)
                if more:
                    k_lo(at, 2)
                if at.seg != "first":
                    dense_sum(at, GT - 1)
                ot_lo(at, GT - 1)
                if more:
                    k_lo(at, 3)
                add_attention(at, GT - 1)
                if more:
                    def between(r):
                        if r == 0:
                            layernorm_scale(g)
                        layernorm(g, r)
                    next_scores(at, mid, between)
                    v_copy(at, WT - 1)
                else:
                    layernorm_scale(g)
                    for j in range(GT):
                        layernorm(g, j)
                x2_lo(at, 0)
                x2_lo(at, 1)
                gelu_lo(g)
            turns_of(dve, turn)
            for j in range(GT):
                dense_sum(TRAILING, j)

            wait_dense_done(dve)
            for p in range(2):
                nc.vector.tensor_copy(ht[:, p, 0, FCH - 1, :], cst[:, C_HOT:C_HOT + 1].to_broadcast([P, BT])).then_inc(pad_high, 1)

            def gu_high(b, p, c):
                if c == 0:
                    dve.wait_ge(gu_loaded[p], through(b, p, 16))
                    if not isinstance(b, int) or b >= 2:
                        dve.wait_ge(gu_full, (b - 1) * FCH)
                nc.vector.tensor_copy(gu_s[:, p, 0, gu_cols(c)], raw_gu[:, p, gu_cols(c)]).then_inc(gu_hi, 1)

            def gu_low(b, p, c):
                if c < FCH - GA:
                    dve.wait_ge(gu_hi, b * (FCH - GA) + (c + 1))
                else:
                    dve.wait_ge(gu_hi_act, b * GA + (c + 1 - (FCH - GA)))
                nc.vector.tensor_tensor(gu_s[:, p, 1, gu_cols(c)], raw_gu[:, p, gu_cols(c)], gu_s[:, p, 0, gu_cols(c)].bitcast(F32), ALU.subtract).then_inc(gu_split, 1)

            def dw_low(b, p):
                dve.wait_ge(dw_hi, b * 2 + 1)
                cs = slice(0, DV * D)
                nc.vector.tensor_tensor(dw_s[:, p, 1, cs], raw_dw[:, p, cs], dw_s[:, p, 0, cs].bitcast(F32), ALU.subtract).then_inc(dw_split, DV)

            def up_times_gate(b, p, c):
                dve.wait_ge(gs_ready, b * FCH + (c + 1))
                n = before(b, c)
                if n is not None:
                    dve.wait_ge(h_split, n)
                if c < FCH - 1:
                    nc.vector.scalar_tensor_tensor(hf[:, ring(c), :], bank[ring(c)][:, BT:2 * BT], bias[:, p, FCH + c:FCH + c + 1], gs[:, ring(c), :],
                                                   ALU.add, ALU.mult).then_inc(z_ready, 1)
                else:
                    nc.vector.scalar_tensor_tensor(hf[0:FR, 3, :], bank[3][WIN:WIN + FR, 0:BT], bias[WIN:WIN + FR, p, FCH + c:FCH + c + 1], gs[WIN:WIN + FR, 3, :],
                                                   ALU.add, ALU.mult).then_inc(z_ready, 1)

            def rows_lo(b, p):
                dve.wait_ge(ct_hi, b + 1)
                nc.vector.tensor_tensor(xt_l[:, p], bank[4][:, :].rearrange("p (k c) -> p k c", k=KC), xt_h[:, p].bitcast(F32), ALU.subtract).then_inc(ct_split, 1)

            def weigh(b, p):
                dve.wait_ge(y_full, b + 1)
                dve.wait_ge(y_kept, b * 2 + 2)
                if not isinstance(b, int) or b >= 2:
                    dve.wait_ge(y_sent[p], (b - p) * 16)
                for t in range(2):
                    ins = nc.vector.tensor_scalar(ys[:, p, t, :], bank[5 + p][:, t * D:(t + 1) * D], wgt[:, p, t:t + 1], None, ALU.mult)
                ins.then_inc(y_ready, 1)

            def body(b, p):
                dve.wait_ge(bi_loaded[p], through(b, p, 16))
                more = not isinstance(b, int) or b < NB - 1
                for c in range(FCH):
                    if more and c < FCH - GA:
                        gu_high(b + 1, 1 - p, c)
                    up_times_gate(b, p, c)
                    if more and c < FCH - GA:
                        gu_low(b + 1, 1 - p, c)
                    if more and c == ROWS_AT:
                        rows_lo(b + 1, 1 - p)
                if more:
                    for c in range(FCH - GA, FCH):
                        gu_low(b + 1, 1 - p, c)
                dw_low(b, p)
                if not isinstance(b, int) or b >= 1:
                    weigh(b - 1, 1 - p)
            for c in range(FCH):
                if c < FCH - GA:
                    gu_high(0, 0, c)
                gu_low(0, 0, c)
            rows_lo(0, 0)
            blocks_of(dve, body)
            weigh(NB - 1, (NB - 1) % 2)

            def add_rows(g, p, n):
                dve.wait_ge(yg_loaded[p], n * 32 + 32)
                span = xn[:, ds(g * GT, GT), :]
                nc.vector.tensor_tensor(span, span, yg[:, p, 0], ALU.add).then_inc(sum_1, 1)
                dve.wait_ge(sum_1, g + 1)
                nc.vector.tensor_tensor(span, span, yg[:, p, 1], ALU.add).then_inc(sum_2, 1)
            with dve.Fori(0, NG // 2) as i:
                for p in range(2):
                    add_rows(i * 2 + p, p, i)

        @block.tensor
        def _(pe):
            def passes(dst, lhs, rhs, start, stop):
                nc.tensor.matmul(dst, lhs[0], rhs[0], start=start, stop=False)
                nc.tensor.matmul(dst, lhs[0], rhs[1], start=False, stop=False)
                return nc.tensor.matmul(dst, lhs[1], rhs[0], start=False, stop=stop)

            pe.sem_inc(gate_full, 2)
            pe.wait_ge(const_loaded, 16)
            pe.wait_ge(small_loaded, 16 * 9)
            with pe.Fori(0, NG // 2) as i:
                for par in range(2):
                    g = i * 2 + par
                    pe.wait_ge(xn_ready, g * GT + GT)
                    pe.wait_ge(xt_copied, i * 4 + 4)
                    for k in range(KC):
                        for t in range(GT):
                            ins = nc.tensor.transpose(bank[2 * par + k][:, t * P:(t + 1) * P], xg[:, par, t, k * P:(k + 1) * P], ident)
                    ins.then_inc(xt_full, 1)
                    pe.wait_ge(xt_copied, g * 2 + 6)
                    for t in range(GT):
                        for k in range(KC):
                            ins = nc.tensor.matmul(bank[4][:, ds(g * (GT * E) + t * E, E)], xt[:, par, k, t * P:(t + 1) * P], gate_s[:, k, :],
                                                   start=(k == 0), stop=(k == KC - 1))
                    ins.then_inc(gate_full, 1)
            pe.wait_ge(route, ROUTE_PICKS)
            picks = rt[9][:, :, :].rearrange("p t e -> p (t e)")
            nc.tensor.matmul(bank[5][:, 0:NT * E], cst[:, C_TRI:C_TRI + P], picks, start=True, stop=True)
            nc.tensor.matmul(bank[5][:, NT * E:2 * NT * E], cst[:, C_ONE:C_ONE + P], picks, start=True, stop=True).then_inc(counts_full, 1)

            def take(name, at, after=()):
                b, n = m_use(name, at)
                for other in after:
                    bo, no = m_use(other, at)
                    if bo != b:
                        pe.wait_ge(m_free[bo], no + 1)
                if not isinstance(n, int) or n > 0:
                    pe.wait_ge(m_free[b], n)
                return m_bank[b], m_full[b]

            every = slice(None)

            def parts(w, k, cs):
                return [w[:, part, k, cs] for part in range(2)]

            def pair(h, l, *index):
                return [h[index], l[index]]

            def window(at, n):
                bk, full = take(f"XT{n}", at)
                for j in range(2 * n, min(2 * n + 2, WT)):
                    for k in range(KC):
                        ins = nc.tensor.transpose(bk[:, k * BT + (j % 2) * P:k * BT + (j % 2) * P + P], xwin[:, j, k * P:(k + 1) * P], ident)
                ins.then_inc(full, 1)

            def query(at, c):
                bk, full = take(f"Q{c}", at, ("XT2",) if c == 0 else ("XT1",))
                for k in range(KC):
                    ins = passes(bk[:, :], parts(wq_s, k, slice(c * P, (c + 1) * P)), pair(xw_h, xw_l, every, k, slice(WIN, WIN + GN)), k == 0, k == KC - 1)
                ins.then_inc(full, 1)

            def keys(at, n):
                c, half = n // 2, n % 2
                bk, full = take(f"K{n}", at)
                for k in range(KC):
                    ins = passes(bk[:, 0:WN // 2], parts(wk_s, k, slice(c * P, (c + 1) * P)),
                                 pair(xw_h, xw_l, every, k, slice(half * WN // 2, (half + 1) * WN // 2)), k == 0, k == KC - 1)
                ins.then_inc(full, 1)

            def values(at, j):
                bk, full = take(f"V{j}", at)
                for k in range(KC):
                    ins = passes(bk[:, 0:D], pair(xw_h, xw_l, every, k, slice(j * P, (j + 1) * P)), parts(wv_s, k, every), k == 0, k == KC - 1)
                ins.then_inc(full, 1)

            def scores(at, j, r):
                b, n = s_use(at, j, r)
                pe.wait_ge(s_free[b], n * KC + KC)
                rows = slice(r * DH, (r + 1) * DH)
                for c in range(KC):
                    ins = passes(s_bank[b][:, c * 2 * P:(c + 1) * 2 * P], pair(q_h, q_l, rows, c, slice(j % GT * P, (j % GT + 1) * P)),
                                 pair(k_h, k_l, rows, c, slice(j % GT * P, (j % GT + 2) * P)), True, True)
                ins.then_inc(s_full[b], 1)

            def next_scores(at):
                values(at, 0)
                values(at, 1)
                for r in range(PAIRS):
                    scores(at, GT, r)
                    if r + 2 < WT - 1:
                        values(at, r + 2)

            def turn_probs(at, j, r):
                n = at.g * GT + j
                pe.wait_ge(probs_ready, n * H + (2 * r + 2))
                pe.wait_ge(t_free[r % 2], n * 2 + (r // 2 + 1))
                for c in range(KC):
                    for kb in range(2):
                        ins = nc.tensor.transpose(t_bank[r % 2][:, (2 * c + kb) * P:(2 * c + kb + 1) * P], sm[:, j % 2, r + 4 * c, kb * P:(kb + 1) * P], ident)
                ins.then_inc(t_full[r % 2], 1)

            def times_v(at, j, r):
                n = at.g * GT + j
                if r == 0:
                    pe.wait_ge(o_free, n + 1)
                pe.wait_ge(t_free[r % 2], n * 2 + (r // 2 + 2))
                for c in range(KC):
                    h = r + 4 * c
                    for kb in range(2):
                        ins = nc.tensor.matmul(o_bank[:, h * (DH + 1):(h + 1) * (DH + 1)], pt[:, r % 2, 2 * c + kb, :], v[:, j + kb, h, :],
                                               start=(kb == 0), stop=(kb == 1))
                if r == PAIRS - 1:
                    ins.then_inc(o_full, 1)

            def turn_o(at, j):
                bk, full = take(f"OT{j}", at)
                pe.wait_ge(o_free, at.g * GT + (j + 2))
                for k in range(KC):
                    ins = nc.tensor.transpose(bk[:, k * P:(k + 1) * P], on[:, k * P:(k + 1) * P], ident)
                ins.then_inc(full, 1)

            def out_project(at, j):
                bk, full = take(f"A{j}", at, (f"OT{j}",))
                for k in range(KC):
                    ins = passes(bk[:, 0:D], pair(ot_h, ot_l, every, k, every), parts(wo_s, k, every), k == 0, k == KC - 1)
                ins.then_inc(full, 1)

            def turn_x2(at, n):
                bk, full = take(f"X{n}", at)
                for j in range(2 * n, 2 * n + 2):
                    pe.wait_ge(x2_ready, at.g * GT + (j + 1))
                    for k in range(KC):
                        ins = nc.tensor.transpose(bk[:, k * BT + (j % 2) * P:k * BT + (j % 2) * P + P], x2[:, j, k * P:(k + 1) * P], ident)
                ins.then_inc(full, 1)

            def widen(at):
                bk, full = take("F0", at)
                for n in range(2):
                    b, k = m_use(f"X{n}", at)
                    pe.wait_ge(m_free[b], k + 1)
                    cs = slice(n * BT, (n + 1) * BT)
                    for k in range(KC):
                        ins = passes(bk[:, cs], parts(w1_s, k, slice(0, P)), pair(x2t_h, x2t_l, every, k, cs), k == 0, k == KC - 1)
                ins.then_inc(full, 1)
                for c in range(1, FC1):
                    bk, full = take(f"F{c}", at)
                    for k in range(KC):
                        ins = passes(bk[:, :], parts(w1_s, k, slice(c * P, (c + 1) * P)), pair(x2t_h, x2t_l, every, k, every), k == 0, k == KC - 1)
                    ins.then_inc(full, 1)

            def narrow(at, j, chunks):
                for c in chunks:
                    if c == 0:
                        bk, full = take(f"Y{j}", at)
                    else:
                        b, _ = m_use(f"Y{j}", at)
                        bk, full = m_bank[b], m_full[b]
                    if j == 0:
                        pe.wait_ge(gelu_split, at.f * FC1 + (c + 1))
                    ins = passes(bk[:, 0:D], pair(h_h, h_l, every, c, slice(j * P, (j + 1) * P)), parts(w2_s, c, every), c == 0, c == FC1 - 1)
                if c == FC1 - 1:
                    ins.then_inc(full, 1)

            pe.wait_ge(slots_ready, 1)
            pe.wait_ge(wraw_split, len(DENSE))
            pe.wait_ge(win_loaded, 16)
            for n in range(3):
                window(LEADING, n)
            query(LEADING, 0)
            query(LEADING, 1)
            for n in range(4):
                keys(LEADING, n)
            next_scores(LEADING)
            values(LEADING, WT - 1)
            for b in range(2):
                pe.wait_ge(m_free[b], len(LEAD) // 2)
            pe.wait_ge(ones_set, 1)

            def turn(at):
                g, more = at.g, at.seg != "last"

                def fill(j, *chunks):
                    if at.seg != "first":
                        narrow(at, j, chunks)
                for j in range(GT - 1):
                    scores(at, j + 1, 0)
                    if j:
                        turn_o(at, j - 1)
                    scores(at, j + 1, 1)
                    scores(at, j + 1, 2)
                    if j == 0:
                        fill(j, 0, 1, 2, 3)
                    turn_probs(at, j, 0)
                    if j:
                        out_project(at, j - 1)
                    turn_probs(at, j, 1)
                    scores(at, j + 1, 3)
                    if j:
                        fill(j, 0, 1)
                    times_v(at, j, 0)
                    turn_probs(at, j, 2)
                    fill(j, *((2, 3) if j else (4, 5)))
                    times_v(at, j, 1)
                    turn_probs(at, j, 3)
                    fill(j, *((4, 5) if j else (6,)))
                    times_v(at, j, 2)
                    fill(j, *((6, 7) if j else (7,)))
                    times_v(at, j, 3)
                    if more:
                        if j == 0:
                            pe.wait_ge(win_loaded, g * 16 + 32)
                        window(at, j)
                j = GT - 1
                turn_probs(at, j, 0)
                turn_o(at, j - 1)
                turn_probs(at, j, 1)
                if more:
                    query(at, 0)
                out_project(at, j - 1)
                times_v(at, j, 0)
                turn_probs(at, j, 2)
                if more:
                    query(at, 1)
                times_v(at, j, 1)
                turn_probs(at, j, 3)
                if more:
                    keys(at, 0)
                times_v(at, j, 2)
                if more:
                    keys(at, 1)
                times_v(at, j, 3)
                if more:
                    keys(at, 2)
                fill(j, *range(FC1))
                turn_o(at, j)
                if more:
                    keys(at, 3)
                out_project(at, j)
                if more:
                    next_scores(at)
                    values(at, WT - 1)
                turn_x2(at, 0)
                turn_x2(at, 1)
                widen(at)
            turns_of(pe, turn)
            for j in range(GT):
                narrow(TRAILING, j, range(FC1))

            wait_dense_done(pe)

            def turn_rows(b, p):
                pe.wait_ge(xr_loaded[p], through(b, p, 16))
                pe.wait_ge(ct_split, b)
                for k in range(KC):
                    for t in range(2):
                        ins = nc.tensor.transpose(bank[4][:, k * BT + t * P:k * BT + (t + 1) * P], xr[:, p, t, k * P:(k + 1) * P], ident)
                ins.then_inc(ct_full, 1)

            def gate_up(b, p):
                pe.wait_ge(ct_split, b + 1)
                for c in range(FCH):
                    pe.wait_ge(gu_split, b * FCH + (c + 1))
                    n = before(b, c)
                    if n is not None:
                        pe.wait_ge(z_ready, n)
                    w = P if c < FCH - 1 else GRW
                    for part in range(2 if c < FCH - 1 else 1):
                        for k in range(KC):
                            o = c * GUC + (k * 2 * P + part * P if c < FCH - 1 else k * GRW)
                            ins = passes(bank[ring(c)][0:w, part * BT:(part + 1) * BT], [gu_s[:, p, i, o:o + w] for i in range(2)],
                                         [xt_h[:, p, k, :], xt_l[:, p, k, :]], k == 0, k == KC - 1)
                    ins.then_inc(gu_full, 1)
                    if c == ROWS_AT - 1 and (not isinstance(b, int) or b < NB - 1):
                        turn_rows(b + 1, 1 - p)

            def down(b, p):
                pe.wait_ge(dw_split, b * DV + DV)
                pe.wait_ge(dw_split_pool, b * (FCH - DV) + (FCH - DV))
                pe.wait_ge(h_split, b * FCH + FCH)
                if not isinstance(b, int) or b >= 2:
                    pe.wait_ge(y_ready, b - 1)
                for t in range(2):
                    for c in range(FCH):
                        ins = passes(bank[5 + p][:, t * D:(t + 1) * D], [ht[:, p, i, c, t * P:(t + 1) * P] for i in range(2)],
                                     [dw_s[:, p, i, c * D:(c + 1) * D] for i in range(2)], c == 0, c == FCH - 1)
                ins.then_inc(y_full, 1)

            def body(b, p):
                gate_up(b, p)
                if not isinstance(b, int) or b >= 1:
                    down(b - 1, 1 - p)
            turn_rows(0, 0)
            blocks_of(pe, body)
            down(NB - 1, (NB - 1) % 2)


def kernel(**inputs):
    import concourse.bacc as bacc
    from concourse.bass_utils import run_bass_kernel_spmd

    a = {n: np.ascontiguousarray(v) for n, v in inputs.items()}

    def attn(n):
        return a["L0_attn_" + n]
    rows = np.zeros((6, D), np.float32)
    for n, name in enumerate(("bv", "bo", "gamma", "beta", "b2")):
        rows[n] = attn(name)
    rows[5, 0:E] = a["L0_ffn_gate_b"]
    cols = np.concatenate([attn("bq").reshape(KC, P).T, attn("bk").reshape(KC, P).T, attn("b1").reshape(FC1, P).T], axis=1)
    gate = a["L0_ffn_gate_w"].T.reshape(KC, P, E).transpose(1, 0, 2)
    gate_t = a["L0_ffn_gp_w"].transpose(0, 2, 1).reshape(E, KC, P, F)
    up_t = a["L0_ffn_up_w"].transpose(0, 2, 1).reshape(E, KC, P, F)
    gu = np.zeros((E, P, GUW), np.float32)
    for c in range(FCH):
        for k in range(KC):
            if c < FCH - 1:
                o = c * GUC + k * 2 * P
                gu[:, :, o:o + P] = gate_t[:, k, :, c * P:(c + 1) * P]
                gu[:, :, o + P:o + 2 * P] = up_t[:, k, :, c * P:(c + 1) * P]
            else:
                o = c * GUC + k * GRW
                gu[:, :, o:o + FR] = gate_t[:, k, :, c * P:F]
                gu[:, :, o + WIN:o + WIN + FR] = up_t[:, k, :, c * P:F]
    down = np.zeros((E, FCH * P, D), np.float32)
    down[:, 0:F] = a["L0_ffn_down_w"].transpose(0, 2, 1)
    down[:, F] = a["L0_ffn_down_b"]
    down = down.reshape(E, FCH, P, D).transpose(0, 2, 1, 3).reshape(E, P, DWW)
    bi = np.zeros((E, P, BIW), np.float32)
    for n, (name, last) in enumerate((("gp_b", 0), ("up_b", WIN))):
        v = a["L0_ffn_" + name]
        bi[:, :, n * FCH:n * FCH + FCH - 1] = v[:, 0:(FCH - 1) * P].reshape(E, FCH - 1, P).transpose(0, 2, 1)
        bi[:, last:last + FR, n * FCH + FCH - 1] = v[:, (FCH - 1) * P:F]

    named = [("x", attn("x").reshape(S, D)), ("wq", attn("Wq")), ("wk", attn("Wk")), ("wv", attn("Wv")), ("wo", attn("Wo")), ("w1", attn("W1")), ("w2", attn("W2")),
             ("gate", gate), ("rows", rows), ("cols", cols), ("gu", gu), ("dw", down), ("bi", bi), ("const", constants())]
    nc = bacc.Bacc("TRN2", target_bir_lowering=False, num_devices=1)
    arrays, args = {}, []
    for name, v in named:
        v = np.ascontiguousarray(v)
        arrays[f"in_{name}_dram"] = v
        args.append(nc.dram_tensor(f"in_{name}_dram", v.shape, mybir.dt.from_np(v.dtype), kind="ExternalInput").ap())
    args.append(nc.dram_tensor("out_0_dram", (S, D), F32, kind="ExternalOutput").ap())
    program(nc, *args)
    r = run_bass_kernel_spmd(nc, [arrays], core_ids=[0])
    return r.results[0]["out_0_dram"].reshape(1, S, D)
```

```python
import concourse.bass as bass
from concourse import mybir
from collections import namedtuple
from contextlib import ExitStack
import numpy as np

F32, F32R = mybir.dt.float32, mybir.dt.float32r
I32, U32 = mybir.dt.int32, mybir.dt.uint32
ALU, ACT, AX = mybir.AluOpType, mybir.ActivationFunctionType, mybir.AxisListType
ds = bass.ds

P = 128
S, D, H, DH, WIN = 4096, 256, 8, 32, 64
KC = D // P
F1 = 4 * D
FC1 = F1 // P
E, F = 8, 816
NT = S // P
GT = 4
YB = 4
XB = 4
FILLS = 6
GN = GT * P
NG = S // GN
WT = GT + 1
WN = WT * P
PADROWS = S + 2 * WIN
BT = 2 * P
NB = (2 * S - E) // BT + E
SLOTS = NB * BT
REC = D + 2
FCH = 7
FR = F - (FCH - 1) * P
GRW = WIN + FR
GUC = 2 * KC * P
GUW = (FCH - 1) * GUC + KC * GRW
DWW = FCH * D
ROWS_AT = 4
DV = 4
GA = 3
BIW = 2 * FCH
EPS = 1e-5
SCALE = float(DH) ** -0.5
NEG = -1e30

C_ID, C_TRI, C_ONE, C_REV, C_TOK, C_BLK = 0, P, 2 * P, 3 * P, 3 * P + E, 3 * P + E + NT
C_EPS = C_BLK + NB
C_HOT = C_EPS + 1
C_W = C_HOT + 1
C_MID, C_LAST, C_FIRST = C_W, C_W + 2 * P, C_W + 4 * P
C_ALL = C_W + 6 * P


def constants():
    c = np.zeros((P, C_ALL), np.float32)
    q, k = np.arange(P)[:, None], np.arange(2 * P)[None, :]
    band = (k >= q) & (k <= q + 2 * WIN)
    c[:, C_ID:C_ID + P] = np.eye(P)
    c[:, C_MID:C_MID + 2 * P] = np.where(band, 0, NEG)
    c[:, C_LAST:C_LAST + 2 * P] = np.where(band & (k < P + WIN), 0, NEG)
    c[:, C_FIRST:C_FIRST + 2 * P] = np.where(band & (k >= WIN), 0, NEG)
    c[:, C_TRI:C_TRI + P] = np.arange(P)[:, None] < np.arange(P)[None, :]
    c[:, C_ONE:C_ONE + P] = 1
    c[:, C_REV:C_REV + E] = E - np.arange(E)
    c[:, C_TOK:C_TOK + NT] = np.arange(P)[:, None] + P * np.arange(NT)[None, :]
    c[:, C_BLK:C_BLK + NB] = BT * np.arange(NB)[None, :]
    c[:, C_EPS] = EPS
    c[FR, C_HOT] = 1
    return c


V = [f"V{j}" for j in range(WT)]
LEAD = ["XT0", "XT1", "XT2", "Q0", "Q1", "K0", "K1", "K2", "K3"] + V
TURN = (["Y0", "XT0", "OT0", "A0", "Y1", "XT1", "OT1", "A1", "Y2", "XT2", "OT2", "Q0", "A2", "Q1", "K0", "K1", "K2", "Y3", "OT3", "K3", "A3"]
        + V + ["X0", "X1"] + [f"F{c}" for c in range(FC1)])
FIRST = [u for u in TURN if u[0] != "Y"]
FIRST[1:1] = ["C", "BO"]
LAST = [u for u in TURN if u not in LEAD]
TAIL = [f"Y{j}" for j in range(GT)]
SEGMENTS = dict(lead=LEAD, first=FIRST, mid=TURN, last=LAST, tail=TAIL)
HI = ("XT", "OT", "Q", "K", "X")
assert all(len(uses) % 2 == 0 for uses in SEGMENTS.values())

Turn = namedtuple("Turn", "seg g f")
LEADING, OPENING, CLOSING, TRAILING = Turn("lead", 0, 0), Turn("first", 0, 0), Turn("last", NG - 1, NG - 2), Turn("tail", NG, NG - 1)


def uses_before(turn, count):
    lead, opening, middle = count(LEAD), count(FIRST), count(TURN)
    if turn.seg == "lead":
        return 0
    if turn.seg == "first":
        return lead
    if turn.seg == "tail":
        return lead + opening + (NG - 2) * middle + count(LAST)
    return turn.f * middle + lead + opening


def m_use(name, turn):
    n = SEGMENTS[turn.seg].index(name)
    return n % 2, uses_before(turn, lambda uses: len(uses) // 2) + n // 2


def hi_use(name, turn):
    def rounded(uses):
        return sum(u.startswith(HI) for u in uses)
    uses = SEGMENTS[turn.seg]
    return uses_before(turn, rounded) + rounded(uses[:uses.index(name)])


SB = 3
PAIRS = 4


def s_use(turn, j, r):
    n = (j - 1) * PAIRS + r
    if turn.seg == "lead":
        return r % SB, r // SB
    b = n % SB
    return b, turn.g * len(range(b, GT * PAIRS, SB)) + len(range(b, PAIRS, SB)) + n // SB


ROUTE_EXP, ROUTE_PICKS = 14, 15
ROUTE_SLOTS = 23


def program(nc, x, wq, wk, wv, wo, w1, w2, gate, rows, cols, gu_rec, dw_rec, bi_rec, const, out):
    xn_dram = nc.dram_tensor("xn_dram", (PADROWS, D), F32, kind="Internal").ap()
    xs_dram = nc.dram_tensor("xs_dram", (SLOTS, REC), F32, kind="Internal").ap()
    y_dram = nc.dram_tensor("y_dram", (2 * S, D), F32, kind="Internal").ap()

    with ExitStack() as ctx:
        def sems(names):
            return [ctx.enter_context(nc.semaphore(n)) for n in names.split()]

        def phase():
            stack = ExitStack()

            def tile(name, shape, dtype=F32):
                return stack.enter_context(nc.sbuf_tensor(name, [P, *shape] if isinstance(shape, list) else shape, dtype))
            return stack, tile

        bank = [ctx.enter_context(nc.psum_tensor(f"bank{i}", [P, 512], F32)) for i in range(8)]
        s_bank, o_bank, t_bank, m_bank = bank[0:SB], bank[SB], bank[4:6], bank[6:8]

        whole, tile = phase()
        ctx.enter_context(whole)
        cst = tile("cst", [C_W])
        ident, eps = cst[:, C_ID:C_ID + P], cst[:, C_EPS:C_EPS + 1]
        xn = tile("xn", [NT, D])
        blk_e = tile("blk_e", (1, 2 * NB), I32)

        dense, tile = phase()
        wq_s, wk_s, wv_s = (tile(n, [2, KC, D], F32R) for n in ("wq_s", "wk_s", "wv_s"))
        xwin = tile("xwin", [WT, D])
        xw_h, xw_l = (tile(n, [KC, WN], F32R) for n in ("xw_h", "xw_l"))
        k_h, k_l = (tile(n, [KC, WN], F32R) for n in ("k_h", "k_l"))
        wo_s = tile("wo_s", [2, KC, D], F32R)
        w1_s = tile("w1_s", [2, KC, F1], F32R)
        w2_s = tile("w2_s", [2, FC1, D], F32R)
        masks = tile("masks", [3, 2 * P])
        mid, end, begin = (masks[:, n, :] for n in range(3))
        rowb = tile("rowb", [4, D])
        bo_b, gam_b, bet_b, b2_b = (rowb[:, n, :] for n in range(4))
        gb_b = tile("gb_b", [E])
        col = tile("col", [3 * KC + FC1])
        slot = tile("slot", [2, NT], U32)
        meta = tile("meta", [2, NT, 2])
        stage = tile("stage", [2, REC])
        sidx = tile("sidx", [2], U32)
        zrec = tile("zrec", [REC])
        q_h, q_l = (tile(n, [KC, GN], F32R) for n in ("q_h", "q_l"))
        v = tile("v", [WT, H, DH + 1])
        sm = tile("sm", [2, H, 2 * P])
        mx, nmx = (tile(n, [2, H]) for n in ("mx", "nmx"))
        first, tile = phase()
        gate_s = tile("gate_s", [KC, E])
        wraw = tile("wraw", [2, KC * F1])
        xg = tile("xg", [XB, GT, D])
        xt = tile("xt", [2, KC, GN])
        st6 = tile("st6", [2, GT, 6])
        mv = tile("mv", [2, GT, 2])
        sd = tile("sd", [2, GT])
        rstd = tile("rstd", [2, GT])
        rt = [tile(f"rt{n}", [NT, E]) for n in range(12)]
        r1 = [tile(f"r1_{n}", [NT]) for n in range(10)]
        r8 = [tile(f"r8_{n}", [E]) for n in range(6)]
        r8i = [tile(f"r8i_{n}", [E], I32) for n in range(2)]
        rb, fold = tile("rb", [NB, E]), tile("fold", [NT, E])
        rbs, new = tile("rbs", [NB]), tile("new", [NB])
        first.close()
        second, tile = phase()
        xres = tile("xres", [GT, D])
        pt = tile("pt", [2, 4, P])
        rsum = tile("rsum", [H])
        on = tile("on", [D])
        ot_h, ot_l = (tile(n, [KC, P], F32R) for n in ("ot_h", "ot_l"))
        x2 = tile("x2", [GT, D])
        st2, mv2, sd2, rs2 = tile("st2", [GT, 6]), tile("mv2", [GT, 2]), tile("sd2", [GT]), tile("rs2", [GT])
        x2t_h, x2t_l = (tile(n, [KC, GN], F32R) for n in ("x2t_h", "x2t_l"))
        h1 = tile("h1", [2, GN])
        h_h, h_l = (tile(n, [FC1, GN], F32R) for n in ("h_h", "h_l"))
        second.close()
        dense.close()
        third, tile = phase()
        raw_gu = tile("raw_gu", [2, GUW])
        xr = tile("xr", [2, 2, REC])
        raw_dw = tile("raw_dw", [2, DWW])
        bias = tile("bias", [2, BIW])
        assert 2 * GUW <= 3 * 2 * KC * D + WT * D + 2 * KC * WN
        gu_s = tile("gu_s", [2, 2, GUW], F32R)
        dw_s = tile("dw_s", [2, 2, DWW], F32R)
        ht = tile("ht", [2, 2, FCH, BT], F32R)
        xt_h, xt_l = (tile(n, [2, KC, BT], F32R) for n in ("xt_h", "xt_l"))
        gs, hf = (tile(n, [4, BT]) for n in ("gs", "hf"))
        ys = tile("ys", [2, 2, D])
        dest = tile("dest", [4], U32)
        wgt = tile("wgt", [2, 2])
        third.close()
        fourth, tile = phase()
        yg = tile("yg", [YB, 2, GT, D])
        fourth.close()

        const_loaded, small_loaded, zrec_ready, xs_filled, pads_filled = sems("const_loaded small_loaded zrec_ready xs_filled pads_filled")
        wraw_loaded = sems("wraw_loaded_0 wraw_loaded_1")
        wraw_hi, wraw_split = sems("wraw_hi wraw_split")
        xg_loaded = sems("xg_loaded_0 xg_loaded_1 xg_loaded_2 xg_loaded_3")
        xn_stored = sems("xn_stored_0 xn_stored_1")
        stats6, stats_ready, sd_ready, rstd_ready, xn_ready, xn_kept = sems("stats6 stats_ready sd_ready rstd_ready xn_ready xn_kept")
        xt_full, xt_copied, gate_full = sems("xt_full xt_copied gate_full")
        route, route_exp, slots_ready, counts_kept, starts_ready, slot_step = sems("route route_exp slots_ready counts_kept starts_ready slot_step")
        staged, = sems("staged")
        scattered = sems("scattered_0 scattered_1")
        win_loaded, xres_loaded = sems("win_loaded xres_loaded")
        m_full, m_free = sems("m_full_0 m_full_1"), sems("m_free_0 m_free_1")
        m_hi, = sems("m_hi")
        s_full, s_free = sems("s_full_0 s_full_1 s_full_2"), sems("s_free_0 s_free_1 s_free_2")
        o_full, o_free = sems("o_full o_free")
        t_full, t_free = sems("t_full_0 t_full_1"), sems("t_free_0 t_free_1")
        neg_max, probs_ready, rsum_ready, ones_set, bv_split = sems("neg_max probs_ready rsum_ready ones_set bv_split")
        pre_ready, ln6, ln_stats, ln_sd, ln_rstd, scaled, x2_ready, x2_half, x2_summed = sems(
            "pre_ready ln6 ln_stats ln_sd ln_rstd scaled x2_ready x2_half x2_summed")
        gelu_hi, gelu_split = sems("gelu_hi gelu_split")
        gu_loaded, dw_loaded, bi_loaded, xr_loaded = (sems(f"{n}_0 {n}_1") for n in ("gu_loaded", "dw_loaded", "bi_loaded", "xr_loaded"))
        gu_hi, gu_hi_act, gu_split, dw_hi, dw_split, dw_split_pool = sems("gu_hi gu_hi_act gu_split dw_hi dw_split dw_split_pool")
        ct_full, ct_hi, ct_split = sems("ct_full ct_hi ct_split")
        gu_full, gs_ready, z_ready, hf_ready, hhi_ready, h_split, pad_low, pad_high = sems("gu_full gs_ready z_ready hf_ready hhi_ready h_split pad_low pad_high")
        y_full, y_ready, y_kept = sems("y_full y_ready y_kept")
        y_sent = sems("y_sent_0 y_sent_1")
        yg_loaded = sems("yg_loaded_0 yg_loaded_1 yg_loaded_2 yg_loaded_3")
        sum_1, sum_2, out_stored = sems("sum_1 sum_2 out_stored")

        x_g = x.rearrange("(g t p) d -> g p t d", t=GT, p=P)
        out_g = out.rearrange("(g t p) d -> g p t d", t=GT, p=P)

        DENSE = [(wq, wq_s, KC, D), (wk, wk_s, KC, D), (wv, wv_s, KC, D), (wo, wo_s, KC, D), (w1, w1_s, KC, F1), (w2, w2_s, FC1, D)]

        passed = dict(zip((mybir.EngineType.SP, mybir.EngineType.Pool, mybir.EngineType.DVE), sems("passed_sp passed_pool passed_dve")))

        def one(ap):
            return ap.rearrange("p o d -> p (o d)")

        def spread(ap, shape):
            return ap.rearrange("p (n o) -> p n o", o=1).to_broadcast(shape)

        def across(ap, shape):
            return ap.rearrange("p (o n) -> p o n", o=1).to_broadcast(shape)

        def wait_first_done(eng):
            for stored in xn_stored:
                eng.wait_ge(stored, 16 * NG // 2)
            eng.wait_ge(xn_kept, NG)
            eng.wait_ge(gate_full, NG + 2)
            eng.wait_ge(wraw_split, len(DENSE))

        def wait_dense_done(eng):
            b, n = m_use("Y3", TRAILING)
            eng.wait_ge(m_free[b], n + 1)
            for k in range(2):
                eng.wait_ge(scattered[k], 16 * NT)

        def ring(c):
            return c % 3 if c < FCH - 1 else 3

        def before(b, c):
            n = FCH * b + (c - 2 if 3 <= c < FCH - 1 else c - 3 if c < 3 else 0)
            return None if isinstance(b, int) and n <= 0 else n

        def settle(eng):
            eng.sem_inc(passed[eng.engine])

        def through(b, p, n):
            return (b - p) * (n // 2) + n

        def blocks_of(eng, body):
            body(0, 0)
            body(1, 1)
            with eng.Fori(0, (NB - 3) // 2) as i:
                body(i * 2 + 2, 0)
                body(i * 2 + 3, 1)
            body(NB - 1, (NB - 1) % 2)

        def gu_cols(c):
            return slice(c * GUC, (c + 1) * GUC if c < FCH - 1 else GUW)

        def turns_of(eng, turn):
            turn(OPENING)
            with eng.Fori(0, NG - 2) as f:
                turn(Turn("mid", f + 1, f))
            turn(CLOSING)

        block = ctx.enter_context(nc.Block())

        @block.sync
        def _(sp):
            for g in range(XB):
                sp.dma_start(xg[:, g], x_g[g]).then_inc(xg_loaded[g], 16)
                if g == 0:
                    sp.dma_start(cst[:, :], const[:, 0:C_W]).then_inc(const_loaded, 16)
            sp.dma_start(gate_s[:, :, :], gate).then_inc(small_loaded, 16)
            sp.dma_start(gb_b[:, :], rows[4:5, 0:E].to_broadcast([P, E])).then_inc(small_loaded, 16)
            sp.dma_start(col[:, :], cols).then_inc(small_loaded, 16)
            sp.dma_start(masks[:, :, :].rearrange("p n c -> p (n c)"), const[:, C_W:C_ALL]).then_inc(small_loaded, 16)
            for n in range(4):
                sp.dma_start(rowb[:, n, :], rows[n:n + 1, :].to_broadcast([P, D])).then_inc(small_loaded, 16)
            sp.wait_ge(zrec_ready, 2)
            sp.dma_start(xn_dram[0:WIN, :], zrec[0:WIN, 0:D]).then_inc(pads_filled, 16)
            sp.dma_start(xn_dram[WIN + S:PADROWS, :], zrec[0:WIN, 0:D]).then_inc(pads_filled, 16)

            def store_xn(g):
                sp.wait_ge(xn_ready, g * GT + GT)
                sp.dma_start(xn_dram[g * GN + WIN:(g + 1) * GN + WIN, :].rearrange("(t p) d -> p t d", p=P), xg[:, g % XB]).then_inc(xn_stored[g % 2], 16)

            def load_again(g):
                sp.wait_ge(xn_stored[g % 2], 16 * (g // 2 + 1))
                sp.wait_ge(xn_kept, g + 1)
                sp.wait_ge(xt_full, g + 1)
                sp.dma_start(xg[:, g % XB], x_g[g + XB]).then_inc(xg_loaded[g % XB], 16)

            def fill(n):
                rows_at = n * (SLOTS // P // FILLS)
                sp.dma_start(xs_dram.rearrange("(n p) c -> p n c", p=P)[:, rows_at:rows_at + SLOTS // P // FILLS, :],
                             across(zrec[:, :], [P, SLOTS // P // FILLS, REC])).then_inc(xs_filled, 16)
            assert SLOTS // P % FILLS == 0

            def load_group(g):
                sp.dma_start(xwin[:, :, :], xn_dram[ds(g * GN, WN), :].rearrange("(t p) d -> p t d", p=P)).then_inc(win_loaded, 16)

            def load_residual(g):
                sp.dma_start(xres[:, :, :], x_g[ds(g, 1)].rearrange("o p t d -> p (o t) d")).then_inc(xres_loaded, 16)
            store_xn(0)
            for g in range(XB):
                store_xn(g + 1)
                load_again(g)
                if g == 1:
                    sp.wait_ge(pads_filled, 32)
                    load_group(0)
            for g in range(XB + 1, NG):
                for n in range(2):
                    fill(2 * (g - XB - 1) + n)
                store_xn(g)
            wait_first_done(sp)
            load_residual(0)
            b, n = m_use("XT2", LEADING)
            sp.wait_ge(m_full[b], n + 1)
            settle(sp)
            load_group(1)

            def load_record(dst, records, b, loaded):
                e = sp.value_load(blk_e[0:1, ds(b, 1)], min_val=0, max_val=E - 1)
                new = sp.value_load(blk_e[0:1, ds(b + NB, 1)], min_val=0, max_val=1)
                sp.dma_start(dst, records[ds(e, 1)].rearrange("o p w -> p (o w)"), cond=new).then_inc(loaded, 16)

            def load_gu(b, p, wait=True):
                if wait:
                    sp.wait_ge(gu_split, (b - 1) * FCH)
                settle(sp)
                load_record(raw_gu[:, p], gu_rec, b, gu_loaded[p])

            def load_rows_of(b, p, wait=True):
                if wait:
                    sp.wait_ge(ct_full, b - 1)
                    settle(sp)
                    sp.wait_ge(y_kept, (b - 1) * 2)
                    settle(sp)
                sp.dma_start(xr[:, p], xs_dram[ds(b * BT, BT), :].rearrange("(t p) c -> p t c", p=P)).then_inc(xr_loaded[p], 16)

            def load_dw(b, p, wait=True):
                if wait:
                    sp.wait_ge(dw_split, (b - 1) * DV)
                    settle(sp)
                    sp.wait_ge(dw_split_pool, (b - 1) * (FCH - DV))
                settle(sp)
                load_record(raw_dw[:, p], dw_rec, b, dw_loaded[p])

            def load_bias(b, p, wait=True):
                if wait:
                    sp.wait_ge(z_ready, (b - 1) * FCH)
                settle(sp)
                load_record(bias[:, p], bi_rec, b, bi_loaded[p])
            def turn(at):
                if at.seg != "last":
                    b, n = m_use("XT2", at)
                    sp.wait_ge(m_full[b], n + 1)
                    settle(sp)
                if at.seg == "first":
                    load_group(2)
                    return
                b, n = m_use("Y3", at)
                sp.wait_ge(m_free[b], n + 1)
                settle(sp)
                load_residual(at.g)
            turn(OPENING)
            with sp.Fori(0, NG - 3) as f:
                turn(Turn("mid", f + 1, f))
                load_group(f + 3)
            turn(Turn("mid", NG - 2, NG - 3))
            b, n = m_use("V4", Turn("mid", NG - 2, NG - 3))
            sp.wait_ge(m_full[b], n + 1)
            sp.wait_ge(slots_ready, 1)
            for b in range(2):
                load_gu(b, b, False)
            turn(CLOSING)
            b, n = m_use("OT3", CLOSING)
            sp.wait_ge(m_full[b], n + 1)
            for k in range(2):
                sp.wait_ge(scattered[k], 16 * NT)
            sp.wait_ge(xs_filled, 16 * FILLS)
            for b in range(2):
                load_rows_of(b, b, False)

            wait_dense_done(sp)
            sp.wait_ge(xs_filled, 16 * FILLS)

            load_bias(0, 0, False)
            load_bias(1, 1, False)
            load_dw(0, 0, False)
            load_gu(2, 0)
            load_dw(1, 1, False)
            load_rows_of(2, 0)
            load_bias(2, 0)
            with sp.Fori(0, (NB - 3) // 2) as i:
                for b, p in ((i * 2 + 3, 1), (i * 2 + 4, 0)):
                    load_gu(b, p)
                    load_dw(b - 1, 1 - p)
                    load_rows_of(b, p)
                    load_bias(b, p)
            load_dw(NB - 1, (NB - 1) % 2)

            sp.wait_ge(y_sent[0], 32 * ((NB + 1) // 2))
            sp.wait_ge(y_sent[1], 32 * (NB // 2))

            def load_rows(g, p):
                for k in range(2):
                    sp.dma_start(yg[:, p, k], y_dram[ds(g * GN + k * S, GN), :].rearrange("(t p) d -> p t d", p=P)).then_inc(yg_loaded[p], 16)

            def store_out(g):
                sp.wait_ge(sum_2, g + 1)
                settle(sp)
                sp.dma_start(out_g[ds(g, 1)].rearrange("o p t d -> p (o t) d"), xn[:, ds(g * GT, GT), :]).then_inc(out_stored, 16)
            for g in range(YB):
                load_rows(g, g)
            with sp.Fori(0, NG // YB - 1) as i:
                for p in range(YB):
                    store_out(i * YB + p)
                    load_rows(i * YB + (p + YB), p)
            for g in range(NG - YB, NG):
                store_out(g)
            sp.wait_ge(out_stored, 16 * NG)

        @block.gpsimd
        def _(pool):
            def load_dense(n):
                src, _, chunks, width = DENSE[n]
                if n >= 2:
                    pool.wait_ge(wraw_split, n - 1)
                pool.dma_start(wraw[:, n % 2, 0:chunks * width].rearrange("p (c n) -> p c n", c=chunks),
                               src.rearrange("(c p) n -> p c n", p=P)).then_inc(wraw_loaded[n % 2], 16)
            load_dense(0)
            nc.gpsimd.memset(zrec[:, :], 0.0).then_inc(zrec_ready, 1)
            pool.wait_ge(zrec_ready, 1)
            nc.gpsimd.iota(zrec[:, D:D + 1].bitcast(I32), [[0, 1]], base=2 * S, channel_multiplier=1).then_inc(zrec_ready, 1)
            for n, (_, dst, chunks, width) in enumerate(DENSE):
                if n + 1 < len(DENSE):
                    load_dense(n + 1)
                pool.wait_ge(wraw_loaded[n % 2], 16 * (n // 2 + 1))
                w = wraw[:, n % 2, 0:chunks * width]
                hi, lo = (dst[:, part].rearrange("p c n -> p (c n)") for part in range(2))
                nc.gpsimd.tensor_copy(hi, w).then_inc(wraw_hi, 1)
                pool.wait_ge(wraw_hi, n + 1)
                nc.gpsimd.tensor_tensor(lo, w, hi.bitcast(F32), ALU.subtract).then_inc(wraw_split, 1)

            done = [0]

            def follow(ins):
                done[0] += 1
                ins.then_inc(slot_step, 1)
                pool.wait_ge(slot_step, done[0])
            big = [P, NT, E]
            pool.wait_ge(counts_kept, 1)
            src, other = rt[5], [rt[10], rt[11]]
            for n in range(5):
                dst, ahead = other[n % 2], 1 << n
                follow(nc.gpsimd.tensor_tensor(dst[:, ahead:NT, :], src[:, ahead:NT, :], src[:, 0:NT - ahead, :], ALU.add))
                follow(nc.gpsimd.tensor_copy(dst[:, 0:ahead, :], src[:, 0:ahead, :]))
                src = dst
            follow(nc.gpsimd.tensor_tensor(rt[11][:, :, :], src[:, :, :], rt[5][:, :, :], ALU.subtract))
            follow(nc.gpsimd.tensor_tensor(rt[11][:, :, :], rt[11][:, :, :], rt[3][:, :, :], ALU.add))
            pool.wait_ge(starts_ready, 1)
            follow(nc.gpsimd.tensor_tensor(rt[11][:, :, :], rt[11][:, :, :], across(r8[4][:, :], big), ALU.add))
            for k, sel in enumerate((rt[2], rt[6])):
                follow(nc.gpsimd.tensor_tensor(fold[:, :, :], rt[11][:, :, :], sel[:, :, :], ALU.mult))
                for width in (4, 2, 1):
                    follow(nc.gpsimd.tensor_tensor(fold[:, :, 0:width], fold[:, :, 0:width], fold[:, :, width:2 * width], ALU.add))
                follow(nc.gpsimd.tensor_copy(slot[:, k, :], fold[:, :, 0]))
            assert done[0] == ROUTE_SLOTS

            def scatter(g):
                for j in range(GT):
                    t = g * GT + j
                    for k in range(2):
                        nc.gpsimd.tensor_copy(stage[:, k, 0:D], one(xn[:, ds(t, 1), :])).then_inc(staged, 1)
                        nc.gpsimd.tensor_copy(stage[:, k, D:REC], one(meta[:, k, ds(t, 1), :])).then_inc(staged, 1)
                        nc.gpsimd.tensor_copy(sidx[:, k:k + 1], slot[:, k, ds(t, 1)]).then_inc(staged, 1)
                        pool.wait_ge(staged, t * 6 + (3 * k + 3))
                        settle(pool)
                        nc.gpsimd.indirect_dma_start(xs_dram, bass.IndirectOffsetOnAxis(sidx[:, k:k + 1], 0), stage[:, k, :], None).then_inc(scattered[k], 16)
                    for k in range(2):
                        pool.wait_ge(scattered[k], t * 16 + 16)
                    settle(pool)

            def residual(g):
                pool.wait_ge(xres_loaded, g * 16 + 16)
                for j in range(GT):
                    pool.wait_ge(x2_ready, g * GT + (j + 1))
                    nc.gpsimd.tensor_tensor(xres[:, j, :], xres[:, j, :], x2[:, j, :], ALU.add).then_inc(x2_half, 1)
                    pool.wait_ge(x2_half, g * GT + (j + 1))
                    nc.gpsimd.tensor_tensor(xres[:, j, :], xres[:, j, :], b2_b, ALU.add).then_inc(x2_summed, 1)
            pool.wait_ge(small_loaded, 16 * 8)
            pool.wait_ge(xs_filled, 16 * FILLS)
            pool.wait_ge(slots_ready, 1)
            pool.wait_ge(xn_kept, NG)
            with pool.Fori(0, NG) as g:
                scatter(g)
                residual(g)

            wait_dense_done(pool)
            for p in range(2):
                nc.gpsimd.memset(ht[:, p, 1, FCH - 1, :].bitcast(F32), 0.0).then_inc(pad_low, 1)
            pool.wait_ge(pad_low, 2)

            def keep_meta(b, p):
                pool.wait_ge(xr_loaded[p], through(b, p, 16))
                if not isinstance(b, int) or b >= 2:
                    pool.wait_ge(y_sent[p], (b - p) * 16)
                    pool.wait_ge(y_ready, b - 1)
                settle(pool)
                nc.gpsimd.tensor_copy(dest[:, 2 * p:2 * p + 2], xr[:, p, :, D].bitcast(U32)).then_inc(y_kept, 1)
                nc.gpsimd.tensor_copy(wgt[:, p, :], xr[:, p, :, D + 1]).then_inc(y_kept, 1)

            def dw_low(b, p, c):
                cs = slice(c * D, (c + 1) * D)
                if c == DV:
                    pool.wait_ge(dw_hi, b * 2 + 2)
                nc.gpsimd.tensor_tensor(dw_s[:, p, 1, cs], raw_dw[:, p, cs], dw_s[:, p, 0, cs].bitcast(F32), ALU.subtract).then_inc(dw_split_pool, 1)

            def h_low(b, p, c):
                m = P if c < FCH - 1 else FR
                pool.wait_ge(hhi_ready, b * FCH + (c + 1))
                nc.gpsimd.tensor_tensor(ht[0:m, p, 1, c, :], hf[0:m, ring(c), :], ht[0:m, p, 0, c, :].bitcast(F32), ALU.subtract).then_inc(h_split, 1)

            def send(b, p):
                pool.wait_ge(y_ready, b + 1)
                settle(pool)
                for t in range(2):
                    index = dest[:, 2 * p + t:2 * p + t + 1]
                    nc.gpsimd.indirect_dma_start(y_dram, bass.IndirectOffsetOnAxis(index, 0), ys[:, p, t, :], None,
                                                 bounds_check=2 * S - 1, oob_is_err=False).then_inc(y_sent[p], 16)

            def body(b, p):
                for c in range(FCH):
                    h_low(b, p, c)
                    if c == 2:
                        keep_meta(b, p)
                for c in range(DV, FCH):
                    dw_low(b, p, c)
                if not isinstance(b, int) or b >= 1:
                    send(b - 1, 1 - p)
            blocks_of(pool, body)
            send(NB - 1, (NB - 1) % 2)

        @block.scalar
        def _(act):
            def sqrt_group(g, par):
                act.wait_ge(stats_ready, g * GT + GT)
                nc.scalar.activation(sd[:, par], mv[:, par, :, 1], ACT.Sqrt, bias=eps).then_inc(sd_ready, 1)

            def copy_group(g, par):
                act.wait_ge(xn_ready, g * GT + GT)
                nc.scalar.activation(xn[:, ds(g * GT, GT), :], xg[:, par], ACT.Copy).then_inc(xn_kept, 1)
                act.wait_ge(xt_full, g + 1)
                act.wait_ge(gate_full, g + 1)
                for k in range(KC):
                    nc.scalar.activation(xt[:, par % 2, k, :], bank[2 * (par % 2) + k][:, :], ACT.Copy).then_inc(xt_copied, 1)
            act.sem_inc(xt_copied, 4)
            act.wait_ge(const_loaded, 16)
            with act.Fori(0, NG // XB) as i:
                sqrt_group(i * XB, 0)
                for par in range(XB):
                    if par + 1 < XB:
                        sqrt_group(i * XB + (par + 1), (par + 1) % 2)
                    copy_group(i * XB + par, par)

            def full(name, at):
                b, n = m_use(name, at)
                act.wait_ge(m_full[b], n + 1)
                return m_bank[b]

            def window_hi(at, n):
                w = BT if n < 2 else P
                bk = full(f"XT{n}", at)
                nc.scalar.activation(xw_h[:, :, n * BT:n * BT + w], bk[:, :].rearrange("p (k c) -> p k c", k=KC)[:, :, 0:w], ACT.Copy).then_inc(m_hi, 1)

            def q_hi(at, c):
                bk = full(f"Q{c}", at)
                nc.scalar.activation(q_h[:, c, :], bk[:, :], ACT.Identity, bias=col[:, c:c + 1]).then_inc(m_hi, 1)

            def k_hi(at, n):
                c, half = n // 2, n % 2
                bk = full(f"K{n}", at)
                nc.scalar.activation(k_h[:, c, half * WN // 2:(half + 1) * WN // 2], bk[:, 0:WN // 2], ACT.Identity, bias=col[:, 2 + c:3 + c]).then_inc(m_hi, 1)

            def v_copy(at, j):
                b, n = m_use(f"V{j}", at)
                bk = full(f"V{j}", at)
                nc.scalar.activation(v[:, j, :, 0:DH], bk[:, 0:D].rearrange("p (h d) -> p h d", d=DH), ACT.Copy).then_inc(m_free[b], 1)

            def probs(g, j, pairs):
                if 0 in pairs:
                    act.wait_ge(neg_max, g * GT + (j + 1))
                for r in pairs:
                    for c in range(KC):
                        h = r + 4 * c
                        nc.scalar.activation(sm[:, j % 2, h, :], sm[:, j % 2, h, :], ACT.Exp, bias=nmx[:, j % 2, h:h + 1], scale=SCALE).then_inc(probs_ready, 1)

            def pt_copy(g, j, u):
                act.wait_ge(t_full[1], (g * GT + j) * 2 + (u // 2 + 1))
                nc.scalar.activation(pt[:, 1].rearrange("p a n -> p (a n)"), t_bank[1][:, :], ACT.Copy).then_inc(t_free[1], 1)

            def ot_hi(at, j):
                bk = full(f"OT{j}", at)
                nc.scalar.activation(ot_h[:, :, :].rearrange("p k n -> p (k n)"), bk[:, 0:D], ACT.Copy).then_inc(m_hi, 1)

            def x2_hi(at):
                for n in range(2):
                    bk = full(f"X{n}", at)
                    nc.scalar.activation(x2t_h[:, :, n * BT:(n + 1) * BT], bk[:, :].rearrange("p (k c) -> p k c", k=KC), ACT.Copy).then_inc(m_hi, 1)

            def gelu(at):
                for c in range(FC1):
                    bk = full(f"F{c}", at)
                    b, n = m_use(f"F{c}", at)
                    if c >= 2:
                        act.wait_ge(gelu_split, at.g * FC1 + (c - 1))
                    nc.scalar.activation(h1[:, c % 2, :], bk[:, :], ACT.Gelu, bias=col[:, 4 + c:5 + c]).then_inc(m_free[b], 1)
                    act.wait_ge(m_free[b], n + 1)
                    nc.scalar.activation(h_h[:, c, :], h1[:, c % 2, :], ACT.Copy).then_inc(gelu_hi, 1)

            act.sem_inc(t_free[1], 1)
            act.wait_ge(small_loaded, 16 * 8)
            for n in range(3):
                window_hi(LEADING, n)
            for c in range(KC):
                q_hi(LEADING, c)
            for n in range(4):
                k_hi(LEADING, n)
            for j in range(WT):
                v_copy(LEADING, j)

            def turn(at):
                g, more = at.g, at.seg != "last"
                probs(g, 0, range(PAIRS))
                for j in range(GT - 1):
                    if j:
                        ot_hi(at, j - 1)
                    pt_copy(g, j, 1)
                    probs(g, j + 1, range(2))
                    pt_copy(g, j, 3)
                    probs(g, j + 1, range(2, PAIRS))
                    if more:
                        window_hi(at, j)
                    if at.seg == "first" and j == 1:
                        act.wait_ge(route, ROUTE_EXP)
                        nc.scalar.activation(rt[8][:, :, :], rt[7][:, :, :], ACT.Exp).then_inc(route_exp, 1)
                        nc.scalar.activation(r1[6][:, :], r1[5][:, :], ACT.Exp).then_inc(route_exp, 1)
                ot_hi(at, GT - 2)
                pt_copy(g, GT - 1, 1)
                if more:
                    q_hi(at, 0)
                    q_hi(at, 1)
                pt_copy(g, GT - 1, 3)
                if more:
                    k_hi(at, 0)
                    k_hi(at, 1)
                    k_hi(at, 2)
                ot_hi(at, GT - 1)
                if more:
                    k_hi(at, 3)
                    v_copy(at, 0)
                    v_copy(at, 1)
                act.wait_ge(ln_stats, g * GT + GT)
                nc.scalar.activation(sd2[:, :], mv2[:, :, 1], ACT.Sqrt, bias=eps).then_inc(ln_sd, 1)
                if more:
                    for j in range(2, WT):
                        v_copy(at, j)
                x2_hi(at)
                gelu(at)
            turns_of(act, turn)

            wait_dense_done(act)

            def rows_hi(b, p):
                act.wait_ge(ct_full, b + 1)
                nc.scalar.activation(xt_h[:, p], bank[4][:, :].rearrange("p (k c) -> p k c", k=KC), ACT.Copy).then_inc(ct_hi, 1)

            def gate_bias(b, p, c):
                act.wait_ge(gu_full, b * FCH + (c + 1))
                if c < FCH - 1:
                    nc.scalar.activation(gs[:, ring(c), :], bank[ring(c)][:, 0:BT], ACT.Identity, bias=bias[:, p, c:c + 1]).then_inc(gs_ready, 1)
                else:
                    nc.scalar.activation(gs[WIN:WIN + FR, 3, :], bank[3][0:FR, 0:BT], ACT.Identity, bias=bias[0:FR, p, c:c + 1]).then_inc(gs_ready, 1)

            def silu(b, p, c):
                m = P if c < FCH - 1 else FR
                act.wait_ge(z_ready, b * FCH + (c + 1))
                nc.scalar.activation(hf[0:m, ring(c), :], hf[0:m, ring(c), :], ACT.Silu).then_inc(hf_ready, 1)
                if c == 0 and (not isinstance(b, int) or b >= 2):
                    act.wait_ge(y_full, b - 1)
                act.wait_ge(hf_ready, b * FCH + (c + 1))
                nc.scalar.activation(ht[0:m, p, 0, c, :], hf[0:m, ring(c), :], ACT.Copy).then_inc(hhi_ready, 1)

            def gu_high(b, p, c):
                if c == FCH - GA:
                    act.wait_ge(gu_loaded[p], through(b, p, 16))
                    if not isinstance(b, int) or b >= 2:
                        act.wait_ge(gu_full, (b - 1) * FCH)
                nc.scalar.activation(gu_s[:, p, 0, gu_cols(c)], raw_gu[:, p, gu_cols(c)], ACT.Copy).then_inc(gu_hi_act, 1)

            def dw_high(b, p):
                act.wait_ge(dw_loaded[p], through(b, p, 16))
                if not isinstance(b, int) or b >= 2:
                    act.wait_ge(y_full, b - 1)
                for cs in (slice(0, DV * D), slice(DV * D, DWW)):
                    nc.scalar.activation(dw_s[:, p, 0, cs], raw_dw[:, p, cs], ACT.Copy).then_inc(dw_hi, 1)

            def body(b, p):
                act.wait_ge(bi_loaded[p], through(b, p, 16))
                more = not isinstance(b, int) or b < NB - 1
                for c in range(FCH + 1):
                    if c < FCH:
                        gate_bias(b, p, c)
                    if c >= 1:
                        silu(b, p, c - 1)
                    if c == ROWS_AT and more:
                        rows_hi(b + 1, 1 - p)
                if more:
                    for c in range(FCH - GA, FCH):
                        gu_high(b + 1, 1 - p, c)
                dw_high(b, p)
            act.wait_ge(pad_high, 2)
            rows_hi(0, 0)
            for c in range(FCH - GA, FCH):
                gu_high(0, 0, c)
            blocks_of(act, body)

        @block.vector
        def _(dve):
            dve.wait_ge(const_loaded, 16)

            def statistics(g, i, par):
                dve.wait_ge(xg_loaded[par], i * 16 + 16)
                for t in range(GT):
                    nc.vector.bn_stats(st6[:, par % 2, t, :], xg[:, par, t, :]).then_inc(stats6, 1)
                dve.wait_ge(stats6, g * GT + GT)
                settle(dve)
                for t in range(GT):
                    nc.vector.bn_aggr(mv[:, par % 2, t, :], st6[:, par % 2, t, :]).then_inc(stats_ready, 1)

            def standardise(g, par):
                dve.wait_ge(stats_ready, g * GT + GT)
                dve.wait_ge(sd_ready, g + 1)
                nc.vector.reciprocal(rstd[:, par % 2], sd[:, par % 2]).then_inc(rstd_ready, 1)
                dve.wait_ge(rstd_ready, g + 1)
                for t in range(GT):
                    nc.vector.tensor_scalar(xg[:, par, t, :], xg[:, par, t, :], mv[:, par % 2, t, 0:1], rstd[:, par % 2, t:t + 1],
                                            ALU.subtract, ALU.mult).then_inc(xn_ready, 1)
            with dve.Fori(0, NG // XB) as i:
                statistics(i * XB, i, 0)
                for par in range(XB):
                    if par + 1 < XB:
                        statistics(i * XB + (par + 1), i, par + 1)
                    standardise(i * XB + par, par)

            steps = [0]

            def link(ins):
                steps[0] += 1
                ins.then_inc(route, 1)
                dve.wait_ge(route, steps[0])
            big = [P, NT, E]
            rev = across(cst[:, C_REV:C_REV + E], big)
            logits, one1, one2 = rt[0], rt[2], rt[6]
            dve.wait_ge(gate_full, NG + 2)
            dve.wait_ge(small_loaded, 16 * 8)
            link(nc.vector.tensor_tensor(logits[:, :, :], bank[4][:, 0:NT * E].rearrange("p (t e) -> p t e", e=E), across(gb_b[:, :], big), ALU.add))

            def pick(values, top, sel, scratch, index):
                link(nc.vector.tensor_reduce(top[:, :], values[:, :, :], AX.X, ALU.max))
                link(nc.vector.tensor_tensor(scratch[:, :, :], values[:, :, :], spread(top[:, :], big), ALU.is_equal))
                link(nc.vector.tensor_tensor(scratch[:, :, :], scratch[:, :, :], rev, ALU.mult))
                link(nc.vector.tensor_reduce(index[:, :], scratch[:, :, :], AX.X, ALU.max))
                link(nc.vector.tensor_tensor(sel[:, :, :], spread(index[:, :], big), rev, ALU.is_equal))

            def route_first():
                pick(logits, r1[0], one1, rt[1], r1[1])

            def route_second():
                link(nc.vector.scalar_tensor_tensor(rt[3][:, :, :], one1[:, :, :], -3e38, logits[:, :, :], ALU.mult, ALU.add))
                pick(rt[3], r1[2], one2, rt[4], r1[3])
                link(nc.vector.tensor_tensor(rt[7][:, :, :], logits[:, :, :], spread(r1[0][:, :], big), ALU.subtract))
                link(nc.vector.tensor_tensor(r1[5][:, :], r1[2][:, :], r1[0][:, :], ALU.subtract))
                assert steps[0] == ROUTE_EXP
                link(nc.vector.tensor_tensor(rt[9][:, :, :], one1[:, :, :], one2[:, :, :], ALU.add))
                assert steps[0] == ROUTE_PICKS

            def route_weights():
                dve.wait_ge(route_exp, 2)
                link(nc.vector.tensor_reduce(r1[4][:, :], rt[8][:, :, :], AX.X, ALU.add))
                link(nc.vector.scalar_tensor_tensor(r1[7][:, :], r1[4][:, :], 1e-20, r1[6][:, :], ALU.mult, ALU.add))
                link(nc.vector.tensor_scalar(r1[8][:, :], r1[7][:, :], 1.0, None, ALU.add))
                link(nc.vector.reciprocal(r1[9][:, :], r1[8][:, :]))
                link(nc.vector.tensor_copy(meta[:, 0, :, 1], r1[9][:, :]))
                link(nc.vector.tensor_tensor(meta[:, 1, :, 1], r1[9][:, :], r1[6][:, :], ALU.mult))
                for k in range(2):
                    link(nc.vector.tensor_scalar(meta[:, k, :, 0].bitcast(I32), cst[:, C_TOK:C_TOK + NT], float(k * S), None, ALU.add))

            def route_starts(at):
                bk, free = full("C", at)
                for n, part in enumerate((rt[3], rt[5])):
                    ins = nc.vector.tensor_copy(part[:, :, :], bk[:, n * NT * E:(n + 1) * NT * E].rearrange("p (t e) -> p t e", e=E))
                ins.then_inc(free, 1)
                b, n = m_use("C", at)
                dve.wait_ge(m_free[b], n + 1)
                dve.sem_inc(counts_kept, 1)
                link(nc.vector.tensor_reduce(r8[5][:, :], rt[5][:, :, :].rearrange("p t e -> p e t"), AX.X, ALU.add))
                link(nc.vector.tensor_scalar(r8i[0][:, :], r8[5][:, :], float(BT - 1), None, ALU.add))
                link(nc.vector.tensor_scalar(r8i[1][:, :], r8i[0][:, :], BT.bit_length() - 1, None, ALU.logical_shift_right))
                link(nc.vector.tensor_scalar(r8[0][:, :], r8i[1][:, :], float(BT), None, ALU.mult))
                src = r8[0]
                for n in range(3):
                    dst, ahead = r8[1 + n], 1 << n
                    link(nc.vector.tensor_tensor(dst[:, ahead:E], src[:, ahead:E], src[:, 0:E - ahead], ALU.add))
                    link(nc.vector.tensor_copy(dst[:, 0:ahead], src[:, 0:ahead]))
                    src = dst
                nc.vector.tensor_tensor(r8[4][:, :], r8[3][:, :], r8[0][:, :], ALU.subtract).then_inc(starts_ready, 1)

            def route_blocks():
                wide = [P, NB, E]
                link(nc.vector.tensor_tensor(rb[:, :, :], spread(cst[:, C_BLK:C_BLK + NB], wide), across(r8[3][:, :], wide), ALU.is_ge))
                link(nc.vector.tensor_reduce(rbs[:, :], rb[:, :, :], AX.X, ALU.add))
                link(nc.vector.tensor_scalar(rbs[0:1, :], rbs[0:1, :], float(E - 1), None, ALU.min))
                link(nc.vector.tensor_copy(new[0:1, :], cst[0:1, C_ONE:C_ONE + NB]))
                link(nc.vector.tensor_tensor(new[0:1, 2:NB], rbs[0:1, 2:NB], rbs[0:1, 0:NB - 2], ALU.not_equal))
                link(nc.vector.tensor_copy(blk_e[0:1, NB:2 * NB], new[0:1, :]))
                nc.vector.tensor_copy(blk_e[0:1, 0:NB], rbs[0:1, :]).then_inc(slots_ready, 1)

            def full(name, at):
                b, n = m_use(name, at)
                dve.wait_ge(m_full[b], n + 1)
                if name.startswith(HI):
                    dve.wait_ge(m_hi, hi_use(name, at) + 1)
                return m_bank[b], m_free[b]

            def window_lo(at, n):
                w = BT if n < 2 else P
                bk, free = full(f"XT{n}", at)
                cs = slice(n * BT, n * BT + w)
                nc.vector.tensor_tensor(xw_l[:, :, cs], bk[:, :].rearrange("p (k c) -> p k c", k=KC)[:, :, 0:w], xw_h[:, :, cs].bitcast(F32), ALU.subtract).then_inc(free, 1)

            def q_lo(at, c):
                bk, free = full(f"Q{c}", at)
                nc.vector.scalar_tensor_tensor(q_l[:, c, :], bk[:, :], col[:, c:c + 1], q_h[:, c, :].bitcast(F32), ALU.add, ALU.subtract).then_inc(free, 1)

            def k_lo(at, n):
                c, half = n // 2, n % 2
                bk, free = full(f"K{n}", at)
                cs = slice(half * WN // 2, (half + 1) * WN // 2)
                nc.vector.scalar_tensor_tensor(k_l[:, c, cs], bk[:, 0:WN // 2], col[:, 2 + c:3 + c], k_h[:, c, cs].bitcast(F32), ALU.add, ALU.subtract).then_inc(free, 1)

            def split_bv():
                for k in range(KC):
                    bv = col[:, 2 * KC + FC1 + k:2 * KC + FC1 + k + 1].to_broadcast([P, P])
                    nc.vector.tensor_copy(ot_h[:, k, :], bv).then_inc(bv_split, 1)
                    dve.wait_ge(bv_split, 2 * k + 1)
                    nc.vector.tensor_tensor(ot_l[:, k, :], bv, ot_h[:, k, :].bitcast(F32), ALU.subtract).then_inc(bv_split, 1)

            def add_bv(at):
                bk, free = full("BO", at)
                nc.vector.tensor_tensor(bo_b, bk[:, 0:D], bo_b, ALU.add).then_inc(free, 1)

            def masked_max(at, j, r, mask):
                b, n = s_use(at, j, r)
                dve.wait_ge(s_full[b], n + 1)
                settle(dve)
                for c in range(KC):
                    h = r + 4 * c
                    nc.vector.tensor_tensor_reduce(out=sm[:, j % 2, h, :], in0=s_bank[b][:, c * 2 * P:(c + 1) * 2 * P], in1=mask, scale=1.0,
                                                   scalar=-3e38, op0=ALU.add, op1=ALU.max, accum_out=mx[:, j % 2, h:h + 1]).then_inc(s_free[b], 1)

            def negate_max(at, j):
                for r in range(1, PAIRS):
                    b, n = s_use(at, j, r)
                    dve.wait_ge(s_free[b], (n + 1) * KC + KC)
                nc.vector.tensor_scalar(nmx[:, j % 2, :], mx[:, j % 2, :], -SCALE, None, ALU.mult).then_inc(neg_max, 1)

            def pt_copy(g, j, u):
                dve.wait_ge(t_full[0], (g * GT + j) * 2 + (u // 2 + 1))
                nc.vector.tensor_copy(pt[:, 0].rearrange("p a n -> p (a n)"), t_bank[0][:, :]).then_inc(t_free[0], 1)

            def normalise(at, j):
                n = at.g * GT + j
                o = o_bank[:, 0:H * (DH + 1)].rearrange("p (h d) -> p h d", d=DH + 1)
                dve.wait_ge(o_full, n + 1)
                nc.vector.reciprocal(rsum[:, :], o[:, :, DH]).then_inc(rsum_ready, 1)
                dve.wait_ge(rsum_ready, n + 1)
                nc.vector.tensor_tensor(on[:, :].rearrange("p (h d) -> p h d", d=DH), o[:, :, 0:DH],
                                        spread(rsum[:, :], [P, H, DH]), ALU.mult).then_inc(o_free, 1)

            def ot_lo(at, j):
                bk, free = full(f"OT{j}", at)
                nc.vector.tensor_tensor(ot_l[:, :, :].rearrange("p k n -> p (k n)"), bk[:, 0:D], ot_h[:, :, :].rearrange("p k n -> p (k n)").bitcast(F32), ALU.subtract).then_inc(free, 1)

            def add_attention(at, j):
                bk, free = full(f"A{j}", at)
                n = at.g * GT + (j + 1)
                _, k = m_use(f"A{j}", at)
                nc.vector.tensor_tensor(x2[:, j, :], bk[:, 0:D], one(xn[:, ds(at.g * GT + j, 1), :]), ALU.add).then_inc(free, 1)
                dve.wait_ge(free, k + 1)
                nc.vector.tensor_tensor(x2[:, j, :], x2[:, j, :], bo_b, ALU.add).then_inc(pre_ready, 1)
                dve.wait_ge(pre_ready, n)
                nc.vector.bn_stats(st2[:, j, :], x2[:, j, :]).then_inc(ln6, 1)
                dve.wait_ge(ln6, n)
                settle(dve)
                nc.vector.bn_aggr(mv2[:, j, :], st2[:, j, :]).then_inc(ln_stats, 1)
                dve.wait_ge(ln_stats, n)
                nc.vector.scalar_tensor_tensor(x2[:, j, :], x2[:, j, :], mv2[:, j, 0:1], gam_b, ALU.subtract, ALU.mult).then_inc(scaled, 1)

            def layernorm_scale(g):
                dve.wait_ge(ln_sd, g + 1)
                nc.vector.reciprocal(rs2[:, :], sd2[:, :]).then_inc(ln_rstd, 1)
                dve.wait_ge(ln_rstd, g + 1)
                dve.wait_ge(scaled, g * GT + GT)

            def layernorm(g, j):
                nc.vector.scalar_tensor_tensor(x2[:, j, :], x2[:, j, :], rs2[:, j:j + 1], bet_b, ALU.mult, ALU.add).then_inc(x2_ready, 1)

            def x2_lo(at, n):
                bk, free = full(f"X{n}", at)
                cs = slice(n * BT, (n + 1) * BT)
                nc.vector.tensor_tensor(x2t_l[:, :, cs], bk[:, :].rearrange("p (k c) -> p k c", k=KC), x2t_h[:, :, cs].bitcast(F32), ALU.subtract).then_inc(free, 1)

            def gelu_lo(g):
                for c in range(FC1):
                    dve.wait_ge(gelu_hi, g * FC1 + (c + 1))
                    nc.vector.tensor_tensor(h_l[:, c, :], h1[:, c % 2, :], h_h[:, c, :].bitcast(F32), ALU.subtract).then_inc(gelu_split, 1)

            def dense_sum(at, j):
                if j == 0:
                    for k in range(2):
                        dve.wait_ge(scattered[k], at.f * (16 * GT) + 16 * GT)
                dve.wait_ge(x2_summed, at.f * GT + (j + 1))
                bk, free = full(f"Y{j}", at)
                nc.vector.tensor_tensor(one(xn[:, ds(at.f * GT + j, 1), :]), bk[:, 0:D], xres[:, j, :], ALU.add).then_inc(free, 1)

            for b in range(SB):
                dve.sem_inc(s_free[b], KC)
            dve.sem_inc(t_free[0], 1)
            dve.sem_inc(o_free, 1)
            nc.vector.tensor_copy(v[:, :, :, DH], cst[:, C_ONE:C_ONE + WT * H].rearrange("p (j h) -> p j h", h=H)).then_inc(ones_set, 1)
            for n in range(3):
                window_lo(LEADING, n)
            route_first()
            for c in range(KC):
                q_lo(LEADING, c)
            for n in range(4):
                k_lo(LEADING, n)
            route_second()

            for r in range(PAIRS):
                masked_max(LEADING, GT, r, begin)
            negate_max(LEADING, GT)

            def turn(at):
                g, more = at.g, at.seg != "last"
                for j in range(GT - 1):
                    mask = end if at.seg == "last" and j == GT - 2 else mid
                    masked_max(at, j + 1, 0, mask)
                    if j:
                        ot_lo(at, j - 1)
                    masked_max(at, j + 1, 1, mask)
                    masked_max(at, j + 1, 2, mask)
                    pt_copy(g, j, 0)
                    if j:
                        add_attention(at, j - 1)
                    masked_max(at, j + 1, 3, mask)
                    negate_max(at, j + 1)
                    pt_copy(g, j, 2)
                    if at.seg != "first":
                        dense_sum(at, j)
                    normalise(at, j)
                    if more:
                        window_lo(at, j)
                    if at.seg == "first":
                        if j == 0:
                            wait_first_done(dve)
                            split_bv()
                            route_starts(at)
                            add_bv(at)
                        elif j == 1:
                            route_weights()
                        else:
                            route_blocks()
                pt_copy(g, GT - 1, 0)
                ot_lo(at, GT - 2)
                if more:
                    q_lo(at, 0)
                add_attention(at, GT - 2)
                pt_copy(g, GT - 1, 2)
                if more:
                    q_lo(at, 1)
                    k_lo(at, 0)
                    k_lo(at, 1)
                normalise(at, GT - 1)
                if more:
                    k_lo(at, 2)
                if at.seg != "first":
                    dense_sum(at, GT - 1)
                ot_lo(at, GT - 1)
                if more:
                    k_lo(at, 3)
                add_attention(at, GT - 1)
                if more:
                    masked_max(at, GT, 0, mid)
                layernorm_scale(g)
                layernorm(g, 0)
                layernorm(g, 1)
                layernorm(g, 2)
                layernorm(g, 3)
                if more:
                    masked_max(at, GT, 1, mid)
                x2_lo(at, 0)
                x2_lo(at, 1)
                if more:
                    masked_max(at, GT, 2, mid)
                    masked_max(at, GT, 3, mid)
                    negate_max(at, GT)
                gelu_lo(g)
            turns_of(dve, turn)
            for j in range(GT):
                dense_sum(TRAILING, j)

            wait_dense_done(dve)
            for p in range(2):
                nc.vector.tensor_copy(ht[:, p, 0, FCH - 1, :], cst[:, C_HOT:C_HOT + 1].to_broadcast([P, BT])).then_inc(pad_high, 1)

            def gu_high(b, p, c):
                if c == 0:
                    dve.wait_ge(gu_loaded[p], through(b, p, 16))
                    if not isinstance(b, int) or b >= 2:
                        dve.wait_ge(gu_full, (b - 1) * FCH)
                nc.vector.tensor_copy(gu_s[:, p, 0, gu_cols(c)], raw_gu[:, p, gu_cols(c)]).then_inc(gu_hi, 1)

            def gu_low(b, p, c):
                if c < FCH - GA:
                    dve.wait_ge(gu_hi, b * (FCH - GA) + (c + 1))
                else:
                    dve.wait_ge(gu_hi_act, b * GA + (c + 1 - (FCH - GA)))
                nc.vector.tensor_tensor(gu_s[:, p, 1, gu_cols(c)], raw_gu[:, p, gu_cols(c)], gu_s[:, p, 0, gu_cols(c)].bitcast(F32), ALU.subtract).then_inc(gu_split, 1)

            def dw_low(b, p):
                dve.wait_ge(dw_hi, b * 2 + 1)
                cs = slice(0, DV * D)
                nc.vector.tensor_tensor(dw_s[:, p, 1, cs], raw_dw[:, p, cs], dw_s[:, p, 0, cs].bitcast(F32), ALU.subtract).then_inc(dw_split, DV)

            def up_times_gate(b, p, c):
                dve.wait_ge(gs_ready, b * FCH + (c + 1))
                n = before(b, c)
                if n is not None:
                    dve.wait_ge(h_split, n)
                if c < FCH - 1:
                    nc.vector.scalar_tensor_tensor(hf[:, ring(c), :], bank[ring(c)][:, BT:2 * BT], bias[:, p, FCH + c:FCH + c + 1], gs[:, ring(c), :],
                                                   ALU.add, ALU.mult).then_inc(z_ready, 1)
                else:
                    nc.vector.scalar_tensor_tensor(hf[0:FR, 3, :], bank[3][WIN:WIN + FR, 0:BT], bias[WIN:WIN + FR, p, FCH + c:FCH + c + 1], gs[WIN:WIN + FR, 3, :],
                                                   ALU.add, ALU.mult).then_inc(z_ready, 1)

            def rows_lo(b, p):
                dve.wait_ge(ct_hi, b + 1)
                nc.vector.tensor_tensor(xt_l[:, p], bank[4][:, :].rearrange("p (k c) -> p k c", k=KC), xt_h[:, p].bitcast(F32), ALU.subtract).then_inc(ct_split, 1)

            def weigh(b, p):
                dve.wait_ge(y_full, b + 1)
                dve.wait_ge(y_kept, b * 2 + 2)
                if not isinstance(b, int) or b >= 2:
                    dve.wait_ge(y_sent[p], (b - p) * 16)
                for t in range(2):
                    ins = nc.vector.tensor_scalar(ys[:, p, t, :], bank[5 + p][:, t * D:(t + 1) * D], wgt[:, p, t:t + 1], None, ALU.mult)
                ins.then_inc(y_ready, 1)

            def body(b, p):
                dve.wait_ge(bi_loaded[p], through(b, p, 16))
                more = not isinstance(b, int) or b < NB - 1
                for c in range(FCH):
                    if more and c < FCH - GA:
                        gu_high(b + 1, 1 - p, c)
                    up_times_gate(b, p, c)
                    if more and c < FCH - GA:
                        gu_low(b + 1, 1 - p, c)
                    if more and c == ROWS_AT:
                        rows_lo(b + 1, 1 - p)
                if more:
                    for c in range(FCH - GA, FCH):
                        gu_low(b + 1, 1 - p, c)
                dw_low(b, p)
                if not isinstance(b, int) or b >= 1:
                    weigh(b - 1, 1 - p)
            for c in range(FCH):
                if c < FCH - GA:
                    gu_high(0, 0, c)
                gu_low(0, 0, c)
                if c == 0:
                    rows_lo(0, 0)
            blocks_of(dve, body)
            weigh(NB - 1, (NB - 1) % 2)

            def add_rows(g, p, n):
                dve.wait_ge(yg_loaded[p], n * 32 + 32)
                span = xn[:, ds(g * GT, GT), :]
                nc.vector.tensor_tensor(span, span, yg[:, p, 0], ALU.add).then_inc(sum_1, 1)
                dve.wait_ge(sum_1, g + 1)
                nc.vector.tensor_tensor(span, span, yg[:, p, 1], ALU.add).then_inc(sum_2, 1)
            with dve.Fori(0, NG // YB) as i:
                for p in range(YB):
                    add_rows(i * YB + p, p, i)

        @block.tensor
        def _(pe):
            def passes(dst, lhs, rhs, start, stop):
                nc.tensor.matmul(dst, lhs[0], rhs[0], start=start, stop=False)
                nc.tensor.matmul(dst, lhs[0], rhs[1], start=False, stop=False)
                return nc.tensor.matmul(dst, lhs[1], rhs[0], start=False, stop=stop)

            pe.sem_inc(gate_full, 2)
            pe.wait_ge(const_loaded, 16)
            pe.wait_ge(small_loaded, 16 * 8)

            def turn_group(g, par):
                pe.wait_ge(xn_ready, g * GT + GT)
                pe.wait_ge(xt_copied, g * 2 + 2)
                for k in range(KC):
                    for t in range(GT):
                        ins = nc.tensor.transpose(bank[2 * (par % 2) + k][:, t * P:(t + 1) * P], xg[:, par, t, k * P:(k + 1) * P], ident)
                ins.then_inc(xt_full, 1)

            def gate_group(g, par):
                pe.wait_ge(xt_copied, g * 2 + 6)
                for t in range(GT):
                    for k in range(KC):
                        ins = nc.tensor.matmul(bank[4][:, ds(g * (GT * E) + t * E, E)], xt[:, par % 2, k, t * P:(t + 1) * P], gate_s[:, k, :],
                                               start=(k == 0), stop=(k == KC - 1))
                ins.then_inc(gate_full, 1)
            with pe.Fori(0, NG // XB) as i:
                turn_group(i * XB, 0)
                for par in range(XB):
                    if par + 1 < XB:
                        turn_group(i * XB + (par + 1), par + 1)
                    gate_group(i * XB + par, par)

            def take(name, at, after=()):
                b, n = m_use(name, at)
                for other in after:
                    bo, no = m_use(other, at)
                    if bo != b:
                        pe.wait_ge(m_free[bo], no + 1)
                if not isinstance(n, int) or n > 0:
                    pe.wait_ge(m_free[b], n)
                return m_bank[b], m_full[b]

            every = slice(None)

            def parts(w, k, cs):
                return [w[:, part, k, cs] for part in range(2)]

            def pair(h, l, *index):
                return [h[index], l[index]]

            def window(at, n):
                bk, full = take(f"XT{n}", at)
                for j in range(2 * n, min(2 * n + 2, WT)):
                    for k in range(KC):
                        ins = nc.tensor.transpose(bk[:, k * BT + (j % 2) * P:k * BT + (j % 2) * P + P], xwin[:, j, k * P:(k + 1) * P], ident)
                ins.then_inc(full, 1)

            def query(at, c):
                bk, full = take(f"Q{c}", at, ("XT2",) if c == 0 else ("XT1",))
                for k in range(KC):
                    ins = passes(bk[:, :], parts(wq_s, k, slice(c * P, (c + 1) * P)), pair(xw_h, xw_l, every, k, slice(WIN, WIN + GN)), k == 0, k == KC - 1)
                ins.then_inc(full, 1)

            def keys(at, n):
                c, half = n // 2, n % 2
                bk, full = take(f"K{n}", at)
                for k in range(KC):
                    ins = passes(bk[:, 0:WN // 2], parts(wk_s, k, slice(c * P, (c + 1) * P)),
                                 pair(xw_h, xw_l, every, k, slice(half * WN // 2, (half + 1) * WN // 2)), k == 0, k == KC - 1)
                ins.then_inc(full, 1)

            def values(at, j):
                bk, full = take(f"V{j}", at)
                for k in range(KC):
                    ins = passes(bk[:, 0:D], pair(xw_h, xw_l, every, k, slice(j * P, (j + 1) * P)), parts(wv_s, k, every), k == 0, k == KC - 1)
                ins.then_inc(full, 1)

            def scores(at, j, r):
                b, n = s_use(at, j, r)
                pe.wait_ge(s_free[b], n * KC + KC)
                rows = slice(r * DH, (r + 1) * DH)
                for c in range(KC):
                    ins = passes(s_bank[b][:, c * 2 * P:(c + 1) * 2 * P], pair(q_h, q_l, rows, c, slice(j % GT * P, (j % GT + 1) * P)),
                                 pair(k_h, k_l, rows, c, slice(j % GT * P, (j % GT + 2) * P)), True, True)
                ins.then_inc(s_full[b], 1)

            def next_scores(at):
                values(at, 0)
                values(at, 1)
                for r in range(PAIRS):
                    scores(at, GT, r)
                    if r + 2 < WT - 1:
                        values(at, r + 2)

            def turn_probs(at, j, r):
                n = at.g * GT + j
                pe.wait_ge(probs_ready, n * H + (2 * r + 2))
                pe.wait_ge(t_free[r % 2], n * 2 + (r // 2 + 1))
                for c in range(KC):
                    for kb in range(2):
                        ins = nc.tensor.transpose(t_bank[r % 2][:, (2 * c + kb) * P:(2 * c + kb + 1) * P], sm[:, j % 2, r + 4 * c, kb * P:(kb + 1) * P], ident)
                ins.then_inc(t_full[r % 2], 1)

            def times_v(at, j, r):
                n = at.g * GT + j
                if r == 0:
                    pe.wait_ge(o_free, n + 1)
                pe.wait_ge(t_free[r % 2], n * 2 + (r // 2 + 2))
                for c in range(KC):
                    h = r + 4 * c
                    for kb in range(2):
                        ins = nc.tensor.matmul(o_bank[:, h * (DH + 1):(h + 1) * (DH + 1)], pt[:, r % 2, 2 * c + kb, :], v[:, j + kb, h, :],
                                               start=(kb == 0), stop=(kb == 1))
                if r == PAIRS - 1:
                    ins.then_inc(o_full, 1)

            def turn_o(at, j):
                bk, full = take(f"OT{j}", at)
                pe.wait_ge(o_free, at.g * GT + (j + 2))
                for k in range(KC):
                    ins = nc.tensor.transpose(bk[:, k * P:(k + 1) * P], on[:, k * P:(k + 1) * P], ident)
                ins.then_inc(full, 1)

            def out_project(at, j):
                bk, full = take(f"A{j}", at, (f"OT{j}",))
                for k in range(KC):
                    ins = passes(bk[:, 0:D], pair(ot_h, ot_l, every, k, every), parts(wo_s, k, every), k == 0, k == KC - 1)
                ins.then_inc(full, 1)

            def turn_x2(at, n):
                bk, full = take(f"X{n}", at)
                for j in range(2 * n, 2 * n + 2):
                    pe.wait_ge(x2_ready, at.g * GT + (j + 1))
                    for k in range(KC):
                        ins = nc.tensor.transpose(bk[:, k * BT + (j % 2) * P:k * BT + (j % 2) * P + P], x2[:, j, k * P:(k + 1) * P], ident)
                ins.then_inc(full, 1)

            def widen(at):
                bk, full = take("F0", at)
                for n in range(2):
                    b, k = m_use(f"X{n}", at)
                    pe.wait_ge(m_free[b], k + 1)
                    cs = slice(n * BT, (n + 1) * BT)
                    for k in range(KC):
                        ins = passes(bk[:, cs], parts(w1_s, k, slice(0, P)), pair(x2t_h, x2t_l, every, k, cs), k == 0, k == KC - 1)
                ins.then_inc(full, 1)
                for c in range(1, FC1):
                    bk, full = take(f"F{c}", at)
                    for k in range(KC):
                        ins = passes(bk[:, :], parts(w1_s, k, slice(c * P, (c + 1) * P)), pair(x2t_h, x2t_l, every, k, every), k == 0, k == KC - 1)
                    ins.then_inc(full, 1)

            def narrow(at, j, chunks):
                for c in chunks:
                    if c == 0:
                        bk, full = take(f"Y{j}", at)
                    else:
                        b, _ = m_use(f"Y{j}", at)
                        bk, full = m_bank[b], m_full[b]
                    if j == 0:
                        pe.wait_ge(gelu_split, at.f * FC1 + (c + 1))
                    ins = passes(bk[:, 0:D], pair(h_h, h_l, every, c, slice(j * P, (j + 1) * P)), parts(w2_s, c, every), c == 0, c == FC1 - 1)
                if c == FC1 - 1:
                    ins.then_inc(full, 1)

            def counts(at):
                bk, full = take("C", at)
                pe.wait_ge(route, ROUTE_PICKS)
                for n, ones in enumerate((C_TRI, C_ONE)):
                    ins = nc.tensor.matmul(bk[:, n * NT * E:(n + 1) * NT * E], cst[:, ones:ones + P], rt[9][:, :, :].rearrange("p t e -> p (t e)"), start=True, stop=True)
                ins.then_inc(full, 1)

            def project_bv(at):
                bk, full = take("BO", at)
                pe.wait_ge(bv_split, 2 * KC)
                for k in range(KC):
                    ins = passes(bk[:, 0:D], pair(ot_h, ot_l, every, k, every), parts(wo_s, k, every), k == 0, k == KC - 1)
                ins.then_inc(full, 1)

            pe.wait_ge(wraw_split, 3)
            pe.wait_ge(win_loaded, 16)
            for n in range(3):
                window(LEADING, n)
            query(LEADING, 0)
            query(LEADING, 1)
            for n in range(4):
                keys(LEADING, n)
            next_scores(LEADING)
            values(LEADING, WT - 1)
            for b in range(2):
                pe.wait_ge(m_free[b], len(LEAD) // 2)
            pe.wait_ge(ones_set, 1)
            wait_first_done(pe)

            def turn(at):
                g, more = at.g, at.seg != "last"

                def fill(j, *chunks):
                    if at.seg != "first":
                        narrow(at, j, chunks)
                for j in range(GT - 1):
                    scores(at, j + 1, 0)
                    if j:
                        turn_o(at, j - 1)
                    scores(at, j + 1, 1)
                    scores(at, j + 1, 2)
                    if j == 0:
                        fill(j, 0, 1, 2, 3, 4)
                    turn_probs(at, j, 0)
                    if j:
                        out_project(at, j - 1)
                        turn_probs(at, j, 1)
                        scores(at, j + 1, 3)
                        fill(j, 0, 1)
                    else:
                        scores(at, j + 1, 3)
                        turn_probs(at, j, 1)
                    times_v(at, j, 0)
                    turn_probs(at, j, 2)
                    fill(j, *((2, 3) if j else (5,)))
                    times_v(at, j, 1)
                    turn_probs(at, j, 3)
                    fill(j, *((4, 5) if j else (6,)))
                    times_v(at, j, 2)
                    fill(j, *((6, 7) if j else (7,)))
                    times_v(at, j, 3)
                    if more:
                        if j == 0:
                            pe.wait_ge(win_loaded, g * 16 + 32)
                        window(at, j)
                    if at.seg == "first" and j == 0:
                        counts(at)
                        project_bv(at)
                j = GT - 1
                turn_probs(at, j, 0)
                turn_o(at, j - 1)
                turn_probs(at, j, 1)
                if more:
                    query(at, 0)
                out_project(at, j - 1)
                times_v(at, j, 0)
                turn_probs(at, j, 2)
                if more:
                    query(at, 1)
                times_v(at, j, 1)
                turn_probs(at, j, 3)
                if more:
                    keys(at, 0)
                times_v(at, j, 2)
                if more:
                    keys(at, 1)
                times_v(at, j, 3)
                if more:
                    keys(at, 2)
                fill(j, *range(FC1))
                turn_o(at, j)
                if more:
                    keys(at, 3)
                out_project(at, j)
                if more:
                    next_scores(at)
                    values(at, WT - 1)
                turn_x2(at, 0)
                turn_x2(at, 1)
                if at.seg == "first":
                    pe.wait_ge(slot_step, ROUTE_SLOTS)
                widen(at)
            turns_of(pe, turn)
            for j in range(GT):
                narrow(TRAILING, j, range(FC1))

            wait_dense_done(pe)

            def turn_rows(b, p):
                pe.wait_ge(xr_loaded[p], through(b, p, 16))
                pe.wait_ge(ct_split, b)
                for k in range(KC):
                    for t in range(2):
                        ins = nc.tensor.transpose(bank[4][:, k * BT + t * P:k * BT + (t + 1) * P], xr[:, p, t, k * P:(k + 1) * P], ident)
                ins.then_inc(ct_full, 1)

            def gate_up(b, p):
                pe.wait_ge(ct_split, b + 1)
                for c in range(FCH):
                    pe.wait_ge(gu_split, b * FCH + (c + 1))
                    n = before(b, c)
                    if n is not None:
                        pe.wait_ge(z_ready, n)
                    w = P if c < FCH - 1 else GRW
                    for part in range(2 if c < FCH - 1 else 1):
                        for k in range(KC):
                            o = c * GUC + (k * 2 * P + part * P if c < FCH - 1 else k * GRW)
                            ins = passes(bank[ring(c)][0:w, part * BT:(part + 1) * BT], [gu_s[:, p, i, o:o + w] for i in range(2)],
                                         [xt_h[:, p, k, :], xt_l[:, p, k, :]], k == 0, k == KC - 1)
                    ins.then_inc(gu_full, 1)
                    if c == ROWS_AT - 1 and (not isinstance(b, int) or b < NB - 1):
                        turn_rows(b + 1, 1 - p)

            def down(b, p):
                pe.wait_ge(dw_split, b * DV + DV)
                pe.wait_ge(dw_split_pool, b * (FCH - DV) + (FCH - DV))
                pe.wait_ge(h_split, b * FCH + FCH)
                if not isinstance(b, int) or b >= 2:
                    pe.wait_ge(y_ready, b - 1)
                for t in range(2):
                    for c in range(FCH):
                        ins = passes(bank[5 + p][:, t * D:(t + 1) * D], [ht[:, p, i, c, t * P:(t + 1) * P] for i in range(2)],
                                     [dw_s[:, p, i, c * D:(c + 1) * D] for i in range(2)], c == 0, c == FCH - 1)
                ins.then_inc(y_full, 1)

            def body(b, p):
                gate_up(b, p)
                if not isinstance(b, int) or b >= 1:
                    down(b - 1, 1 - p)
            turn_rows(0, 0)
            blocks_of(pe, body)
            down(NB - 1, (NB - 1) % 2)


def kernel(**inputs):
    import concourse.bacc as bacc
    from concourse.bass_utils import run_bass_kernel_spmd

    a = {n: np.ascontiguousarray(v) for n, v in inputs.items()}

    def attn(n):
        return a["L0_attn_" + n]
    rows = np.zeros((5, D), np.float32)
    for n, name in enumerate(("bo", "gamma", "beta", "b2")):
        rows[n] = attn(name)
    rows[4, 0:E] = a["L0_ffn_gate_b"]
    cols = np.concatenate([attn("bq").reshape(KC, P).T, attn("bk").reshape(KC, P).T, attn("b1").reshape(FC1, P).T, attn("bv").reshape(KC, P).T], axis=1)
    gate = a["L0_ffn_gate_w"].T.reshape(KC, P, E).transpose(1, 0, 2)
    gate_t = a["L0_ffn_gp_w"].transpose(0, 2, 1).reshape(E, KC, P, F)
    up_t = a["L0_ffn_up_w"].transpose(0, 2, 1).reshape(E, KC, P, F)
    gu = np.zeros((E, P, GUW), np.float32)
    for c in range(FCH):
        for k in range(KC):
            if c < FCH - 1:
                o = c * GUC + k * 2 * P
                gu[:, :, o:o + P] = gate_t[:, k, :, c * P:(c + 1) * P]
                gu[:, :, o + P:o + 2 * P] = up_t[:, k, :, c * P:(c + 1) * P]
            else:
                o = c * GUC + k * GRW
                gu[:, :, o:o + FR] = gate_t[:, k, :, c * P:F]
                gu[:, :, o + WIN:o + WIN + FR] = up_t[:, k, :, c * P:F]
    down = np.zeros((E, FCH * P, D), np.float32)
    down[:, 0:F] = a["L0_ffn_down_w"].transpose(0, 2, 1)
    down[:, F] = a["L0_ffn_down_b"]
    down = down.reshape(E, FCH, P, D).transpose(0, 2, 1, 3).reshape(E, P, DWW)
    bi = np.zeros((E, P, BIW), np.float32)
    for n, (name, last) in enumerate((("gp_b", 0), ("up_b", WIN))):
        v = a["L0_ffn_" + name]
        bi[:, :, n * FCH:n * FCH + FCH - 1] = v[:, 0:(FCH - 1) * P].reshape(E, FCH - 1, P).transpose(0, 2, 1)
        bi[:, last:last + FR, n * FCH + FCH - 1] = v[:, (FCH - 1) * P:F]

    named = [("x", attn("x").reshape(S, D)), ("wq", attn("Wq")), ("wk", attn("Wk")), ("wv", attn("Wv")), ("wo", attn("Wo")), ("w1", attn("W1")), ("w2", attn("W2")),
             ("gate", gate), ("rows", rows), ("cols", cols), ("gu", gu), ("dw", down), ("bi", bi), ("const", constants())]
    nc = bacc.Bacc("TRN2", target_bir_lowering=False, num_devices=1)
    arrays, args = {}, []
    for name, v in named:
        v = np.ascontiguousarray(v)
        arrays[f"in_{name}_dram"] = v
        args.append(nc.dram_tensor(f"in_{name}_dram", v.shape, mybir.dt.from_np(v.dtype), kind="ExternalInput").ap())
    args.append(nc.dram_tensor("out_0_dram", (S, D), F32, kind="ExternalOutput").ap())
    program(nc, *args)
    r = run_bass_kernel_spmd(nc, [arrays], core_ids=[0])
    return r.results[0]["out_0_dram"].reshape(1, S, D)
```
